# Optimizing a Trainium2 kernel written in Bass

```python
import numpy as np
import jax
import jax.numpy as jnp

def _softmax(x, axis=-1):
    return jax.nn.softmax(x, axis=axis)

def _gelu(x):
    return jax.nn.gelu(x, approximate=True)

def _silu(x):
    return jax.nn.silu(x)

def _sigmoid(x):
    return jax.nn.sigmoid(x)

def _layernorm(x, axis=-1, eps=1e-05):
    m = jnp.mean(x, axis=axis, keepdims=True)
    v = jnp.var(x, axis=axis, keepdims=True)
    return (x - m) / jnp.sqrt(v + eps)

def _scatter_add(tgt, idx, src, axis=0):
    return tgt.at[idx].add(src)

def _segment_sum(src, seg, n):
    return jax.ops.segment_sum(src, seg, n)
kernel_name = 'mk_lm_tower_d1_tok_ids768_r4_75bcf1'

def setup_inputs(seed: int=0):
    np.random.seed(seed)
    _w = jnp.asarray

    def _rec_inputs():
        import jax
        import jax.numpy as jnp
        _rk = jax.random.key(seed)
        x = jax.random.randint(jax.random.fold_in(_rk, 1), (16, 128), 0, 8000, jnp.int32)
        mask_BS_i1_0 = jnp.where(jnp.ones((16, 128), dtype=bool), 1, 0).astype(jnp.int32)
        return (x, mask_BS_i1_0)
    x, mask_BS_i1_0 = _rec_inputs()

    def _L0_tok_setup():
        import jax, jax.numpy as jnp
        import numpy as np
        VOCAB = 8000
        MAX_POS = 128
        TYPE_VOCAB = 2
        D = 192
        EPS = 1e-12
        STD = 0.02
        key = jax.random.key(seed)
        k1, k2, k3, k4, k5 = jax.random.split(key, 5)
        B, S = (64, 128)
        input_ids = jax.random.randint(k1, (B, S), 0, VOCAB, dtype=jnp.int32)
        token_type_ids = jax.random.randint(k2, (B, S), 0, TYPE_VOCAB, dtype=jnp.int32)
        token_emb = jax.random.normal(k3, (VOCAB, D), dtype=jnp.float32) * STD
        pos_emb = jax.random.normal(k4, (MAX_POS, D), dtype=jnp.float32) * STD
        type_emb = jax.random.normal(k5, (TYPE_VOCAB, D), dtype=jnp.float32) * STD
        gamma = jnp.ones((D,), dtype=jnp.float32)
        beta = jnp.zeros((D,), dtype=jnp.float32)
        return {'input_ids': input_ids, 'token_type_ids': token_type_ids, 'token_emb': token_emb, 'pos_emb': pos_emb, 'type_emb': type_emb, 'gamma': gamma, 'beta': beta}
    _L0_tok_all = _L0_tok_setup()
    _L0_tok_in = {k: v for k, v in _L0_tok_all.items() if k in ('token_emb', 'pos_emb', 'type_emb', 'gamma', 'beta')}
    del _L0_tok_all

    def _L0_attn_setup():
        import jax, jax.numpy as jnp
        import numpy as np
        HIDDEN = 192
        HEADS = 8
        key = jax.random.key(seed)
        ks = jax.random.split(key, 5)
        b, n = (2, 256)
        x = jax.random.normal(ks[0], (b, n, HIDDEN), dtype=jnp.float32)
        W_qkv = jax.random.normal(ks[1], (HIDDEN, 3 * HIDDEN * HEADS), dtype=jnp.float32) * 0.02
        b_qkv = jnp.zeros((3 * HIDDEN * HEADS,), dtype=jnp.float32)
        W_proj = jax.random.normal(ks[2], (HEADS * HIDDEN, HIDDEN), dtype=jnp.float32) * 0.02
        b_proj = jnp.zeros((HIDDEN,), dtype=jnp.float32)
        return {'x': x, 'W_qkv': W_qkv, 'b_qkv': b_qkv, 'W_proj': W_proj, 'b_proj': b_proj}
    _L0_attn_all = _L0_attn_setup()
    _L0_attn_in = {k: v for k, v in _L0_attn_all.items() if k in ('W_qkv', 'b_qkv', 'W_proj', 'b_proj')}
    del _L0_attn_all

    def _L0_ffn_setup():
        import jax, jax.numpy as jnp
        import numpy as np
        E = 192
        H = 12
        D = E // H
        HID = 768
        NEXP = 4
        TOPK = 2
        EPS = 1e-05

        def _ln(x, g, b):
            m = jnp.mean(x, axis=-1, keepdims=True)
            v = jnp.mean(jnp.square(x - m), axis=-1, keepdims=True)
            return (x - m) * jax.lax.rsqrt(v + EPS) * g + b
        key = jax.random.key(seed)
        ks = jax.random.split(key, 10)
        s = 0.02
        return {'x': jax.random.normal(ks[0], (8, 256, E), jnp.float32), 'ln1_g': jnp.ones((E,), jnp.float32), 'ln1_b': jnp.zeros((E,), jnp.float32), 'in_w': jax.random.normal(ks[1], (3 * E, E), jnp.float32) * s, 'in_b': jnp.zeros((3 * E,), jnp.float32), 'out_w': jax.random.normal(ks[2], (E, E), jnp.float32) * s, 'out_b': jnp.zeros((E,), jnp.float32), 'mlp_w1': jax.random.normal(ks[3], (E, HID), jnp.float32) * s, 'mlp_b1': jnp.zeros((HID,), jnp.float32), 'mlp_w2': jax.random.normal(ks[4], (HID, E), jnp.float32) * s, 'mlp_b2': jnp.zeros((E,), jnp.float32), 'ln2_g': jnp.ones((E,), jnp.float32), 'ln2_b': jnp.zeros((E,), jnp.float32), 'gate_w': jax.random.normal(ks[5], (NEXP, E), jnp.float32) * s, 'gate_b': jnp.zeros((NEXP,), jnp.float32), 'exp_w1': jax.random.normal(ks[6], (NEXP, E, HID), jnp.float32) * s, 'exp_b1': jnp.zeros((NEXP, HID), jnp.float32), 'exp_w2': jax.random.normal(ks[7], (NEXP, HID, E), jnp.float32) * s, 'exp_b2': jnp.zeros((NEXP, E), jnp.float32)}
    _L0_ffn_all = _L0_ffn_setup()
    _L0_ffn_in = {k: v for k, v in _L0_ffn_all.items() if k in ('ln1_g', 'ln1_b', 'in_w', 'in_b', 'out_w', 'out_b', 'mlp_w1', 'mlp_b1', 'mlp_w2', 'mlp_b2', 'ln2_g', 'ln2_b', 'gate_w', 'gate_b', 'exp_w1', 'exp_b1', 'exp_w2', 'exp_b2')}
    del _L0_ffn_all
    return {'x': x, 'mask_BS_i1_0': mask_BS_i1_0, 'L0_tok_token_emb': _L0_tok_in['token_emb'], 'L0_tok_pos_emb': _L0_tok_in['pos_emb'], 'L0_tok_type_emb': _L0_tok_in['type_emb'], 'L0_tok_gamma': _L0_tok_in['gamma'], 'L0_tok_beta': _L0_tok_in['beta'], 'L0_attn_W_qkv': _L0_attn_in['W_qkv'], 'L0_attn_b_qkv': _L0_attn_in['b_qkv'], 'L0_attn_W_proj': _L0_attn_in['W_proj'], 'L0_attn_b_proj': _L0_attn_in['b_proj'], 'L0_ffn_ln1_g': _L0_ffn_in['ln1_g'], 'L0_ffn_ln1_b': _L0_ffn_in['ln1_b'], 'L0_ffn_in_w': _L0_ffn_in['in_w'], 'L0_ffn_in_b': _L0_ffn_in['in_b'], 'L0_ffn_out_w': _L0_ffn_in['out_w'], 'L0_ffn_out_b': _L0_ffn_in['out_b'], 'L0_ffn_mlp_w1': _L0_ffn_in['mlp_w1'], 'L0_ffn_mlp_b1': _L0_ffn_in['mlp_b1'], 'L0_ffn_mlp_w2': _L0_ffn_in['mlp_w2'], 'L0_ffn_mlp_b2': _L0_ffn_in['mlp_b2'], 'L0_ffn_ln2_g': _L0_ffn_in['ln2_g'], 'L0_ffn_ln2_b': _L0_ffn_in['ln2_b'], 'L0_ffn_gate_w': _L0_ffn_in['gate_w'], 'L0_ffn_gate_b': _L0_ffn_in['gate_b'], 'L0_ffn_exp_w1': _L0_ffn_in['exp_w1'], 'L0_ffn_exp_b1': _L0_ffn_in['exp_b1'], 'L0_ffn_exp_w2': _L0_ffn_in['exp_w2'], 'L0_ffn_exp_b2': _L0_ffn_in['exp_b2']}

def reference(x, mask_BS_i1_0, L0_tok_token_emb, L0_tok_pos_emb, L0_tok_type_emb, L0_tok_gamma, L0_tok_beta, L0_attn_W_qkv, L0_attn_b_qkv, L0_attn_W_proj, L0_attn_b_proj, L0_ffn_ln1_g, L0_ffn_ln1_b, L0_ffn_in_w, L0_ffn_in_b, L0_ffn_out_w, L0_ffn_out_b, L0_ffn_mlp_w1, L0_ffn_mlp_b1, L0_ffn_mlp_w2, L0_ffn_mlp_b2, L0_ffn_ln2_g, L0_ffn_ln2_b, L0_ffn_gate_w, L0_ffn_gate_b, L0_ffn_exp_w1, L0_ffn_exp_b1, L0_ffn_exp_w2, L0_ffn_exp_b2):
    import jax
    import jax.numpy as jnp

    def _L0_tok_ref(input_ids, token_type_ids, token_emb, pos_emb, type_emb, gamma, beta):
        import jax, jax.numpy as jnp
        import numpy as np
        VOCAB = 8000
        MAX_POS = 128
        TYPE_VOCAB = 2
        D = 192
        EPS = 1e-12
        STD = 0.02
        S = input_ids.shape[1]
        emb = token_emb[input_ids] + type_emb[token_type_ids] + pos_emb[:S][None, :, :]
        mean = jnp.mean(emb, axis=-1, keepdims=True)
        var = jnp.mean(jnp.square(emb - mean), axis=-1, keepdims=True)
        normed = (emb - mean) * jax.lax.rsqrt(var + EPS)
        return normed * gamma + beta

    def _L0_attn_ref(x, W_qkv, b_qkv, W_proj, b_proj):
        import jax, jax.numpy as jnp
        import numpy as np
        HIDDEN = 192
        HEADS = 8
        b, n, c = x.shape
        qkv = x @ W_qkv + b_qkv
        q, k, v = jnp.split(qkv, 3, axis=-1)
        q = q.reshape(b, HEADS, n, HIDDEN)
        k = k.reshape(b, HEADS, n, HIDDEN)
        v = v.reshape(b, HEADS, n, HIDDEN)
        energy = jnp.einsum('bhqd,bhkd->bhqk', q, k)
        scaling = jnp.float32(HIDDEN ** 0.5)
        attn = jax.nn.softmax(energy, axis=-1) / scaling
        out = jnp.einsum('bhal,bhlv->bhav', attn, v)
        out = out.reshape(b, n, HEADS * HIDDEN)
        return out @ W_proj + b_proj

    def _L0_ffn_ref(x, ln1_g, ln1_b, in_w, in_b, out_w, out_b, mlp_w1, mlp_b1, mlp_w2, mlp_b2, ln2_g, ln2_b, gate_w, gate_b, exp_w1, exp_b1, exp_w2, exp_b2):
        import jax, jax.numpy as jnp
        import numpy as np
        E = 192
        H = 12
        D = E // H
        HID = 768
        NEXP = 4
        TOPK = 2
        EPS = 1e-05

        def _ln(x, g, b):
            m = jnp.mean(x, axis=-1, keepdims=True)
            v = jnp.mean(jnp.square(x - m), axis=-1, keepdims=True)
            return (x - m) * jax.lax.rsqrt(v + EPS) * g + b
        B, N, _ = x.shape
        h = _ln(x, ln1_g, ln1_b)
        qkv = h @ in_w.T + in_b
        q, k, v = jnp.split(qkv, 3, axis=-1)
        q = q.reshape(B, N, H, D)
        k = k.reshape(B, N, H, D)
        v = v.reshape(B, N, H, D)
        scores = jnp.einsum('bqhd,bkhd->bhqk', q, k) / jnp.sqrt(jnp.float32(D))
        attn = jax.nn.softmax(scores, axis=-1)
        ctx = jnp.einsum('bhqk,bkhd->bqhd', attn, v).reshape(B, N, E)
        x = x + ctx @ out_w.T + out_b
        x = x + jax.nn.gelu(x @ mlp_w1 + mlp_b1, approximate=False) @ mlp_w2 + mlp_b2
        xm = _ln(x, ln2_g, ln2_b)
        logits = xm @ gate_w.T + gate_b
        topv, topi = jax.lax.top_k(logits, TOPK)
        gates = jax.nn.softmax(topv, axis=-1)
        onehot = jax.nn.one_hot(topi, NEXP, dtype=x.dtype)
        comb = jnp.einsum('bnk,bnke->bne', gates, onehot)
        moe_out = jnp.zeros_like(x)
        for e in range(NEXP):
            he = jax.nn.gelu(xm @ exp_w1[e] + exp_b1[e], approximate=False)
            oe = he @ exp_w2[e] + exp_b2[e]
            moe_out = moe_out + comb[..., e:e + 1] * oe
        return x + moe_out
    h = _L0_tok_ref(x, mask_BS_i1_0, L0_tok_token_emb, L0_tok_pos_emb, L0_tok_type_emb, L0_tok_gamma, L0_tok_beta)
    h = h + _L0_attn_ref(_layernorm(h, axis=-1), L0_attn_W_qkv, L0_attn_b_qkv, L0_attn_W_proj, L0_attn_b_proj)
    h = h + _L0_ffn_ref(_layernorm(h, axis=-1), L0_ffn_ln1_g, L0_ffn_ln1_b, L0_ffn_in_w, L0_ffn_in_b, L0_ffn_out_w, L0_ffn_out_b, L0_ffn_mlp_w1, L0_ffn_mlp_b1, L0_ffn_mlp_w2, L0_ffn_mlp_b2, L0_ffn_ln2_g, L0_ffn_ln2_b, L0_ffn_gate_w, L0_ffn_gate_b, L0_ffn_exp_w1, L0_ffn_exp_b1, L0_ffn_exp_w2, L0_ffn_exp_b2)
    return h

_drawn_inputs = setup_inputs


def setup_inputs(seed=0):
    import zlib

    import numpy as np

    out = dict(_drawn_inputs(seed))
    spreads = {'L0_tok_gamma': (1.0, 0.2),
     'L0_tok_beta': (0.0, 0.1),
     'L0_attn_b_qkv': (0.0, 0.8),
     'L0_attn_b_proj': (0.0, 0.1),
     'L0_ffn_ln1_g': (1.0, 0.6),
     'L0_ffn_ln1_b': (0.0, 0.8),
     'L0_ffn_in_b': (0.0, 0.569),
     'L0_ffn_out_b': (0.0, 0.1),
     'L0_ffn_mlp_b1': (0.0, 0.46),
     'L0_ffn_mlp_b2': (0.0, 0.1),
     'L0_ffn_ln2_g': (1.0, 0.6),
     'L0_ffn_ln2_b': (0.0, 0.733),
     'L0_ffn_gate_b': (0.0, 0.377),
     'L0_ffn_exp_b1': (0.0, 0.749),
     'L0_ffn_exp_b2': (0.0, 0.276)}
    factors = {'L0_attn_W_qkv': 8.0, 'L0_attn_W_proj': 8.0}
    for name, (base, spread) in spreads.items():
        noise = np.random.default_rng([zlib.crc32(name.encode()), seed]).standard_normal(out[name].shape)
        drawn = base * np.exp(spread * noise) if base else spread * noise
        out[name] = jnp.asarray(drawn.astype(out[name].dtype))
    for name, factor in factors.items():
        out[name] = (out[name] * factor).astype(out[name].dtype)
    return out
```

```python
import numpy as np
from contextlib import ExitStack

import concourse.bass as bass
from concourse import mybir
from concourse.alu_op_type import AluOpType as ALU


F32 = mybir.dt.float32
F32R = mybir.dt.float32r
I32 = mybir.dt.int32
U32 = mybir.dt.uint32
ACT = mybir.ActivationFunctionType
X = mybir.AxisListType.X

P = 128
BATCH, SEQ = 16, 128
TOKENS = BATCH * SEQ
TILES = TOKENS // P
D = 192
MAIN, TAIL = P, D - P
CHUNKS = 8
QKV = CHUNKS * D
GROUP = P // CHUNKS
GROUPS = P // GROUP
QUAD = 4
HEADS, HD = 12, 16
HID = 768
HC = HID // P
NEXP = 4
FFNS = 1 + NEXP


class Signal:

    def __init__(self, sem, per_turn, before=0, lent=0, step=1):
        self.sem, self.per_turn, self.before, self.lent, self.step = sem, per_turn, before + lent, lent, step

    def lend(self, engine):
        engine.sem_inc(self.sem, self.lent * self.step)

    def at(self, turn, event):
        if isinstance(turn, int) and isinstance(event, int):
            value = (self.before + turn * self.per_turn + event + 1) * self.step
            assert value > 0
            return value
        return turn * (self.per_turn * self.step) + (self.before + event + 1) * self.step



class Steps:

    def __init__(self, engine, signal, turn, first=0, passed=None):
        self.engine, self.mark, self.turn, self.count, self.passed = engine, signal, turn, first, passed

    def then(self, instruction, settle=True):
        instruction.then_inc(self.mark.sem, 1)
        self.count += 1
        if settle:
            self.settle()

    def settle(self):
        self.engine.wait_ge(self.mark.sem, self.mark.at(self.turn, self.count - 1))


def apart(engine, passed):
    engine.sem_inc(passed, 1)


def raw(hi):
    return hi.bitcast(F32)


def inverse_root(nc, steps, variance, eps, half, guess, rstd, work):
    MAGIC = 0x5F3759DF
    steps.then(nc.vector.tensor_scalar(work, variance, eps, 1.0, ALU.add, ALU.mult))
    nc.vector.tensor_scalar(half, work, -0.5, 1.0, ALU.mult, ALU.mult)
    steps.then(nc.vector.tensor_scalar(guess.bitcast(I32), work.bitcast(I32), 1, None, ALU.arith_shift_right))
    steps.then(nc.vector.tensor_scalar(rstd.bitcast(I32), guess.bitcast(I32), -1.0, float(MAGIC), ALU.mult, ALU.add))
    for _ in range(3):
        steps.then(nc.vector.tensor_tensor(work, rstd, rstd, ALU.mult))
        steps.then(nc.vector.tensor_tensor(work, work, half, ALU.mult))
        steps.then(nc.vector.scalar_tensor_tensor(out=rstd, in0=work, scalar=1.5, in1=rstd, op0=ALU.add, op1=ALU.mult))


ROOT_STEPS = 12


def moments_of(nc, steps, stats, moments, tiles):
    for i, tile in enumerate(tiles):
        last = nc.vector.bn_stats(stats[:, i, :], tile)
    steps.then(last)
    apart(steps.engine, steps.passed)
    for i in range(len(tiles)):
        last = nc.vector.bn_aggr(moments[:, i, :], stats[:, i, :])
    steps.then(last)


NORM_STEPS = 2 + ROOT_STEPS


def embed(nc, keep, dram):
    TAKE = 4
    TAKES = TILES // TAKE
    with ExitStack() as ctx:
        sb = lambda name, shape, dt=F32: ctx.enter_context(nc.sbuf_tensor(f"embed_{name}", shape, dt))
        sem = lambda name: ctx.enter_context(nc.semaphore(f"embed_{name}"))
        ids = sb("ids", [P, 2, TILES], I32)
        emb = sb("emb", [P, TILES, D])
        typ = sb("typ", [P, TILES, D])
        pos = sb("pos", [P, D])
        gamma = sb("gamma", [P, D])
        beta = sb("beta", [P, D])
        stats = sb("stats", [P, TAKE, 6])
        moments = sb("moments", [P, TAKE, 2])
        half, guess, rstd, work = (sb(n, [P, TAKE]) for n in ("half", "guess", "rstd", "work"))
        stage = [(sb(f"stage_main{i}", [P, QKV]), sb(f"stage_tail{i}", [P, QKV])) for i in range(4)]
        low_half = sb("low_half", [P, QKV], F32R)

        ids_loaded, rows_loaded, pos_loaded = sem("ids_loaded"), sem("rows_loaded"), sem("pos_loaded")
        token_rows = [sem(f"token_rows{i}") for i in range(TAKES)]
        type_rows = [sem(f"type_rows{i}") for i in range(TAKES)]
        weights_loaded = [sem(f"weights_loaded{i}") for i in range(4)]
        const_ready = sem("const_ready")
        h0_ready, h0_stored = sem("h0_ready"), sem("h0_stored")
        hi_ready, half_ready, half_used = sem("w_hi_ready"), sem("w_half_ready"), sem("w_half_used")
        dve_step = Signal(sem("dve_step"), 0)
        block = ctx.enter_context(nc.Block())
        targets = keep["w_qkv"] + [keep["w_proj"]]

        @block.sync
        def _(sp):
            sp.dma_start(ids[:, :, :], dram["ids"].rearrange("p (a b) -> p a b", a=2)).then_inc(ids_loaded, 16)
            for i in range(4):
                main, tail = stage[i]
                cut = dram["w_qkv"][:, i * QKV:(i + 1) * QKV] if i < 3 else None
                src_main = cut[0:MAIN, :] if i < 3 else dram["w_proj_main"]
                src_tail = cut[MAIN:D, :] if i < 3 else dram["w_proj_tail"]
                sp.dma_start(main[:, :], src_main).then_inc(weights_loaded[i], 16)
                for half in range(2):
                    sp.dma_start(tail[half * TAIL:(half + 1) * TAIL, :], src_tail).then_inc(weights_loaded[i], 16)
            for t in range(TAKES):
                sp.wait_ge(h0_ready, t + 1)
                sp.dma_start(dram["h0"].rearrange("(b p) d -> p b d", p=P)[:, t * TAKE:(t + 1) * TAKE, :],
                             emb[:, t * TAKE:(t + 1) * TAKE, :]).then_inc(h0_stored, 16)
            sp.wait_ge(h0_stored, 16 * TAKES)

        @block.gpsimd
        def _(pool):
            pool.wait_ge(ids_loaded, 16)
            for t in range(TAKES):
                for i in range(t * TAKE, (t + 1) * TAKE):
                    nc.gpsimd.indirect_dma_start(emb[:, i, :], None, dram["token_emb"],
                                                 bass.IndirectOffsetOnAxis(ap=ids[:, 0, i:i + 1], axis=0)).then_inc(token_rows[t], 16)
                    nc.gpsimd.indirect_dma_start(typ[:, i, :], None, dram["type_emb"],
                                                 bass.IndirectOffsetOnAxis(ap=ids[:, 1, i:i + 1], axis=0)).then_inc(type_rows[t], 16)
            nc.gpsimd.memset(keep["ident"][:, :], 0.0).then_inc(const_ready, 1)
            pool.wait_ge(const_ready, 1)
            nc.gpsimd.affine_select(out=keep["ident"][:, :], in_=keep["ident"][:, :], compare_op=ALU.not_equal,
                                    fill=1.0, base=0, pattern=[[-1, P]], channel_multiplier=1).then_inc(const_ready, 1)

        @block.scalar
        def _(act):
            act.dma_start(pos[:, :], dram["pos_emb"]).then_inc(pos_loaded, 16)
            act.dma_start(gamma[:, :], dram["gamma"].to_broadcast([P, D])).then_inc(rows_loaded, 16)
            act.dma_start(beta[:, :], dram["beta"].to_broadcast([P, D])).then_inc(rows_loaded, 16)
            for i in range(4):
                main, tail = stage[i]
                main_hi, main_lo, tail_a, tail_b = targets[i]
                act.wait_ge(weights_loaded[i], 48)
                nc.scalar.activation(main_hi, main[:, :], ACT.Copy).then_inc(hi_ready, 1)
                if i < 3:
                    if i == 0:
                        act.wait_ge(dve_step.sem, 2)
                    else:
                        act.wait_ge(half_used, i)
                    nc.scalar.activation(low_half[:, :], tail[:, :], ACT.Copy,
                                         scale=keep["low_rows"][:, 0:1]).then_inc(half_ready, 1)
                else:
                    nc.scalar.activation(tail_a, tail[:, :], ACT.Copy).then_inc(half_ready, 1)

        @block.vector
        def _(dve):
            steps = Steps(dve, dve_step, 0, passed=keep["passed"])
            steps.then(nc.vector.memset(keep["low_rows"][0:TAIL, :], 0.0))
            steps.then(nc.vector.memset(keep["low_rows"][TAIL:P, :], 1.0))

            def tokens(t):
                take = slice(t * TAKE, (t + 1) * TAKE)
                dve.wait_ge(token_rows[t], 16 * TAKE)
                dve.wait_ge(type_rows[t], 16 * TAKE)
                steps.then(nc.vector.tensor_tensor(emb[:, take, :], emb[:, take, :], typ[:, take, :], ALU.add))
                if t == 0:
                    dve.wait_ge(pos_loaded, 16)
                    dve.wait_ge(rows_loaded, 32)
                wide = lambda row: row[:, :].unsqueeze(1).to_broadcast([P, TAKE, D])
                steps.then(nc.vector.tensor_tensor(emb[:, take, :], emb[:, take, :], wide(pos), ALU.add))
                moments_of(nc, steps, stats, moments, [emb[:, i, :] for i in range(t * TAKE, (t + 1) * TAKE)])
                inverse_root(nc, steps, moments[:, :, 1], 1e-12, half[:, :], guess[:, :], rstd[:, :], work[:, :])
                for i in range(TAKE):
                    last = nc.vector.tensor_scalar(emb[:, t * TAKE + i, :], emb[:, t * TAKE + i, :], moments[:, i, 0:1],
                                                   rstd[:, i:i + 1], ALU.subtract, ALU.mult)
                steps.then(last)
                steps.then(nc.vector.tensor_tensor(emb[:, take, :], emb[:, take, :], wide(gamma), ALU.mult))
                nc.vector.tensor_tensor(emb[:, take, :], emb[:, take, :], wide(beta), ALU.add).then_inc(h0_ready, 1)

            def weights(i):
                main, tail = stage[i]
                main_hi, main_lo, tail_a, tail_b = targets[i]
                dve.wait_ge(hi_ready, i + 1)
                nc.vector.tensor_tensor(main_lo, main[:, :], raw(main_hi), ALU.subtract)
                dve.wait_ge(half_ready, i + 1)
                if i < 3:
                    nc.vector.tensor_tensor(tail_a, tail[:, :], raw(low_half[:, :]), ALU.subtract).then_inc(half_used, 1)
                else:
                    nc.vector.tensor_tensor(tail_b, tail[:, :], raw(tail_a), ALU.subtract)

            for t in range(4):
                tokens(t)
                weights(t)


def attention(nc, keep, dram):
    UNIT = 2
    UNITS = TILES // UNIT
    UT = UNIT * P
    UG = UNIT * GROUPS
    QUADS = UG // QUAD
    RING = 3
    VCUT = 512
    VCUTS = QKV // VCUT
    PAIRS = CHUNKS // 2
    with ExitStack() as ctx:
        sb = lambda name, shape, dt=F32: ctx.enter_context(nc.sbuf_tensor(f"attn_{name}", shape, dt))
        ps = lambda name, shape: ctx.enter_context(nc.psum_tensor(name, shape, F32))
        sem = lambda name: ctx.enter_context(nc.semaphore(f"attn_{name}"))
        w_q, w_k, w_v = keep["w_qkv"]
        wp_hi, wp_lo, wp_twin_hi, wp_twin_lo = (w.rearrange("p (c n) -> p c n", c=CHUNKS) for w in keep["w_proj"])
        b_qk = sb("b_qk", [P, 2 * QKV // P])
        b_v = sb("b_v", [P, QKV])
        b_proj = sb("b_proj", [P, D])
        xin = sb("xin", [P, UNIT, D])
        xn = sb("xn", [P, UNIT, MAIN + 2 * TAIL])
        xt_hi, xt_lo, xt_twin_hi, xt_twin_lo = (sb(n, [P, UT], F32R) for n in ("xt_hi", "xt_lo", "xt_twin_hi", "xt_twin_lo"))
        q_hi, q_lo, q_stack, k_hi, k_lo, k_twin_hi, k_twin_lo = (
            sb(n, [P, UG, P], F32R) for n in ("q_hi", "q_lo", "q_stack", "k_hi", "k_lo", "k_twin_hi", "k_twin_lo"))
        probs = sb("probs", [P, QUADS, QUAD, P])
        pt_hi = sb("pt_hi", [P, 2, QUAD, P], F32R)
        pt_lo = sb("pt_lo", [P, 2, QUAD, P], F32R)
        v_flat = sb("v_flat", [P, QKV])
        v_rows = sb("v_rows", [P, GROUPS, D])
        v_hi = sb("v_hi", [P, GROUPS, D], F32R)
        v_lo = sb("v_lo", [P, GROUPS, D], F32R)
        o_hi, o_lo, o_stack = (sb(n, [P, CHUNKS, P], F32R) for n in ("o_hi", "o_lo", "o_stack"))
        residual = sb("residual", [P, UNIT, D])
        h1 = sb("h1", [P, UNIT, D])
        neg_max = sb("neg_max", [P, QUADS, QUAD])
        sums = sb("sums", [P, QUADS, QUAD])
        inverse = sb("inverse", [P, QUADS, QUAD])
        stats = sb("stats", [P, UNIT, 6])
        moments = sb("moments", [P, UNIT, 2])
        half, guess, rstd, work = (sb(n, [P, UNIT]) for n in ("half", "guess", "rstd", "work"))
        ring = ps("ring", [P, RING, 512])
        ps_scores = ps("ps_scores", [P, 2, QUAD, P])
        ps_turned = ps("ps_turned", [P, QUAD, P])
        ps_mixed = ps("ps_mixed", [P, QUAD, P])
        ps_mixed_tail = ps("ps_mixed_tail", [P, QUAD, P])

        QK_SLOTS = 2 * QKV // P
        SLOTS_BEFORE = 1 + QK_SLOTS + VCUTS
        SLOTS = VCUTS + 1 + QK_SLOTS + VCUTS + UNIT
        assert SLOTS % RING == 0
        bank = lambda slot: (slot + SLOTS_BEFORE) % RING
        ring_filled = Signal(sem("ring_filled"), SLOTS, SLOTS_BEFORE)
        ring_hi = Signal(sem("ring_hi"), 1 + QK_SLOTS, 1 + QK_SLOTS)
        ring_free = Signal(sem("ring_free"), SLOTS, SLOTS_BEFORE, lent=RING)
        x_loaded = Signal(sem("x_loaded"), 1, 1, step=16)
        xn_ready = Signal(sem("xn_ready"), 1, 1)
        TWIN_STEPS = 4
        twin_step = Signal(sem("k_twin_step"), TWIN_STEPS, TWIN_STEPS)
        scored = Signal(sem("scored"), QUADS)
        max_ready = Signal(sem("max_ready"), QUADS)
        exps_ready = Signal(sem("exps_ready"), QUADS, lent=2)
        inverse_ready = Signal(sem("inverse_ready"), QUADS)
        probs_ready = Signal(sem("probs_ready"), QUADS)
        turned = Signal(sem("turned"), QUADS, lent=QUADS)
        turned_hi = Signal(sem("turned_hi"), QUADS)
        turned_lo = Signal(sem("turned_lo"), QUADS, lent=1)
        mixed = Signal(sem("mixed"), QUADS, lent=2)
        mixed_hi = Signal(sem("mixed_hi"), QUADS)
        mixed_lo = Signal(sem("mixed_lo"), QUADS, lent=1)
        v_sent = Signal(sem("v_sent"), UNIT, 1, lent=1, step=16)
        v_rows_loaded = Signal(sem("v_rows_loaded"), UNIT, 1, step=16 * CHUNKS)
        v_hi_ready = Signal(sem("v_hi_ready"), UNIT)
        v_ready = Signal(sem("v_ready"), UNIT)
        residual_loaded = Signal(sem("residual_loaded"), 1, step=16)
        residual_biased = Signal(sem("residual_biased"), 1)
        h1_stored = [Signal(sem(f"h1_stored{b}"), 1, lent=1, step=16) for b in range(UNIT)]
        biases_loaded = sem("biases_loaded")
        dve_step = Signal(sem("dve_step"), NORM_STEPS, NORM_STEPS)
        block = ctx.enter_context(nc.Block())

        rows = lambda turn: bass.ds(turn * UT, UT)
        v_last_slot = {-1: -1, 0: VCUTS - 1, 1: SLOTS - UNIT - 1}
        out_slot = lambda more, b: (SLOTS - UNIT if more else VCUTS) + b

        def turns(engine, before, body):
            before()
            with engine.Fori(0, UNITS - 1) as turn:
                body(turn, True)
            body(UNITS - 1, False)

        @block.sync
        def _(sp):
            def load_x(turn, event, unit):
                if event == 0:
                    sp.wait_ge(xn_ready.sem, xn_ready.at(turn, -1))
                sp.dma_start(xin[:, :, :], dram["h0"][rows(unit), :].rearrange("(b p) d -> p b d", p=P)).then_inc(x_loaded.sem, 16)

            def move_v(turn, event):
                there = dram["v"][event % 2]
                sp.wait_ge(ring_free.sem, ring_free.at(turn, v_last_slot[event]))
                sp.dma_start(there, v_flat[:, :]).then_inc(v_sent.sem, 16)
                sp.wait_ge(v_sent.sem, v_sent.at(turn, event))
                apart(sp, keep["passed"])
                if event >= 0:
                    sp.wait_ge(v_ready.sem, v_ready.at(turn, event))
                back = there.rearrange("(g t) (c d) -> c t g d", t=GROUP, c=CHUNKS)
                for c in range(CHUNKS):
                    sp.dma_start(v_rows[c * GROUP:(c + 1) * GROUP, :, :], back[c]).then_inc(v_rows_loaded.sem, 16)

            def store(turn, more, b):
                sp.wait_ge(ring_free.sem, ring_free.at(turn, out_slot(more, b)))
                sp.dma_start(dram["h1"][bass.ds(turn * UT + b * P, P), :], h1[:, b, :]).then_inc(h1_stored[b].sem, 16)

            def before():
                load_x(0, -1, 0)
                move_v(0, -1)

            def body(turn, more):
                if more:
                    load_x(turn, 0, turn + 1)
                sp.wait_ge(ring_free.sem, ring_free.at(turn, -1))
                sp.dma_start(residual[:, :, :], dram["h0"][rows(turn), :].rearrange("(b p) d -> p b d", p=P)).then_inc(residual_loaded.sem, 16)
                move_v(turn, 0)
                if more:
                    move_v(turn, 1)
                store(turn, more, 0)
                store(turn, more, 1)

            turns(sp, before, body)
            for b in range(UNIT):
                sp.wait_ge(h1_stored[b].sem, h1_stored[b].at(UNITS - 1, 0))

        @block.gpsimd
        def _(pool):
            def twins(turn, event, slot):
                steps = Steps(pool, twin_step, turn, event * TWIN_STEPS)
                """The tails of k's even chunks stand on the lower partitions, the odd ones' on the upper:
                copy each to the other half."""
                pool.wait_ge(ring_free.sem, ring_free.at(turn, slot))
                apart(pool, keep["passed"])
                for k_twin in (k_twin_hi, k_twin_lo):
                    for odd in range(2):
                        chunks = lambda half: k_twin[half * TAIL:(half + 1) * TAIL, :, :].rearrange(
                            "p g (c o t) -> p g c o t", o=2, t=GROUP)[:, :, :, odd, :]
                        if steps.count % TWIN_STEPS:
                            steps.settle()
                            apart(pool, keep["passed"])
                        steps.then(nc.gpsimd.tensor_scalar(chunks(1 - odd), raw(chunks(odd)), 1.0, 1.0, ALU.mult, ALU.mult), settle=False)

            def body(turn, more):
                for n in range(QUADS):
                    pool.wait_ge(inverse_ready.sem, inverse_ready.at(turn, n))
                    apart(pool, keep["passed"])
                    for j in range(QUAD):
                        last = nc.gpsimd.tensor_scalar(probs[:, n, j, :], probs[:, n, j, :], inverse[:, n, j:j + 1],
                                                       float(D) ** -0.5, ALU.mult, ALU.mult)
                    last.then_inc(probs_ready.sem, 1)
                if more:
                    pool.wait_ge(probs_ready.sem, probs_ready.at(turn, QUADS - 1))
                    twins(turn, 0, VCUTS + QK_SLOTS)

            def before():
                twins(0, -1, QK_SLOTS - SLOTS_BEFORE)

            turns(pool, before, body)

        @block.tensor
        def _(pe):
            def slot_free(turn, slot):
                pe.wait_ge(ring_free.sem, ring_free.at(turn, slot - RING))

            def transposes(turn, slot, event):
                pe.wait_ge(xn_ready.sem, xn_ready.at(turn, event))
                slot_free(turn, slot)
                for part in range(2):
                    for b in range(UNIT):
                        at = (part * UNIT + b) * P
                        last = nc.tensor.transpose(ring[:, bank(slot), at:at + P], xn[:, b, part * P:(part + 1) * P], keep["ident"][:, :])
                last.then_inc(ring_filled.sem, 1)

            def project_qk(turn, slot, event):
                for s in range(QK_SLOTS):
                    w_hi, w_lo, w_stack, _ = (w_q, w_k)[s // (QK_SLOTS // 2)]
                    cols = slice((s % (QK_SLOTS // 2)) * P, (s % (QK_SLOTS // 2) + 1) * P)
                    if s == 0:
                        pe.wait_ge(ring_free.sem, ring_free.at(turn, slot - 1))
                    slot_free(turn, slot + s)
                    out = ring[:, bank(slot + s), 0:UT]
                    passes = ((w_hi, xt_hi), (w_hi, xt_lo), (w_lo, xt_hi), (w_stack, xt_twin_hi), (w_stack, xt_twin_lo))
                    for i, (w, x) in enumerate(passes):
                        last = nc.tensor.matmul(out, w[:, cols], x[:, :], start=i == 0, stop=i == 4)
                    last.then_inc(ring_filled.sem, 1)

            def project_v(turn, slot, b):
                w_hi, w_lo, w_stack, _ = w_v
                tile = slice(b * P, (b + 1) * P)
                for s in range(VCUTS):
                    slot_free(turn, slot + s)
                    cols = slice(s * VCUT, (s + 1) * VCUT)
                    passes = ((xt_hi, w_hi), (xt_lo, w_hi), (xt_hi, w_lo), (xt_twin_hi, w_stack), (xt_twin_lo, w_stack))
                    for i, (x, w) in enumerate(passes):
                        last = nc.tensor.matmul(ring[:, bank(slot + s), :], x[:, tile], w[:, cols], start=i == 0, stop=i == 4)
                    last.then_inc(ring_filled.sem, 1)

            def scores(turn, n):
                pe.wait_ge(exps_ready.sem, exps_ready.at(turn, n - 2))
                for j in range(QUAD):
                    g = n * QUAD + j
                    passes = ((q_hi, k_hi), (q_lo, k_hi), (q_hi, k_lo), (q_stack, k_twin_hi), (q_stack, k_twin_lo))
                    for i, (q, k) in enumerate(passes):
                        last = nc.tensor.matmul(ps_scores[:, n % 2, j, :], q[:, g, :], k[:, g, :], start=i == 0, stop=i == 4)
                last.then_inc(scored.sem, 1)

            def turn_probs(turn, n):
                pe.wait_ge(probs_ready.sem, probs_ready.at(turn, n))
                pe.wait_ge(turned_lo.sem, turned_lo.at(turn, n - 1))
                for j in range(QUAD):
                    last = nc.tensor.transpose(ps_turned[:, j, :], probs[:, n, j, :], keep["ident"][:, :])
                last.then_inc(turned.sem, 1)

            def mix(turn, n):
                b = n // (QUADS // UNIT)
                pe.wait_ge(v_ready.sem, v_ready.at(turn, b))
                pe.wait_ge(turned_lo.sem, turned_lo.at(turn, n))
                pe.wait_ge(mixed_lo.sem, mixed_lo.at(turn, n - 1))
                for cols, out in ((slice(0, MAIN), ps_mixed), (slice(MAIN, D), ps_mixed_tail)):
                    for j in range(QUAD):
                        g = n * QUAD + j - b * GROUPS
                        passes = ((v_hi, pt_hi), (v_lo, pt_hi), (v_hi, pt_lo))
                        for i, (v, p) in enumerate(passes):
                            last = nc.tensor.matmul(out[0:cols.stop - cols.start, j, :], v[:, g, cols], p[:, n % 2, j, :], start=i == 0, stop=i == 2)
                last.then_inc(mixed.sem, 1)

            def project_out(turn, slot, b):
                pe.wait_ge(mixed_lo.sem, mixed_lo.at(turn, (b + 1) * (QUADS // UNIT) - 1))
                slot_free(turn, slot)
                passes = ((o_hi, wp_hi), (o_lo, wp_hi), (o_hi, wp_lo), (o_stack, wp_twin_hi), (o_stack, wp_twin_lo))
                for c in range(CHUNKS):
                    for i, (o, w) in enumerate(passes):
                        last = nc.tensor.matmul(ring[:, bank(slot), 0:D], o[:, c, :], w[:, c, :], start=c + i == 0, stop=c == CHUNKS - 1 and i == 4)
                last.then_inc(ring_filled.sem, 1)

            def before():
                transposes(0, -SLOTS_BEFORE, -1)
                project_qk(0, 1 - SLOTS_BEFORE, -1)
                project_v(0, -VCUTS, 0)

            def body(turn, more):
                pe.wait_ge(twin_step.sem, twin_step.at(turn, -1))
                for n in range(QUADS):
                    scores(turn, n)
                slot = 0
                project_v(turn, slot, 1)
                slot += VCUTS
                if more:
                    transposes(turn, slot, 0)
                    project_qk(turn, slot + 1, 0)
                    slot += 1 + QK_SLOTS
                turn_probs(turn, 0)
                turn_probs(turn, 1)
                mix(turn, 0)
                mix(turn, 1)
                if more:
                    project_v(turn, slot, 0)
                    slot += VCUTS
                project_out(turn, slot, 0)
                turn_probs(turn, 2)
                turn_probs(turn, 3)
                mix(turn, 2)
                mix(turn, 3)
                project_out(turn, slot + 1, 1)

            turns(pe, before, body)

        def qk_place(s):
            first = s % (QK_SLOTS // 2)
            is_k = s >= QK_SLOTS // 2
            return is_k, first if first < CHUNKS else None, 2 * (first - CHUNKS)

        def spread(tensor, half, c):
            part = slice(0, P) if half is None else slice(half * TAIL, (half + 1) * TAIL)
            return tensor[part, :, c * GROUP:(c + 1) * GROUP]

        def from_ring(slot, half=None):
            part = slice(0, P) if half is None else slice(half * TAIL, (half + 1) * TAIL)
            return ring[part, bank(slot), 0:UT].rearrange("p (g t) -> p g t", t=GROUP)

        def o_place(tensor, part, n):
            at = (n % (QUADS // UNIT)) * QUAD * GROUP
            return tensor[part, :, at:at + QUAD * GROUP].rearrange("p c (j t) -> p j c t", t=GROUP)

        def from_mixed(tensor, part):
            return tensor[part, :, :].rearrange("p j (c t) -> p j c t", t=GROUP)

        @block.scalar
        def _(act):
            act.dma_start(b_qk[:, :], dram["b_qk"]).then_inc(biases_loaded, 16)
            act.dma_start(b_v[:, :], dram["b_v"].to_broadcast([P, QKV])).then_inc(biases_loaded, 16)
            act.dma_start(b_proj[:, :], dram["b_proj"].to_broadcast([P, D])).then_inc(biases_loaded, 16)
            for signal in (ring_free, exps_ready, turned, turned_lo, mixed, mixed_lo, v_sent, *h1_stored):
                signal.lend(act)

            def split_x(turn, slot, event):
                act.wait_ge(ring_filled.sem, ring_filled.at(turn, slot))
                nc.scalar.activation(xt_hi[:, :], ring[:, bank(slot), 0:UT], ACT.Copy)
                nc.scalar.activation(xt_twin_hi[:, :], ring[:, bank(slot), UT:2 * UT], ACT.Copy).then_inc(ring_hi.sem, 1)

            def split_qk(turn, slot):
                for s in range(QK_SLOTS):
                    is_k, main, pair = qk_place(s)
                    bias = b_qk[:, s:s + 1]
                    act.wait_ge(ring_filled.sem, ring_filled.at(turn, slot + s))
                    if main is not None:
                        last = nc.scalar.activation(spread(k_hi if is_k else q_hi, None, main), from_ring(slot + s), ACT.Identity, bias=bias)
                    else:
                        for half in range(2):
                            last = nc.scalar.activation(spread(k_twin_hi if is_k else q_stack, half, pair + half), from_ring(slot + s, half),
                                                        ACT.Identity, bias=bias[half * TAIL:(half + 1) * TAIL, :])
                    last.then_inc(ring_hi.sem, 1)

            def split_v(turn, b):
                act.wait_ge(v_rows_loaded.sem, v_rows_loaded.at(turn, b - 1))
                act.wait_ge(mixed.sem, mixed.at(turn, b * (QUADS // UNIT) - 1))
                nc.scalar.activation(v_hi[:, :, :], v_rows[:, :, :], ACT.Copy).then_inc(v_hi_ready.sem, 1)

            def turned_probs(turn, n):
                act.wait_ge(turned.sem, turned.at(turn, n))
                act.wait_ge(mixed.sem, mixed.at(turn, n - 2))
                nc.scalar.activation(pt_hi[:, n % 2, :, :], ps_turned[:, :, :], ACT.Copy).then_inc(turned_hi.sem, 1)

            def mixed_rows(turn, n):
                act.wait_ge(mixed.sem, mixed.at(turn, n))
                full, low = slice(0, P), slice(0, TAIL)
                nc.scalar.activation(o_place(o_hi, full, n), from_mixed(ps_mixed, full), ACT.Copy)
                nc.scalar.activation(o_place(o_stack, low, n), from_mixed(ps_mixed_tail, low), ACT.Copy).then_inc(mixed_hi.sem, 1)

            def before():
                split_x(0, -SLOTS_BEFORE, -1)
                act.wait_ge(biases_loaded, 48)
                split_qk(0, 1 - SLOTS_BEFORE)

            def body(turn, more):
                split_v(turn, 0)
                for n in range(QUADS):
                    act.wait_ge(max_ready.sem, max_ready.at(turn, n))
                    act.wait_ge(turned.sem, turned.at(turn, n - QUADS))
                    for j in range(QUAD):
                        last = nc.scalar.activation(probs[:, n, j, :], ps_scores[:, n % 2, j, :], ACT.Exp,
                                                    bias=neg_max[:, n, j:j + 1], accum_out=sums[:, n, j:j + 1])
                    last.then_inc(exps_ready.sem, 1)
                if more:
                    split_x(turn, VCUTS, 0)
                    split_qk(turn, VCUTS + 1)
                for n in (0, 1):
                    turned_probs(turn, n)
                for n in (0, 1):
                    mixed_rows(turn, n)
                split_v(turn, 1)
                for n in (2, 3):
                    turned_probs(turn, n)
                for n in (2, 3):
                    mixed_rows(turn, n)

            turns(act, before, body)

        @block.vector
        def _(dve):
            def norm(turn, event):
                steps = Steps(dve, dve_step, turn, event * NORM_STEPS, passed=keep["passed"])
                dve.wait_ge(x_loaded.sem, x_loaded.at(turn, event))
                moments_of(nc, steps, stats, moments, [xin[:, b, :] for b in range(UNIT)])
                inverse_root(nc, steps, moments[:, :, 1], 1e-5, half[:, :], guess[:, :], rstd[:, :], work[:, :])
                for b in range(UNIT):
                    for to, of in ((slice(0, D), slice(0, D)), (slice(D, D + TAIL), slice(MAIN, D))):
                        last = nc.vector.tensor_scalar(xn[:, b, to], xin[:, b, of], moments[:, b, 0:1], rstd[:, b:b + 1],
                                                       ALU.subtract, ALU.mult)
                last.then_inc(xn_ready.sem, 1)

            def split_x(turn, slot, event):
                dve.wait_ge(ring_hi.sem, ring_hi.at(turn, event * (1 + QK_SLOTS)))
                nc.vector.tensor_tensor(xt_lo[:, :], ring[:, bank(slot), 0:UT], raw(xt_hi[:, :]), ALU.subtract)
                nc.vector.tensor_tensor(xt_twin_lo[:, :], ring[:, bank(slot), UT:2 * UT], raw(xt_twin_hi[:, :]), ALU.subtract).then_inc(ring_free.sem, 1)

            def split_qk(turn, slot, event):
                for s in range(QK_SLOTS):
                    is_k, main, pair = qk_place(s)
                    bias = b_qk[:, s:s + 1]
                    dve.wait_ge(ring_hi.sem, ring_hi.at(turn, event * (1 + QK_SLOTS) + 1 + s))
                    if main is not None:
                        hi, lo = (k_hi, k_lo) if is_k else (q_hi, q_lo)
                        last = nc.vector.scalar_tensor_tensor(out=spread(lo, None, main), in0=from_ring(slot + s), scalar=bias,
                                                              in1=raw(spread(hi, None, main)), op0=ALU.add, op1=ALU.subtract)
                    else:
                        for half in range(2):
                            hi = spread(k_twin_hi if is_k else q_stack, half, pair + half)
                            lo = spread(k_twin_lo, half, pair + half) if is_k else spread(q_stack, 1 - half, pair + half)
                            last = nc.vector.scalar_tensor_tensor(out=lo, in0=from_ring(slot + s, half), scalar=bias[half * TAIL:(half + 1) * TAIL, :],
                                                                  in1=raw(hi), op0=ALU.add, op1=ALU.subtract)
                    last.then_inc(ring_free.sem, 1)

            def biased_v(turn, slot, event):
                dve.wait_ge(v_sent.sem, v_sent.at(turn, event - 1))
                for s in range(VCUTS):
                    cols = slice(s * VCUT, (s + 1) * VCUT)
                    dve.wait_ge(ring_filled.sem, ring_filled.at(turn, slot + s))
                    nc.vector.tensor_tensor(v_flat[:, cols], ring[:, bank(slot + s), :], b_v[:, cols], ALU.add).then_inc(ring_free.sem, 1)

            def split_v(turn, b):
                dve.wait_ge(v_hi_ready.sem, v_hi_ready.at(turn, b))
                nc.vector.tensor_tensor(v_lo[:, :, :], v_rows[:, :, :], raw(v_hi[:, :, :]), ALU.subtract).then_inc(v_ready.sem, 1)

            def row_max(turn, n):
                dve.wait_ge(scored.sem, scored.at(turn, n))
                nc.vector.tensor_reduce(out=neg_max[:, n, :], in_=ps_scores[:, n % 2, :, :], op=ALU.max, axis=X, negate=True).then_inc(max_ready.sem, 1)

            def invert(turn, n):
                dve.wait_ge(exps_ready.sem, exps_ready.at(turn, n))
                nc.vector.reciprocal(inverse[:, n, :], sums[:, n, :]).then_inc(inverse_ready.sem, 1)

            def turned_probs(turn, n):
                dve.wait_ge(turned_hi.sem, turned_hi.at(turn, n))
                nc.vector.tensor_tensor(pt_lo[:, n % 2, :, :], ps_turned[:, :, :], raw(pt_hi[:, n % 2, :, :]), ALU.subtract).then_inc(turned_lo.sem, 1)

            def mixed_rows(turn, n):
                full, low, high = slice(0, P), slice(0, TAIL), slice(TAIL, P)
                dve.wait_ge(mixed_hi.sem, mixed_hi.at(turn, n))
                nc.vector.tensor_tensor(o_place(o_lo, full, n), from_mixed(ps_mixed, full), raw(o_place(o_hi, full, n)), ALU.subtract)
                nc.vector.tensor_tensor(o_place(o_stack, high, n), from_mixed(ps_mixed_tail, low), raw(o_place(o_stack, low, n)), ALU.subtract).then_inc(mixed_lo.sem, 1)

            def finish(turn, slot, b):
                dve.wait_ge(residual_biased.sem, residual_biased.at(turn, 0))
                dve.wait_ge(h1_stored[b].sem, h1_stored[b].at(turn, -1))
                dve.wait_ge(ring_filled.sem, ring_filled.at(turn, slot))
                nc.vector.tensor_tensor(h1[:, b, :], ring[:, bank(slot), 0:D], residual[:, b, :], ALU.add).then_inc(ring_free.sem, 1)

            def before():
                norm(0, -1)
                dve.wait_ge(biases_loaded, 48)
                split_x(0, -SLOTS_BEFORE, -1)
                split_qk(0, 1 - SLOTS_BEFORE, -1)
                biased_v(0, -VCUTS, -1)

            def body(turn, more):
                split_v(turn, 0)
                row_max(turn, 0)
                row_max(turn, 1)
                for n in range(2, QUADS):
                    invert(turn, n - 2)
                    row_max(turn, n)
                invert(turn, QUADS - 2)
                invert(turn, QUADS - 1)
                dve.wait_ge(residual_loaded.sem, residual_loaded.at(turn, 0))
                nc.vector.tensor_tensor(residual[:, :, :], residual[:, :, :], b_proj[:, :].unsqueeze(1).to_broadcast([P, UNIT, D]), ALU.add).then_inc(residual_biased.sem, 1)
                slot = 0
                biased_v(turn, slot, 0)
                slot += VCUTS
                if more:
                    norm(turn, 0)
                    split_x(turn, slot, 0)
                    split_qk(turn, slot + 1, 0)
                    slot += 1 + QK_SLOTS
                for n in (0, 1):
                    turned_probs(turn, n)
                for n in (0, 1):
                    mixed_rows(turn, n)
                if more:
                    biased_v(turn, slot, 1)
                    slot += VCUTS
                finish(turn, slot, 0)
                split_v(turn, 1)
                for n in (2, 3):
                    turned_probs(turn, n)
                for n in (2, 3):
                    mixed_rows(turn, n)
                finish(turn, slot + 1, 1)

            turns(dve, before, body)


def mixer(nc, keep, dram):
    UNIT = 4
    UNITS = TILES // UNIT
    UT = UNIT * P
    RING = 2
    SETS = HEADS // QUAD
    VV = 2 * HD
    with ExitStack() as ctx:
        sb = lambda name, shape, dt=F32: ctx.enter_context(nc.sbuf_tensor(f"mix_{name}", shape, dt))
        ps = lambda name, shape: ctx.enter_context(nc.psum_tensor(f"mix_{name}", shape, F32))
        sem = lambda name: ctx.enter_context(nc.semaphore(f"mix_{name}"))
        QK = 2 * SETS * P
        W_IN = QK + D
        raw_in = sb("raw_in", [P, 2, W_IN + D])
        w_hi, w_lo, w_half, w_stack = (sb(f"w_{n}", [P, W_IN + D], F32R) for n in ("hi", "lo", "half", "stack"))
        b_qk = sb("b_qk", [P, 2 * SETS])
        b_low = sb("b_low", [P, 2 * SETS])
        b_v, b_out, gain, shift = (sb(n, [P, D]) for n in ("b_v", "b_out", "gain", "shift"))
        low_rows = sb("low_rows", [P, 1])
        lane = sb("lane", [P, 1], I32)
        hin = sb("hin", [P, UNIT, D])
        y = sb("y", [P, UNIT, D])
        residual = sb("residual", [P, UNIT, D])
        zn = sb("zn", [P, UNIT, MAIN + 2 * TAIL])
        zt_hi, zt_lo = (sb(n, [P, 2, UT], F32R) for n in ("zt_hi", "zt_lo"))
        q_low, q_stack, k_hi, k_lo = (sb(n, [P, SETS, UT], F32R) for n in ("q_low", "q_stack", "k_hi", "k_lo"))
        v_sum = sb("v_sum", [P, UNIT, D])
        vv = sb("vv", [P, UNIT, HEADS, VV], F32R)
        probs = sb("probs", [P, 2, HEADS, P])
        pt_hi = sb("pt_hi", [P, 2, QUAD, P], F32R)
        pt_lo = sb("pt_lo", [P, 2, QUAD, P], F32R)
        context = sb("context", [P, 2, MAIN + 2 * TAIL])
        ct_hi, ct_lo = (sb(n, [P, 2, P], F32R) for n in ("ct_hi", "ct_lo"))
        x2 = sb("x2", [P, 2, D])
        top = sb("top", [P, 2, QUAD, SETS])
        neg_max = sb("neg_max", [P, 2, QUAD, SETS])
        sums = sb("sums", [P, 2, HEADS])
        inverse = sb("inverse", [P, 2, HEADS])
        stats = sb("stats", [P, UNIT, 6])
        moments = sb("moments", [P, UNIT, 2])
        half, guess, rstd, work = (sb(n, [P, UNIT]) for n in ("half", "guess", "rstd", "work"))
        stage, w1_half = raw_in[:, :, 0:HID], w_half[:, 0:HID]
        stage2 = sb("stage2", [P, HC, D])
        ps_scores = ps("ps_scores", [P, QUAD, 512])
        ring = ps("ring", [P, RING, 512])
        ps_turned = ps("ps_turned", [P, QUAD, P])
        ps_context = ps("ps_context", [P, 512])

        QK_SLOTS = 2 * SETS
        SLOTS_BEFORE = 2 + QK_SLOTS + UNIT
        SLOTS = SLOTS_BEFORE + 2 * UNIT
        assert SLOTS % RING == 0 and SLOTS_BEFORE % RING == 0
        bank = lambda slot: slot % RING
        SETS_TURN = UNIT * SETS
        ring_filled = Signal(sem("ring_filled"), SLOTS, SLOTS_BEFORE)
        HIS = 2 + QK_SLOTS + UNIT
        ring_hi = Signal(sem("ring_hi"), HIS, 2 + QK_SLOTS)
        ring_free = Signal(sem("ring_free"), SLOTS, SLOTS_BEFORE, lent=RING)
        h_loaded = Signal(sem("h_loaded"), 1, 1, step=16)
        zn_ready = Signal(sem("zn_ready"), 1, 1)
        v_hi_ready = Signal(sem("v_hi_ready"), UNIT, UNIT)
        vv_ready = Signal(sem("vv_ready"), UNIT, UNIT)
        scored = Signal(sem("scored"), UNIT)
        max_ready = Signal(sem("max_ready"), UNIT)
        exps_ready = Signal(sem("exps_ready"), UNIT, lent=1)
        inverse_ready = Signal(sem("inverse_ready"), UNIT)
        turned = Signal(sem("turned"), SETS_TURN, lent=2 * SETS)
        turned_hi = Signal(sem("turned_hi"), SETS_TURN)
        turned_lo = Signal(sem("turned_lo"), SETS_TURN, lent=1)
        mixed = Signal(sem("mixed"), SETS_TURN, lent=2)
        context_read = Signal(sem("context_read"), UNIT, lent=1)
        context_ready = Signal(sem("context_ready"), UNIT)
        x2_stored = [Signal(sem(f"x2_stored{b}"), UNIT // 2, lent=1, step=16) for b in range(2)]
        consts_loaded, weights_ready, lane_ready, raw_loaded = sem("consts_loaded"), sem("weights_ready"), sem("lane_ready"), sem("raw_loaded")
        weight_hi = sem("weight_hi")
        residual_ready = Signal(sem("residual_ready"), 1, 1)
        dve_setup = Signal(sem("dve_setup"), 0)
        NORM = 2 * NORM_STEPS + 4
        dve_norm = Signal(sem("dve_norm"), NORM, NORM)
        MAXES = 1
        dve_max = Signal(sem("dve_max"), UNIT * MAXES)
        CONTEXTS = 1
        dve_context = Signal(sem("dve_context"), UNIT * CONTEXTS)
        pool_step = Signal(sem("pool_step"), 0)
        stage_loaded = sem("stage_loaded")
        block = ctx.enter_context(nc.Block())

        finish_slot = lambda more, b: 2 * b + ((2 + QK_SLOTS) * (b > 1) + UNIT * (b > 2)) * more
        NEXT_X, NEXT_V = 4, 4 + 2 + QK_SLOTS + 2
        his_finish = lambda b: b + (2 + QK_SLOTS) * (b > 1)
        his_next = 2

        def turns(engine, before, body):
            before()
            with engine.Fori(0, UNITS - 1) as turn:
                body(turn, True)
            body(UNITS - 1, False)

        def order(turn, more, scores, mix, finish, project, project_v):
            scores(turn, 0)
            scores(turn, 1)
            mix(turn, 0)
            scores(turn, 2)
            mix(turn, 1)
            finish(turn, more, 0)
            scores(turn, 3)
            mix(turn, 2)
            finish(turn, more, 1)
            if more:
                project(turn, NEXT_X, 0)
            mix(turn, 3)
            finish(turn, more, 2)
            if more:
                project_v(turn, NEXT_V, 0)
            finish(turn, more, 3)

        @block.sync
        def _(sp):
            for part, (to, of) in enumerate(((slice(0, P), slice(0, MAIN)), (slice(0, TAIL), slice(MAIN, D)), (slice(TAIL, P), slice(MAIN, D)))):
                sp.dma_start(raw_in[to, min(part, 1), :], dram["w_mix"][of, :]).then_inc(raw_loaded, 16)

            def load(turn, event, unit):
                if event == 0:
                    sp.wait_ge(zn_ready.sem, zn_ready.at(turn, -1))
                sp.dma_start(hin[:, :, :], dram["h1"][bass.ds(unit * UT, UT), :].rearrange("(b p) d -> p b d", p=P)).then_inc(h_loaded.sem, 16)

            def store(turn, more, b):
                sp.wait_ge(ring_free.sem, ring_free.at(turn, finish_slot(more, b) + 1))
                sp.dma_start(dram["x2"][bass.ds(turn * UT + b * P, P), :], x2[:, b % 2, :]).then_inc(x2_stored[b % 2].sem, 16)

            def body(turn, more):
                if more:
                    load(turn, 0, turn + 1)
                for b in range(UNIT):
                    store(turn, more, b)

            turns(sp, lambda: load(0, -1, 0), body)
            for b in range(2):
                sp.wait_ge(x2_stored[b].sem, x2_stored[b].at(UNITS - 1, UNIT // 2 - 1))

        @block.gpsimd
        def _(pool):
            nc.gpsimd.iota(lane[:, :], pattern=[[0, 1]], base=0, channel_multiplier=1).then_inc(lane_ready, 1)
            steps = Steps(pool, pool_step, 0)
            pool.wait_ge(weights_ready, 1)
            for f in range(FFNS):
                w1_hi, w1_lo, w1_stack, w2_hi, w2_lo = keep["ffn"][f]
                for half_rows in range(2):
                    pool.dma_start(stage[half_rows * TAIL:(half_rows + 1) * TAIL, 1, :], dram["w1"][f, MAIN:D, :]).then_inc(stage_loaded, 16)
                pool.dma_start(stage[:, 0, :], dram["w1"][f, 0:MAIN, :]).then_inc(stage_loaded, 16)
                pool.dma_start(stage2[:, :, :], dram["w2"][f].rearrange("(c p) n -> p c n", p=P)).then_inc(stage_loaded, 16)
                pool.wait_ge(stage_loaded, 64 * (f + 1))
                main, tail = stage[:, 0, :], stage[:, 1, :]
                nc.gpsimd.tensor_scalar(w1_hi[:, :], main, 1.0, 1.0, ALU.mult, ALU.mult)
                nc.gpsimd.tensor_scalar(w2_hi[:, :, :], stage2[:, :, :], 1.0, 1.0, ALU.mult, ALU.mult)
                steps.then(nc.gpsimd.tensor_scalar(w1_half, tail, keep["low_rows"][:, 0:1], 1.0, ALU.mult, ALU.mult))
                nc.gpsimd.tensor_tensor(w1_lo[:, :], main, raw(w1_hi[:, :]), ALU.subtract)
                nc.gpsimd.tensor_tensor(w2_lo[:, :, :], stage2[:, :, :], raw(w2_hi[:, :, :]), ALU.subtract)
                steps.then(nc.gpsimd.tensor_tensor(w1_stack[:, :], tail, raw(w1_half), ALU.subtract))

        @block.tensor
        def _(pe):
            def slot_free(turn, slot):
                pe.wait_ge(ring_free.sem, ring_free.at(turn, slot - RING))

            def scores(turn, b):
                if b == 0:
                    pe.wait_ge(ring_free.sem, ring_free.at(turn, -UNIT - 1))
                pe.wait_ge(exps_ready.sem, exps_ready.at(turn, b - 1))
                tile = slice(b * P, (b + 1) * P)
                for s in range(SETS):
                    for i, k in enumerate((k_hi, k_lo)):
                        for j in range(QUAD):
                            rows = slice(32 * j, 32 * j + 32)
                            last = nc.tensor.matmul(ps_scores[:, j, s * P:(s + 1) * P], q_stack[rows, s, tile], k[rows, s, tile], start=i == 0, stop=i == 1)
                last.then_inc(scored.sem, 1)

            def mix(turn, b):
                pe.wait_ge(exps_ready.sem, exps_ready.at(turn, b))
                pe.wait_ge(vv_ready.sem, vv_ready.at(turn, b - UNIT))

                def turn_set(s):
                    n = b * SETS + s
                    pe.wait_ge(turned_lo.sem, turned_lo.at(turn, n - 1))
                    for j in range(QUAD):
                        last = nc.tensor.transpose(ps_turned[:, j, :], probs[:, b % 2, s * QUAD + j, :], keep["ident"][:, :])
                    last.then_inc(turned.sem, 1)

                turn_set(0)
                for s in range(SETS):
                    n = b * SETS + s
                    if s + 1 < SETS:
                        turn_set(s + 1)
                    pe.wait_ge(turned_lo.sem, turned_lo.at(turn, n))
                    if s == 0:
                        pe.wait_ge(context_read.sem, context_read.at(turn, b - 1))
                    for j in range(QUAD):
                        h = s * QUAD + j
                        nc.tensor.matmul(ps_context[:, h * VV:(h + 1) * VV], pt_hi[:, n % 2, j, :], vv[:, b, h, :], start=True, stop=False)
                        last = nc.tensor.matmul(ps_context[:, h * VV:h * VV + HD], pt_lo[:, n % 2, j, :], vv[:, b, h, 0:HD], start=False, stop=True)
                    last.then_inc(mixed.sem, 1)

            def finish(turn, more, b):
                slot = finish_slot(more, b)
                pe.wait_ge(context_ready.sem, context_ready.at(turn, b))
                slot_free(turn, slot)
                for part in range(2):
                    last = nc.tensor.transpose(ring[:, bank(slot), part * P:(part + 1) * P], context[:, b % 2, part * P:(part + 1) * P], keep["ident"][:, :])
                last.then_inc(ring_filled.sem, 1)
                pe.wait_ge(ring_free.sem, ring_free.at(turn, slot))
                out = slice(W_IN, W_IN + D)
                passes = ((ct_hi[:, 0, :], w_hi), (ct_lo[:, 0, :], w_hi), (ct_hi[:, 0, :], w_lo), (ct_hi[:, 1, :], w_stack), (ct_lo[:, 1, :], w_stack))
                for i, (c, w) in enumerate(passes):
                    last = nc.tensor.matmul(ring[:, bank(slot + 1), 0:D], c, w[:, out], start=i == 0, stop=i == 4)
                last.then_inc(ring_filled.sem, 1)

            def project(turn, slot, event):
                pe.wait_ge(zn_ready.sem, zn_ready.at(turn, event))
                for part in range(2):
                    slot_free(turn, slot + part)
                    for b in range(UNIT):
                        last = nc.tensor.transpose(ring[:, bank(slot + part), b * P:(b + 1) * P], zn[:, b, part * P:(part + 1) * P], keep["ident"][:, :])
                    last.then_inc(ring_filled.sem, 1)
                pe.wait_ge(ring_free.sem, ring_free.at(turn, slot + 1))
                for s in range(QK_SLOTS):
                    slot_free(turn, slot + 2 + s)
                    cols = slice(s * P, (s + 1) * P)
                    passes = ((w_hi, zt_hi, 0), (w_hi, zt_lo, 0), (w_lo, zt_hi, 0), (w_stack, zt_hi, 1), (w_stack, zt_lo, 1))
                    for i, (w, z, part) in enumerate(passes):
                        last = nc.tensor.matmul(ring[:, bank(slot + 2 + s), :], w[:, cols], z[:, part, :], start=i == 0, stop=i == 4)
                    last.then_inc(ring_filled.sem, 1)

            def project_v(turn, slot, event):
                for b in range(UNIT):
                    slot_free(turn, slot + b)
                    tile = slice(b * P, (b + 1) * P)
                    passes = ((w_hi, zt_hi, 0), (w_hi, zt_lo, 0), (w_lo, zt_hi, 0), (w_stack, zt_hi, 1), (w_stack, zt_lo, 1))
                    for i, (w, z, part) in enumerate(passes):
                        last = nc.tensor.matmul(ring[:, bank(slot + b), 0:D], z[:, part, tile], w[:, QK:W_IN], start=i == 0, stop=i == 4)
                    last.then_inc(ring_filled.sem, 1)

            def before():
                pe.wait_ge(weights_ready, 1)
                project(0, -SLOTS_BEFORE, -1)
                project_v(0, -UNIT, -1)

            turns(pe, before, lambda turn, more: order(turn, more, scores, mix, finish, project, project_v))

        @block.scalar
        def _(act):
            act.dma_start(b_qk[:, :], dram["b_mix_qk"]).then_inc(consts_loaded, 16)
            for to, of in ((b_v, "b_mix_v"), (b_out, "b_mix_out"), (gain, "ln1_g"), (shift, "ln1_b")):
                act.dma_start(to[:, :], dram[of].to_broadcast([P, D])).then_inc(consts_loaded, 16)
            for signal in (ring_free, exps_ready, turned, turned_lo, mixed, context_read, *x2_stored):
                signal.lend(act)
            act.wait_ge(raw_loaded, 48)
            nc.scalar.activation(w_hi[:, :], raw_in[:, 0, :], ACT.Copy)
            nc.scalar.activation(w_half[:, :], raw_in[:, 1, :], ACT.Copy, scale=keep["low_rows"][:, 0:1]).then_inc(weight_hi, 1)

            def scores(turn, b):
                act.wait_ge(max_ready.sem, max_ready.at(turn, b))
                act.wait_ge(turned.sem, turned.at(turn, (b - 1) * SETS - 1))
                for s in range(SETS):
                    for j in range(QUAD):
                        h = s * QUAD + j
                        last = nc.scalar.activation(probs[:, b % 2, h, :], ps_scores[:, j, s * P:(s + 1) * P], ACT.Exp,
                                                    bias=neg_max[:, b % 2, j, s:s + 1], scale=float(HD) ** -0.5, accum_out=sums[:, b % 2, h:h + 1])
                last.then_inc(exps_ready.sem, 1)

            def mix(turn, b):
                for s in range(SETS):
                    n = b * SETS + s
                    act.wait_ge(turned.sem, turned.at(turn, n))
                    act.wait_ge(mixed.sem, mixed.at(turn, n - 2))
                    nc.scalar.activation(pt_hi[:, n % 2, :, :], ps_turned[:, :, :], ACT.Copy).then_inc(turned_hi.sem, 1)

            def finish(turn, more, b):
                slot = finish_slot(more, b)
                act.wait_ge(ring_filled.sem, ring_filled.at(turn, slot))
                nc.scalar.activation(ct_hi[:, :, :], ring[:, bank(slot), 0:2 * P].rearrange("p (a t) -> p a t", a=2), ACT.Copy).then_inc(ring_hi.sem, 1)

            def project(turn, slot, event):
                for part in range(2):
                    act.wait_ge(ring_filled.sem, ring_filled.at(turn, slot + part))
                    nc.scalar.activation(zt_hi[:, part, :], ring[:, bank(slot + part), :], ACT.Copy).then_inc(ring_hi.sem, 1)
                for s in range(QK_SLOTS):
                    act.wait_ge(ring_filled.sem, ring_filled.at(turn, slot + 2 + s))
                    if s < SETS:
                        last = nc.scalar.activation(q_low[:, s, :], ring[:, bank(slot + 2 + s), :], ACT.Identity, scale=low_rows[:, 0:1], bias=b_low[:, s:s + 1])
                    else:
                        last = nc.scalar.activation(k_hi[:, s - SETS, :], ring[:, bank(slot + 2 + s), :], ACT.Identity, bias=b_qk[:, s:s + 1])
                    last.then_inc(ring_hi.sem, 1)

            def project_v(turn, slot, event):
                for b in range(UNIT):
                    act.wait_ge(ring_free.sem, ring_free.at(turn, slot + b))
                    nc.scalar.activation(vv[:, b, :, 0:HD], v_sum[:, b, :].rearrange("p (h d) -> p h d", d=HD), ACT.Copy).then_inc(v_hi_ready.sem, 1)

            def before():
                act.wait_ge(weights_ready, 1)
                project(0, -SLOTS_BEFORE, -1)
                project_v(0, -UNIT, -1)

            turns(act, before, lambda turn, more: order(turn, more, scores, mix, finish, project, project_v))

        @block.vector
        def _(dve):
            def setup():
                steps = Steps(dve, dve_setup, 0)
                dve.wait_ge(lane_ready, 1)
                steps.then(nc.vector.tensor_scalar(lane[:, :], lane[:, :], HD, None, ALU.bitwise_and))
                steps.then(nc.vector.tensor_scalar(low_rows[:, :], lane[:, :], 1.0 / HD, 1.0, ALU.mult, ALU.mult))
                dve.wait_ge(consts_loaded, 16 * 5)
                nc.vector.tensor_scalar(b_low[:, :], b_qk[:, :], low_rows[:, 0:1], 1.0, ALU.mult, ALU.mult)
                dve.wait_ge(weight_hi, 1)
                nc.vector.tensor_tensor(w_lo[:, :], raw_in[:, 0, :], raw(w_hi[:, :]), ALU.subtract)
                nc.vector.tensor_tensor(w_stack[:, :], raw_in[:, 1, :], raw(w_half[:, :]), ALU.subtract).then_inc(weights_ready, 1)

            def norm(turn, event):
                steps = Steps(dve, dve_norm, turn, event * NORM, passed=keep["passed"])
                dve.wait_ge(h_loaded.sem, h_loaded.at(turn, event))
                root = lambda: inverse_root(nc, steps, moments[:, :, 1], 1e-5, half[:, :], guess[:, :], rstd[:, :], work[:, :])
                moments_of(nc, steps, stats, moments, [hin[:, b, :] for b in range(UNIT)])
                root()
                for b in range(UNIT):
                    last = nc.vector.tensor_scalar(y[:, b, :], hin[:, b, :], moments[:, b, 0:1], rstd[:, b:b + 1], ALU.subtract, ALU.mult)
                steps.then(last)
                moments_of(nc, steps, stats, moments, [y[:, b, :] for b in range(UNIT)])
                root()
                for b in range(UNIT):
                    last = nc.vector.tensor_scalar(zn[:, b, 0:D], y[:, b, :], moments[:, b, 0:1], rstd[:, b:b + 1], ALU.subtract, ALU.mult)
                steps.then(last)
                wide = lambda row: row[:, :].unsqueeze(1).to_broadcast([P, UNIT, D])
                steps.then(nc.vector.tensor_tensor(zn[:, :, 0:D], zn[:, :, 0:D], wide(gain), ALU.mult))
                steps.then(nc.vector.tensor_tensor(zn[:, :, 0:D], zn[:, :, 0:D], wide(shift), ALU.add))
                nc.vector.tensor_copy(zn[:, :, D:D + TAIL], zn[:, :, MAIN:D]).then_inc(zn_ready.sem, 1)

            def scores(turn, b):
                steps = Steps(dve, dve_max, turn, b)
                dve.wait_ge(scored.sem, scored.at(turn, b))
                steps.then(nc.vector.tensor_reduce(out=top[:, b % 2, :, :], in_=ps_scores[:, :, 0:SETS * P].rearrange("p j (s k) -> p j s k", k=P),
                                                   op=ALU.max, axis=X, negate=True))
                nc.vector.tensor_scalar(neg_max[:, b % 2, :, :], top[:, b % 2, :, :], float(HD) ** -0.5, 1.0, ALU.mult, ALU.mult).then_inc(max_ready.sem, 1)

            def mix(turn, b):
                dve.wait_ge(exps_ready.sem, exps_ready.at(turn, b))
                nc.vector.reciprocal(inverse[:, b % 2, :], sums[:, b % 2, :]).then_inc(inverse_ready.sem, 1)
                for s in range(SETS):
                    n = b * SETS + s
                    dve.wait_ge(turned_hi.sem, turned_hi.at(turn, n))
                    nc.vector.tensor_tensor(pt_lo[:, n % 2, :, :], ps_turned[:, :, :], raw(pt_hi[:, n % 2, :, :]), ALU.subtract).then_inc(turned_lo.sem, 1)
                steps = Steps(dve, dve_context, turn, b * CONTEXTS)
                own = context[:, b % 2, 0:D]
                dve.wait_ge(mixed.sem, mixed.at(turn, (b + 1) * SETS - 1))
                nc.vector.tensor_reduce(out=own, in_=ps_context[:, 0:HEADS * VV].rearrange("p (h a d) -> p h d a", a=2, d=HD),
                                        op=ALU.add, axis=X).then_inc(context_read.sem, 1)
                dve.wait_ge(context_read.sem, context_read.at(turn, b))
                dve.wait_ge(inverse_ready.sem, inverse_ready.at(turn, b))
                by_head = own.rearrange("p (h d) -> p h d", d=HD)
                steps.then(nc.vector.tensor_tensor(by_head, by_head, inverse[:, b % 2, :].unsqueeze(2).to_broadcast([P, HEADS, HD]), ALU.mult))
                nc.vector.tensor_copy(context[:, b % 2, D:D + TAIL], context[:, b % 2, MAIN:D]).then_inc(context_ready.sem, 1)

            def finish(turn, more, b):
                slot = finish_slot(more, b)
                dve.wait_ge(ring_hi.sem, ring_hi.at(turn, his_finish(b) if more else b))
                nc.vector.tensor_tensor(ct_lo[:, :, :], ring[:, bank(slot), 0:2 * P].rearrange("p (a t) -> p a t", a=2), raw(ct_hi[:, :, :]), ALU.subtract).then_inc(ring_free.sem, 1)
                if b == 0:
                    dve.wait_ge(residual_ready.sem, residual_ready.at(turn, -1))
                dve.wait_ge(x2_stored[b % 2].sem, x2_stored[b % 2].at(turn, b // 2 - 1))
                dve.wait_ge(ring_filled.sem, ring_filled.at(turn, slot + 1))
                nc.vector.tensor_tensor(x2[:, b % 2, :], ring[:, bank(slot + 1), 0:D], residual[:, b, :], ALU.add).then_inc(ring_free.sem, 1)

            def project(turn, slot, event):
                norm(turn, event)
                his = his_next + event * (2 + QK_SLOTS) if event == 0 else -(2 + QK_SLOTS)
                for part in range(2):
                    dve.wait_ge(ring_hi.sem, ring_hi.at(turn, his + part))
                    nc.vector.tensor_tensor(zt_lo[:, part, :], ring[:, bank(slot + part), :], raw(zt_hi[:, part, :]), ALU.subtract).then_inc(ring_free.sem, 1)
                for s in range(QK_SLOTS):
                    dve.wait_ge(ring_hi.sem, ring_hi.at(turn, his + 2 + s))
                    out, hi = (q_stack[:, s, :], q_low[:, s, :]) if s < SETS else (k_lo[:, s - SETS, :], k_hi[:, s - SETS, :])
                    nc.vector.scalar_tensor_tensor(out=out, in0=ring[:, bank(slot + 2 + s), :], scalar=b_qk[:, s:s + 1], in1=raw(hi),
                                                   op0=ALU.add, op1=ALU.subtract).then_inc(ring_free.sem, 1)

            def project_v(turn, slot, event):
                for b in range(UNIT):
                    n = event * UNIT + b
                    dve.wait_ge(ring_filled.sem, ring_filled.at(turn, slot + b))
                    nc.vector.tensor_tensor(v_sum[:, b, :], ring[:, bank(slot + b), 0:D], b_v[:, :], ALU.add).then_inc(ring_free.sem, 1)
                for b in range(UNIT):
                    dve.wait_ge(v_hi_ready.sem, v_hi_ready.at(turn, event * UNIT + b))
                    by_head = lambda t: t.rearrange("p (h d) -> p h d", d=HD)
                    nc.vector.tensor_tensor(vv[:, b, :, HD:VV], by_head(v_sum[:, b, :]), raw(vv[:, b, :, 0:HD]), ALU.subtract).then_inc(vv_ready.sem, 1)

            def add_bias(turn, event):
                nc.vector.tensor_tensor(residual[:, :, :], y[:, :, :], b_out[:, :].unsqueeze(1).to_broadcast([P, UNIT, D]), ALU.add).then_inc(residual_ready.sem, 1)

            def before():
                setup()
                project(0, -SLOTS_BEFORE, -1)
                project_v(0, -UNIT, -1)
                add_bias(0, -1)

            def body(turn, more):
                order(turn, more, scores, mix, finish, project, project_v)
                if more:
                    dve.wait_ge(ring_free.sem, ring_free.at(turn, SLOTS - 1))
                    add_bias(turn, 0)

            turns(dve, before, body)


def experts(nc, keep, dram):
    UNIT = 4
    UNITS = TILES // UNIT
    UT = UNIT * P
    RING = 4
    with ExitStack() as ctx:
        sb = lambda name, shape, dt=F32: ctx.enter_context(nc.sbuf_tensor(f"ffn_{name}", shape, dt))
        ps = lambda name, shape: ctx.enter_context(nc.psum_tensor(f"ffn_{name}", shape, F32))
        sem = lambda name: ctx.enter_context(nc.semaphore(f"ffn_{name}"))
        b1 = sb("b1", [P, FFNS * HC])
        b2 = sb("b2", [P, FFNS, D])
        gain, shift = sb("gain", [P, D]), sb("shift", [P, D])
        raw_gate = sb("raw_gate", [P, 2, NEXP])
        g_hi, g_lo, g_half, g_stack = (sb(f"gate_{n}", [P, NEXP], F32R) for n in ("hi", "lo", "half", "stack"))
        b_gate = sb("b_gate", [P, NEXP])
        earlier = sb("earlier", [P, NEXP, NEXP])
        x2 = sb("x2", [P, UNIT, MAIN + 2 * TAIL])
        h1 = sb("h1", [P, UNIT, D])
        x3 = sb("x3", [P, UNIT, D])
        base = sb("base", [P, UNIT, D])
        xn = sb("xn", [P, UNIT, MAIN + 2 * TAIL])
        total = sb("total", [P, UNIT, D])
        xt = {kind: tuple(sb(f"{kind}_{n}", [P, 2, UT], F32R) for n in ("hi", "lo")) for kind in ("mlp", "exp")}
        gelu = sb("gelu", [P, 2, UT])
        hid_hi = sb("hid_hi", [P, 3, UT], F32R)
        hid_lo = sb("hid_lo", [P, 3, UT], F32R)
        logits = sb("logits", [P, UNIT, NEXP])
        rank4 = sb("rank4", [P, UNIT, NEXP, NEXP])
        ties = sb("ties", [P, UNIT, NEXP, NEXP])
        rank = sb("rank", [P, UNIT, NEXP])
        best = sb("best", [P, UNIT])
        chosen = sb("chosen", [P, UNIT, NEXP])
        exps = sb("exps", [P, UNIT, NEXP])
        gates = sb("gates", [P, UNIT, NEXP])
        stats = sb("stats", [P, UNIT, 6])
        moments = sb("moments", [P, UNIT, 2])
        half, guess, rstd, work = (sb(n, [P, UNIT]) for n in ("half", "guess", "rstd", "work"))
        ring = ps("ring", [P, RING, 512])
        ps_out = ps("ps_out", [P, UNIT, 512])

        LAG = 2
        chunks_of = lambda ffns: [(f, c) for f in ffns for c in range(HC)]
        CHUNKS_TURN, CHUNKS_BEFORE = FFNS * HC, HC
        assert CHUNKS_TURN % 6 == 0 and CHUNKS_BEFORE % 6 == 0
        IN, GATE = 2, 2
        SLOTS_BEFORE = IN + CHUNKS_BEFORE + IN + GATE
        SLOTS = IN + CHUNKS_TURN + IN + GATE
        assert SLOTS_BEFORE % RING == 0 and SLOTS % RING == 0
        bank = lambda slot: slot % RING
        ring_filled = Signal(sem("ring_filled"), SLOTS, SLOTS_BEFORE)
        ring_free = Signal(sem("ring_free"), SLOTS, SLOTS_BEFORE, lent=RING)
        chunk_read = Signal(sem("chunk_read"), CHUNKS_TURN, CHUNKS_BEFORE)
        inputs_hi = Signal(sem("inputs_hi"), 2 * IN, 2 * IN)
        hi_ready = Signal(sem("hi_ready"), CHUNKS_TURN, CHUNKS_BEFORE)
        lo_ready = Signal(sem("lo_ready"), CHUNKS_TURN, CHUNKS_BEFORE, lent=2)
        hid_used = Signal(sem("hid_used"), CHUNKS_TURN, CHUNKS_BEFORE, lent=3)
        out_free = Signal(sem("out_free"), FFNS * UNIT, UNIT, lent=UNIT)
        x2_loaded = Signal(sem("x2_loaded"), 1, 1, step=48)
        mlp_done = Signal(sem("mlp_done"), 1, 1)
        xn_ready = Signal(sem("xn_ready"), 1, 1)
        logits_ready = Signal(sem("logits_ready"), 1)
        gate_exps = Signal(sem("gate_exps"), 1)
        total_ready = Signal(sem("total_ready"), NEXP)
        out_stored = Signal(sem("out_stored"), 1, lent=1, step=16)
        consts_loaded, gate_loaded, gate_hi, gate_ready, ones_ready = (sem(n) for n in ("consts_loaded", "gate_loaded", "gate_hi", "gate_ready", "ones_ready"))
        NORM = NORM_STEPS + 5
        dve_norm = Signal(sem("dve_norm"), NORM, NORM)
        GATE_STEPS = 10
        dve_gate = Signal(sem("dve_gate"), GATE_STEPS)
        block = ctx.enter_context(nc.Block())

        def walk(turn, ffns, first, slot, out, following, do):
            chunks = chunks_of(ffns)

            def second(i):
                f, c = chunks[i]
                do.layer2(turn, first + i, out + i // HC, f, c)
                if c == HC - 1:
                    do.finish(turn, first + i, out + i // HC, f)

            for i, (f, c) in enumerate(chunks):
                if (f, c) == (0, 0):
                    do.inputs(turn, slot, 0, following)
                    slot += IN
                do.layer1(turn, first + i, slot, f, c)
                slot += 1
                if i >= LAG:
                    second(i - LAG)
            behind = range(len(chunks) - LAG, len(chunks))
            if ffns[-1] == 0:
                for i in behind:
                    second(i)
            if following is not None:
                do.inputs(turn, slot, 1, following)
                do.gates(turn, slot + IN)
            if ffns[-1] != 0:
                for i in behind:
                    second(i)

        def turns(engine, do):
            walk(0, [0], -CHUNKS_BEFORE, -SLOTS_BEFORE, -1, -1, do)
            with engine.Fori(0, UNITS - 1) as turn:
                do.begin(turn)
                walk(turn, [1, 2, 0, 3, 4], 0, 0, 0, 0, do)
            do.begin(UNITS - 1)
            walk(UNITS - 1, [1, 2, 3, 4], 0, 0, 0, None, do)

        class Steps_of:

            def begin(self, turn): pass
            def inputs(self, turn, slot, kind, event): pass
            def gates(self, turn, slot): pass
            def layer1(self, turn, i, slot, f, c): pass
            def layer2(self, turn, i, out, f, c): pass
            def finish(self, turn, i, out, f): pass

        @block.sync
        def _(sp):
            def load(turn, event, unit):
                if event == 0:
                    sp.wait_ge(mlp_done.sem, mlp_done.at(turn, -1))
                view = lambda name: dram[name][bass.ds(unit * UT, UT), :].rearrange("(b p) d -> p b d", p=P)
                sp.dma_start(x2[:, :, 0:D], view("x2")).then_inc(x2_loaded.sem, 16)
                sp.dma_start(x2[:, :, D:D + TAIL], view("x2")[:, :, MAIN:D]).then_inc(x2_loaded.sem, 16)
                sp.dma_start(h1[:, :, :], view("h1")).then_inc(x2_loaded.sem, 16)

            def store(turn):
                sp.wait_ge(total_ready.sem, total_ready.at(turn, NEXP - 1))
                sp.dma_start(dram["out"][bass.ds(turn * UT, UT), :].rearrange("(b p) d -> p b d", p=P), total[:, :, :]).then_inc(out_stored.sem, 16)

            load(0, -1, 0)
            with sp.Fori(0, UNITS - 1) as turn:
                load(turn, 0, turn + 1)
                store(turn)
            store(UNITS - 1)
            sp.wait_ge(out_stored.sem, out_stored.at(UNITS - 1, 0))

        @block.gpsimd
        def _(pool):
            nc.gpsimd.memset(earlier[:, :, :], 1.0).then_inc(ones_ready, 1)
            pool.wait_ge(ones_ready, 1)
            nc.gpsimd.affine_select(out=earlier[:, :, :], in_=earlier[:, :, :], compare_op=ALU.is_gt, fill=0.0,
                                    base=0, pattern=[[1, NEXP], [-1, NEXP]], channel_multiplier=0).then_inc(ones_ready, 1)

        @block.tensor
        def _(pe):
            def slot_free(turn, slot):
                pe.wait_ge(ring_free.sem, ring_free.at(turn, slot - RING))

            class Do(Steps_of):
                def inputs(self, turn, slot, kind, event):
                    x = (x2, xn)[kind]
                    if kind == 0:
                        pe.wait_ge(x2_loaded.sem, x2_loaded.at(turn, event))
                    else:
                        pe.wait_ge(xn_ready.sem, xn_ready.at(turn, event))
                    for part in range(2):
                        slot_free(turn, slot + part)
                        for b in range(UNIT):
                            last = nc.tensor.transpose(ring[:, bank(slot + part), b * P:(b + 1) * P], x[:, b, part * P:(part + 1) * P], keep["ident"][:, :])
                        last.then_inc(ring_filled.sem, 1)
                    if kind == 0:
                        pe.wait_ge(ring_free.sem, ring_free.at(turn, slot + 1))

                def gates(self, turn, slot):
                    pe.wait_ge(gate_ready, 1)
                    pe.wait_ge(ring_free.sem, ring_free.at(turn, slot - 1))
                    x_hi, x_lo = xt["exp"]
                    passes = ((g_hi, x_hi, 0), (g_hi, x_lo, 0), (g_lo, x_hi, 0), (g_stack, x_hi, 1), (g_stack, x_lo, 1))
                    for b in range(UNIT):
                        at, column = slot + b // 2, (b % 2) * NEXP
                        slot_free(turn, at)
                        for k, (g, x, part) in enumerate(passes):
                            last = nc.tensor.matmul(ring[:, bank(at), column:column + NEXP], x[:, part, b * P:(b + 1) * P], g[:, :], start=k == 0, stop=k == 4)
                        if b % 2:
                            last.then_inc(ring_filled.sem, 1)

                def layer1(self, turn, i, slot, f, c):
                    w1_hi, w1_lo, w1_stack, _, _ = keep["ffn"][f]
                    x_hi, x_lo = xt["mlp" if f == 0 else "exp"]
                    slot_free(turn, slot)
                    cols = slice(c * P, (c + 1) * P)
                    passes = ((w1_hi, x_hi, 0), (w1_hi, x_lo, 0), (w1_lo, x_hi, 0), (w1_stack, x_hi, 1), (w1_stack, x_lo, 1))
                    for k, (w, x, part) in enumerate(passes):
                        last = nc.tensor.matmul(ring[:, bank(slot), :], w[:, cols], x[:, part, :], start=k == 0, stop=k == 4)
                    last.then_inc(ring_filled.sem, 1)

                def layer2(self, turn, i, out, f, c):
                    _, _, _, w2_hi, w2_lo = keep["ffn"][f]
                    pe.wait_ge(lo_ready.sem, lo_ready.at(turn, i))
                    for b in range(UNIT):
                        if c == 0:
                            pe.wait_ge(out_free.sem, out_free.at(turn, (out - 1) * UNIT + b))
                        for k, (h, w) in enumerate(((hid_hi, w2_hi), (hid_lo, w2_hi), (hid_hi, w2_lo))):
                            last = nc.tensor.matmul(ps_out[:, b, 0:D], h[:, i % 3, b * P:(b + 1) * P], w[:, c, :], start=c + k == 0, stop=c == HC - 1 and k == 2)
                    last.then_inc(hid_used.sem, 1)

            turns(pe, Do())

        @block.scalar
        def _(act):
            act.dma_start(b1[:, :], dram["b1"]).then_inc(consts_loaded, 16)
            act.dma_start(b2[:, :, :], dram["b2"].rearrange("a (f d) -> a f d", d=D).to_broadcast([P, FFNS, D])).then_inc(consts_loaded, 16)
            for to, of, n in ((gain, "ln2_g", D), (shift, "ln2_b", D), (b_gate, "b_gate", NEXP)):
                act.dma_start(to[:, :], dram[of].to_broadcast([P, n])).then_inc(consts_loaded, 16)
            for part, (to, of) in enumerate(((slice(0, P), slice(0, MAIN)), (slice(0, TAIL), slice(MAIN, D)), (slice(TAIL, P), slice(MAIN, D)))):
                act.dma_start(raw_gate[to, min(part, 1), :], dram["w_gate"][of, :]).then_inc(gate_loaded, 16)
            for signal in (ring_free, lo_ready, hid_used, out_free, out_stored):
                signal.lend(act)
            act.wait_ge(gate_loaded, 48)
            nc.scalar.activation(g_hi[:, :], raw_gate[:, 0, :], ACT.Copy)
            nc.scalar.activation(g_half[:, :], raw_gate[:, 1, :], ACT.Copy, scale=keep["low_rows"][:, 0:1]).then_inc(gate_hi, 1)
            act.wait_ge(consts_loaded, 16 * 5)

            class Do(Steps_of):
                def inputs(self, turn, slot, kind, event):
                    for part in range(2):
                        act.wait_ge(ring_filled.sem, ring_filled.at(turn, slot + part))
                        nc.scalar.activation(xt[("mlp", "exp")[kind]][0][:, part, :], ring[:, bank(slot + part), :], ACT.Copy).then_inc(inputs_hi.sem, 1)

                def layer1(self, turn, i, slot, f, c):
                    if i == HC - 2:
                        act.wait_ge(logits_ready.sem, logits_ready.at(turn, 0))
                        nc.scalar.activation(exps[:, :, :], logits[:, :, :], ACT.Exp).then_inc(gate_exps.sem, 1)
                    act.wait_ge(ring_filled.sem, ring_filled.at(turn, slot))
                    act.wait_ge(lo_ready.sem, lo_ready.at(turn, i - 2))
                    nc.scalar.activation(gelu[:, i % 2, :], ring[:, bank(slot), :], ACT.Gelu, bias=b1[:, f * HC + c:f * HC + c + 1]).then_inc(chunk_read.sem, 1)
                    act.wait_ge(chunk_read.sem, chunk_read.at(turn, i))
                    act.wait_ge(hid_used.sem, hid_used.at(turn, i - 3))
                    nc.scalar.activation(hid_hi[:, i % 3, :], gelu[:, i % 2, :], ACT.Copy).then_inc(hi_ready.sem, 1)

            turns(act, Do())

        @block.vector
        def _(dve):
            def weighed(b, e):
                return gates[:, b, e:e + 1]

            class Do(Steps_of):
                def inputs(self, turn, slot, kind, event):
                    hi, lo = xt[("mlp", "exp")[kind]]
                    for part in range(2):
                        dve.wait_ge(inputs_hi.sem, inputs_hi.at(turn, 2 * IN * event + IN * kind + part))
                        nc.vector.tensor_tensor(lo[:, part, :], ring[:, bank(slot + part), :], raw(hi[:, part, :]), ALU.subtract).then_inc(ring_free.sem, 1)

                def layer1(self, turn, i, slot, f, c):
                    dve.wait_ge(hi_ready.sem, hi_ready.at(turn, i))
                    dve.sem_inc(ring_free.sem, 1)
                    nc.vector.tensor_tensor(hid_lo[:, i % 3, :], gelu[:, i % 2, :], raw(hid_hi[:, i % 3, :]), ALU.subtract).then_inc(lo_ready.sem, 1)

                def begin(self, turn):
                    steps = Steps(dve, dve_gate, turn)
                    for part in range(GATE):
                        dve.wait_ge(ring_filled.sem, ring_filled.at(turn, part - GATE))
                        nc.vector.tensor_tensor(logits[:, 2 * part:2 * part + 2, :], ring[:, bank(part - GATE), 0:2 * NEXP].rearrange("p (b e) -> p b e", e=NEXP),
                                                b_gate[:, :].unsqueeze(1).to_broadcast([P, 2, NEXP]), ALU.add).then_inc(ring_free.sem, 1)
                    dve.wait_ge(ring_free.sem, ring_free.at(turn, -1))
                    steps.then(nc.vector.tensor_reduce(out=best[:, :], in_=logits[:, :, :], op=ALU.max, axis=X))
                    nc.vector.tensor_tensor(logits[:, :, :], logits[:, :, :], best[:, :].unsqueeze(2).to_broadcast([P, UNIT, NEXP]), ALU.subtract).then_inc(logits_ready.sem, 1)
                    dve.wait_ge(logits_ready.sem, logits_ready.at(turn, 0))
                    pairs = [P, UNIT, NEXP, NEXP]
                    other, own = logits[:, :, :].unsqueeze(2).to_broadcast(pairs), logits[:, :, :].unsqueeze(3).to_broadcast(pairs)
                    nc.vector.tensor_tensor(rank4[:, :, :, :], other, own, ALU.is_gt)
                    steps.then(nc.vector.tensor_tensor(ties[:, :, :, :], other, own, ALU.is_equal))
                    steps.then(nc.vector.tensor_tensor(ties[:, :, :, :], ties[:, :, :, :], earlier[:, :, :].unsqueeze(1).to_broadcast(pairs), ALU.mult))
                    steps.then(nc.vector.tensor_tensor(rank4[:, :, :, :], rank4[:, :, :, :], ties[:, :, :, :], ALU.add))
                    steps.then(nc.vector.tensor_reduce(out=rank[:, :, :], in_=rank4[:, :, :, :], op=ALU.add, axis=X))
                    steps.then(nc.vector.tensor_scalar(chosen[:, :, :], rank[:, :, :], 2.0, None, ALU.is_lt))
                    self.steps = steps

                def weigh(self, turn):
                    steps = self.steps
                    dve.wait_ge(gate_exps.sem, gate_exps.at(turn, 0))
                    steps.then(nc.vector.tensor_tensor(gates[:, :, :], exps[:, :, :], chosen[:, :, :], ALU.mult))
                    steps.then(nc.vector.tensor_reduce(out=best[:, :], in_=gates[:, :, :], op=ALU.add, axis=X))
                    steps.then(nc.vector.reciprocal(best[:, :], best[:, :]))
                    steps.then(nc.vector.tensor_tensor(gates[:, :, :], gates[:, :, :], best[:, :].unsqueeze(2).to_broadcast([P, UNIT, NEXP]), ALU.mult))
                    assert steps.count == GATE_STEPS

                def finish(self, turn, i, out, f):
                    if f == 0:
                        return self.finish_mlp(turn, i, out, -1 if out < 0 else 0)
                    e = f - 1
                    if e == 0:
                        self.weigh(turn)
                        dve.wait_ge(out_stored.sem, out_stored.at(turn, -1))
                    else:
                        dve.wait_ge(total_ready.sem, total_ready.at(turn, e - 1))
                    dve.wait_ge(hid_used.sem, hid_used.at(turn, i))
                    for b in range(UNIT):
                        nc.vector.scalar_tensor_tensor(out=total[:, b, :], in0=ps_out[:, b, 0:D], scalar=weighed(b, e), in1=(total if e else base)[:, b, :],
                                                       op0=ALU.mult, op1=ALU.add).then_inc(out_free.sem, 1)
                    dve.wait_ge(out_free.sem, out_free.at(turn, (out + 1) * UNIT - 1))
                    for b in range(UNIT):
                        last = nc.vector.scalar_tensor_tensor(out=total[:, b, :], in0=b2[:, f, :], scalar=weighed(b, e), in1=total[:, b, :],
                                                              op0=ALU.mult, op1=ALU.add)
                    last.then_inc(total_ready.sem, 1)

                def finish_mlp(self, turn, i, out, event):
                    steps = Steps(dve, dve_norm, turn, event * NORM, passed=keep["passed"])
                    wide = lambda row: row.unsqueeze(1).to_broadcast([P, UNIT, D])
                    dve.wait_ge(hid_used.sem, hid_used.at(turn, i))
                    for b in range(UNIT):
                        nc.vector.tensor_tensor(x3[:, b, :], ps_out[:, b, 0:D], x2[:, b, 0:D], ALU.add).then_inc(out_free.sem, 1)
                    dve.wait_ge(out_free.sem, out_free.at(turn, (out + 1) * UNIT - 1))
                    steps.then(nc.vector.tensor_tensor(x3[:, :, :], x3[:, :, :], wide(b2[:, 0, :]), ALU.add))
                    moments_of(nc, steps, stats, moments, [x3[:, b, :] for b in range(UNIT)])
                    inverse_root(nc, steps, moments[:, :, 1], 1e-5, half[:, :], guess[:, :], rstd[:, :], work[:, :])
                    for b in range(UNIT):
                        last = nc.vector.tensor_scalar(xn[:, b, 0:D], x3[:, b, :], moments[:, b, 0:1], rstd[:, b:b + 1], ALU.subtract, ALU.mult)
                    steps.then(last)
                    steps.then(nc.vector.tensor_tensor(xn[:, :, 0:D], xn[:, :, 0:D], wide(gain[:, :]), ALU.mult))
                    steps.then(nc.vector.tensor_tensor(xn[:, :, 0:D], xn[:, :, 0:D], wide(shift[:, :]), ALU.add))
                    nc.vector.tensor_copy(xn[:, :, D:D + TAIL], xn[:, :, MAIN:D]).then_inc(xn_ready.sem, 1)
                    steps.then(nc.vector.tensor_tensor(base[:, :, :], x3[:, :, :], h1[:, :, :], ALU.add))
                    dve.sem_inc(mlp_done.sem, 1)
                    assert steps.count == (event + 1) * NORM

            dve.wait_ge(gate_hi, 1)
            nc.vector.tensor_tensor(g_lo[:, :], raw_gate[:, 0, :], raw(g_hi[:, :]), ALU.subtract)
            nc.vector.tensor_tensor(g_stack[:, :], raw_gate[:, 1, :], raw(g_half[:, :]), ALU.subtract).then_inc(gate_ready, 1)
            dve.wait_ge(ones_ready, 2)
            dve.wait_ge(consts_loaded, 16 * 5)
            turns(dve, Do())


def tower(nc, given, out, scratch):
    dram = {**given, **scratch, "out": out}
    with ExitStack() as ctx:
        sb = lambda name, shape, dt=F32: ctx.enter_context(nc.sbuf_tensor(name, shape, dt))
        keep = {"ident": sb("ident", [P, P]), "low_rows": sb("low_rows", [P, 1]), "passed": ctx.enter_context(nc.semaphore("passed"))}
        with ExitStack() as weights:
            wb = lambda name: weights.enter_context(nc.sbuf_tensor(name, [P, QKV], F32R))
            keep["w_qkv"] = [(wb(f"w_{x}_hi")[:, :], wb(f"w_{x}_lo")[:, :], wb(f"w_{x}_stack")[:, :], None) for x in "qkv"]
            keep["w_proj"] = tuple(wb(f"w_proj_{x}")[:, :] for x in ("hi", "lo", "twin_hi", "twin_lo"))
            embed(nc, keep, dram)
            attention(nc, keep, dram)
        ffn = lambda name, shape: sb(f"ffn_weights_{name}", shape, F32R)
        keep["ffn"] = [(ffn(f"w1_hi{f}", [P, HID]), ffn(f"w1_lo{f}", [P, HID]), ffn(f"w1_stack{f}", [P, HID]),
                        ffn(f"w2_hi{f}", [P, HC, D]), ffn(f"w2_lo{f}", [P, HC, D])) for f in range(FFNS)]
        mixer(nc, keep, dram)
        experts(nc, keep, dram)


def host_layout(inputs):
    a = {k: np.asarray(v) for k, v in inputs.items()}
    ids = np.stack([a["x"].T, a["mask_BS_i1_0"].T], axis=1).reshape(P, 2 * TILES)
    chunk = np.arange(QKV).reshape(CHUNKS, D)
    order = np.concatenate([chunk[:, :MAIN].ravel(), chunk[:, MAIN:].ravel()])
    w, b = a["L0_attn_W_qkv"], a["L0_attn_b_qkv"]
    w_qkv = np.concatenate([w[:, order], w[:, QKV + order], w[:, 2 * QKV:]], axis=1)
    b_qk = np.concatenate([b[order], b[QKV + order]]).reshape(2 * QKV // P, P).T
    w_proj = a["L0_attn_W_proj"].reshape(CHUNKS, D, D)
    heads = lambda x: x.reshape(*x.shape[:-1], 2 * HEADS, HD)
    twice = lambda x: np.stack([x, x], axis=-2).reshape(*x.shape[:-2], -1)
    w_in = a["L0_ffn_in_w"].T
    w_mix = np.concatenate([twice(heads(w_in[:, :2 * D])), w_in[:, 2 * D:], a["L0_ffn_out_w"].T], axis=1)
    given = {
        "ids": ids, "token_emb": a["L0_tok_token_emb"], "type_emb": a["L0_tok_type_emb"], "pos_emb": a["L0_tok_pos_emb"],
        "gamma": a["L0_tok_gamma"][None], "beta": a["L0_tok_beta"][None],
        "w_qkv": w_qkv, "b_qk": b_qk, "b_v": b[None, 2 * QKV:],
        "w_proj_main": w_proj[:, :MAIN].transpose(1, 0, 2).reshape(MAIN, QKV),
        "w_proj_tail": w_proj[:, MAIN:].transpose(1, 0, 2).reshape(TAIL, QKV),
        "b_proj": a["L0_attn_b_proj"][None],
        "w_mix": w_mix, "b_mix_qk": twice(heads(a["L0_ffn_in_b"][:2 * D])).reshape(-1, P).T,
        "b_mix_v": a["L0_ffn_in_b"][None, 2 * D:], "b_mix_out": a["L0_ffn_out_b"][None],
        "ln1_g": a["L0_ffn_ln1_g"][None], "ln1_b": a["L0_ffn_ln1_b"][None],
        "ln2_g": a["L0_ffn_ln2_g"][None], "ln2_b": a["L0_ffn_ln2_b"][None],
        "w1": np.concatenate([a["L0_ffn_mlp_w1"][None], a["L0_ffn_exp_w1"]]),
        "w2": np.concatenate([a["L0_ffn_mlp_w2"][None], a["L0_ffn_exp_w2"]]),
        "b1": np.concatenate([a["L0_ffn_mlp_b1"][None], a["L0_ffn_exp_b1"]]).reshape(FFNS * HC, P).T,
        "b2": np.concatenate([a["L0_ffn_mlp_b2"][None], a["L0_ffn_exp_b2"]]).reshape(1, FFNS * D),
        "w_gate": a["L0_ffn_gate_w"].T, "b_gate": a["L0_ffn_gate_b"][None],
    }
    return {k: np.ascontiguousarray(v) for k, v in given.items()}


def kernel(**inputs):
    import concourse.bacc as bacc
    from concourse.bass_utils import run_bass_kernel_spmd

    nc = bacc.Bacc("TRN2", target_bir_lowering=False, num_devices=1)
    given = host_layout(inputs)
    aps = {k: nc.dram_tensor(f"in_{k}", v.shape, mybir.dt.from_np(v.dtype), kind="ExternalInput").ap() for k, v in given.items()}
    out = nc.dram_tensor("out", (TOKENS, D), F32, kind="ExternalOutput").ap()
    internal = lambda name, shape: nc.dram_tensor(name, shape, F32, kind="Internal").ap()
    scratch = {k: internal(f"{k}_rows", (TOKENS, D)) for k in ("h0", "h1", "y", "x2")}
    scratch["v"] = [internal(f"v_rows{i}", (P, QKV)) for i in range(2)]
    tower(nc, aps, out, scratch)
    ran = run_bass_kernel_spmd(nc, [{f"in_{k}": v for k, v in given.items()}], core_ids=[0])
    return ran.results[0]["out"].reshape(BATCH, SEQ, D)
```

```python
import numpy as np
from contextlib import ExitStack

import concourse.bass as bass
from concourse import mybir
from concourse.alu_op_type import AluOpType as ALU


F32 = mybir.dt.float32
F32R = mybir.dt.float32r
I32 = mybir.dt.int32
U32 = mybir.dt.uint32
ACT = mybir.ActivationFunctionType
X = mybir.AxisListType.X

P = 128
BATCH, SEQ = 16, 128
TOKENS = BATCH * SEQ
TILES = TOKENS // P
D = 192
MAIN, TAIL = P, D - P
CHUNKS = 8
QKV = CHUNKS * D
GROUP = P // CHUNKS
GROUPS = P // GROUP
QUAD = 4
HEADS, HD = 12, 16
HID = 768
HC = HID // P
NEXP = 4
FFNS = 1 + NEXP


class Signal:

    def __init__(self, sem, per_turn, before=0, lent=0, step=1):
        self.sem, self.per_turn, self.before, self.lent, self.step = sem, per_turn, before + lent, lent, step

    def lend(self, engine):
        engine.sem_inc(self.sem, self.lent * self.step)

    def at(self, turn, event):
        if isinstance(turn, int) and isinstance(event, int):
            value = (self.before + turn * self.per_turn + event + 1) * self.step
            assert value > 0
            return value
        return turn * (self.per_turn * self.step) + (self.before + event + 1) * self.step



class Steps:

    def __init__(self, engine, signal, turn, first=0, passed=None):
        self.engine, self.mark, self.turn, self.count, self.passed = engine, signal, turn, first, passed

    def then(self, instruction, settle=True):
        instruction.then_inc(self.mark.sem, 1)
        self.count += 1
        if settle:
            self.settle()

    def settle(self):
        self.engine.wait_ge(self.mark.sem, self.mark.at(self.turn, self.count - 1))


def apart(engine, passed):
    engine.sem_inc(passed, 1)


def raw(hi):
    return hi.bitcast(F32)


def plan_of(steps, slots_of, his_of, sources, more, first=(0, 0)):
    found, (slot, hi), filled = [], first, {}
    for word in steps.split():
        kind, i = word.strip("+0123456789"), int("".join(c for c in word if c.isdigit()))
        if more or word[0] != "+":
            of = sources.get(kind)
            found.append((kind, i, slot, hi, filled.get((of, i), filled.get((of, 0)))))
            slot += slots_of.get(kind, 0)
            hi += his_of.get(kind, 0)
            filled[kind, i] = slot - 1
    return found, slot, hi


def walk(turn, steps, do):
    for kind, *place in steps:
        if kind in do:
            do[kind](turn, *place)


def event_of(slot):
    return -1 if slot < 0 else 0


def inverse_root(nc, steps, part, variance, eps, half, guess, rstd, work):
    MAGIC = 0x5F3759DF
    if part == 0:
        steps.then(nc.vector.tensor_scalar(work, variance, eps, 1.0, ALU.add, ALU.mult))
        nc.vector.tensor_scalar(half, work, -0.5, 1.0, ALU.mult, ALU.mult)
        steps.then(nc.vector.tensor_scalar(guess.bitcast(I32), work.bitcast(I32), 1, None, ALU.arith_shift_right))
        steps.then(nc.vector.tensor_scalar(rstd.bitcast(I32), guess.bitcast(I32), -1.0, float(MAGIC), ALU.mult, ALU.add))
    else:
        steps.then(nc.vector.tensor_tensor(work, rstd, rstd, ALU.mult))
        steps.then(nc.vector.tensor_tensor(work, work, half, ALU.mult))
        steps.then(nc.vector.scalar_tensor_tensor(out=rstd, in0=work, scalar=1.5, in1=rstd, op0=ALU.add, op1=ALU.mult))


ROOT_PARTS = 4
ROOT_STEPS = 3 * ROOT_PARTS


def moments_of(nc, steps, stats, moments, tiles):
    for i, tile in enumerate(tiles):
        last = nc.vector.bn_stats(stats[:, i, :], tile)
    steps.then(last)
    apart(steps.engine, steps.passed)
    for i in range(len(tiles)):
        last = nc.vector.bn_aggr(moments[:, i, :], stats[:, i, :])
    steps.then(last)


NORM_STEPS = 2 + ROOT_STEPS


def embed(nc, keep, dram):
    TAKE = 4
    TAKES = TILES // TAKE
    with ExitStack() as ctx:
        sb = lambda name, shape, dt=F32: ctx.enter_context(nc.sbuf_tensor(f"embed_{name}", shape, dt))
        sem = lambda name: ctx.enter_context(nc.semaphore(f"embed_{name}"))
        ids = sb("ids", [P, 2, TILES], I32)
        emb = sb("emb", [P, TILES, D])
        typ = sb("typ", [P, TILES, D])
        pos = sb("pos", [P, D])
        gamma = sb("gamma", [P, D])
        beta = sb("beta", [P, D])
        stats = sb("stats", [P, TAKE, 6])
        moments = sb("moments", [P, TAKE, 2])
        half, guess, rstd, work = (sb(n, [P, TAKE]) for n in ("half", "guess", "rstd", "work"))
        stage = [(sb(f"stage_main{i}", [P, QKV]), sb(f"stage_tail{i}", [P, QKV])) for i in range(4)]
        low_half = sb("low_half", [P, QKV], F32R)

        ids_loaded, rows_loaded, pos_loaded = sem("ids_loaded"), sem("rows_loaded"), sem("pos_loaded")
        token_rows = [sem(f"token_rows{i}") for i in range(TAKES)]
        type_rows = [sem(f"type_rows{i}") for i in range(TAKES)]
        weights_loaded = [sem(f"weights_loaded{i}") for i in range(4)]
        const_ready = sem("const_ready")
        h0_ready, h0_stored = sem("h0_ready"), sem("h0_stored")
        hi_ready, half_ready, half_used = sem("w_hi_ready"), sem("w_half_ready"), sem("w_half_used")
        dve_step = Signal(sem("dve_step"), 0)
        block = ctx.enter_context(nc.Block())
        targets = keep["w_qkv"] + [keep["w_proj"]]

        @block.sync
        def _(sp):
            sp.dma_start(ids[:, :, :], dram["ids"].rearrange("p (a b) -> p a b", a=2)).then_inc(ids_loaded, 16)
            for i in range(4):
                main, tail = stage[i]
                cut = dram["w_qkv"][:, i * QKV:(i + 1) * QKV] if i < 3 else None
                src_main = cut[0:MAIN, :] if i < 3 else dram["w_proj_main"]
                src_tail = cut[MAIN:D, :] if i < 3 else dram["w_proj_tail"]
                sp.dma_start(main[:, :], src_main).then_inc(weights_loaded[i], 16)
                for half in range(2):
                    sp.dma_start(tail[half * TAIL:(half + 1) * TAIL, :], src_tail).then_inc(weights_loaded[i], 16)
            for t in range(TAKES):
                sp.wait_ge(h0_ready, t + 1)
                sp.dma_start(dram["h0"].rearrange("(b p) d -> p b d", p=P)[:, t * TAKE:(t + 1) * TAKE, :],
                             emb[:, t * TAKE:(t + 1) * TAKE, :]).then_inc(h0_stored, 16)
            sp.wait_ge(h0_stored, 16 * TAKES)

        @block.gpsimd
        def _(pool):
            pool.wait_ge(ids_loaded, 16)
            for t in range(TAKES):
                for i in range(t * TAKE, (t + 1) * TAKE):
                    nc.gpsimd.indirect_dma_start(emb[:, i, :], None, dram["token_emb"],
                                                 bass.IndirectOffsetOnAxis(ap=ids[:, 0, i:i + 1], axis=0)).then_inc(token_rows[t], 16)
                    nc.gpsimd.indirect_dma_start(typ[:, i, :], None, dram["type_emb"],
                                                 bass.IndirectOffsetOnAxis(ap=ids[:, 1, i:i + 1], axis=0)).then_inc(type_rows[t], 16)
            nc.gpsimd.memset(keep["ident"][:, :], 0.0).then_inc(const_ready, 1)
            pool.wait_ge(const_ready, 1)
            nc.gpsimd.affine_select(out=keep["ident"][:, :], in_=keep["ident"][:, :], compare_op=ALU.not_equal,
                                    fill=1.0, base=0, pattern=[[-1, P]], channel_multiplier=1).then_inc(const_ready, 1)

        @block.scalar
        def _(act):
            act.dma_start(pos[:, :], dram["pos_emb"]).then_inc(pos_loaded, 16)
            act.dma_start(gamma[:, :], dram["gamma"].to_broadcast([P, D])).then_inc(rows_loaded, 16)
            act.dma_start(beta[:, :], dram["beta"].to_broadcast([P, D])).then_inc(rows_loaded, 16)
            for i in range(4):
                main, tail = stage[i]
                main_hi, main_lo, tail_a, tail_b = targets[i]
                act.wait_ge(weights_loaded[i], 48)
                nc.scalar.activation(main_hi, main[:, :], ACT.Copy).then_inc(hi_ready, 1)
                if i < 3:
                    if i == 0:
                        act.wait_ge(dve_step.sem, 2)
                    else:
                        act.wait_ge(half_used, i)
                    nc.scalar.activation(low_half[:, :], tail[:, :], ACT.Copy,
                                         scale=keep["low_rows"][:, 0:1]).then_inc(half_ready, 1)
                else:
                    nc.scalar.activation(tail_a, tail[:, :], ACT.Copy).then_inc(half_ready, 1)

        @block.vector
        def _(dve):
            steps = Steps(dve, dve_step, 0, passed=keep["passed"])
            steps.then(nc.vector.memset(keep["low_rows"][0:TAIL, :], 0.0))
            steps.then(nc.vector.memset(keep["low_rows"][TAIL:P, :], 1.0))

            def tokens(t):
                take = slice(t * TAKE, (t + 1) * TAKE)
                dve.wait_ge(token_rows[t], 16 * TAKE)
                dve.wait_ge(type_rows[t], 16 * TAKE)
                steps.then(nc.vector.tensor_tensor(emb[:, take, :], emb[:, take, :], typ[:, take, :], ALU.add))
                if t == 0:
                    dve.wait_ge(pos_loaded, 16)
                    dve.wait_ge(rows_loaded, 32)
                wide = lambda row: row[:, :].unsqueeze(1).to_broadcast([P, TAKE, D])
                steps.then(nc.vector.tensor_tensor(emb[:, take, :], emb[:, take, :], wide(pos), ALU.add))
                moments_of(nc, steps, stats, moments, [emb[:, i, :] for i in range(t * TAKE, (t + 1) * TAKE)])
                for part in range(ROOT_PARTS):
                    inverse_root(nc, steps, part, moments[:, :, 1], 1e-12, half[:, :], guess[:, :], rstd[:, :], work[:, :])
                for i in range(TAKE):
                    last = nc.vector.tensor_scalar(emb[:, t * TAKE + i, :], emb[:, t * TAKE + i, :], moments[:, i, 0:1],
                                                   rstd[:, i:i + 1], ALU.subtract, ALU.mult)
                steps.then(last)
                steps.then(nc.vector.tensor_tensor(emb[:, take, :], emb[:, take, :], wide(gamma), ALU.mult))
                nc.vector.tensor_tensor(emb[:, take, :], emb[:, take, :], wide(beta), ALU.add).then_inc(h0_ready, 1)

            def weights(i):
                main, tail = stage[i]
                main_hi, main_lo, tail_a, tail_b = targets[i]
                dve.wait_ge(hi_ready, i + 1)
                nc.vector.tensor_tensor(main_lo, main[:, :], raw(main_hi), ALU.subtract)
                dve.wait_ge(half_ready, i + 1)
                if i < 3:
                    nc.vector.tensor_tensor(tail_a, tail[:, :], raw(low_half[:, :]), ALU.subtract).then_inc(half_used, 1)
                else:
                    nc.vector.tensor_tensor(tail_b, tail[:, :], raw(tail_a), ALU.subtract)

            for t in range(4):
                tokens(t)
                weights(t)


def attention(nc, keep, dram):
    UNIT = 2
    UNITS = TILES // UNIT
    UT = UNIT * P
    UG = UNIT * GROUPS
    QUADS = UG // QUAD
    RING = 4
    VCUT = 512
    VCUTS = QKV // VCUT
    PAIRS = CHUNKS // 2
    with ExitStack() as ctx:
        sb = lambda name, shape, dt=F32: ctx.enter_context(nc.sbuf_tensor(f"attn_{name}", shape, dt))
        ps = lambda name, shape: ctx.enter_context(nc.psum_tensor(name, shape, F32))
        sem = lambda name: ctx.enter_context(nc.semaphore(f"attn_{name}"))
        w_q, w_k, w_v = keep["w_qkv"]
        wp_hi, wp_lo, wp_twin_hi, wp_twin_lo = (w.rearrange("p (c n) -> p c n", c=CHUNKS) for w in keep["w_proj"])
        b_qk = sb("b_qk", [P, 2 * QKV // P])
        b_v = sb("b_v", [P, QKV])
        b_proj = sb("b_proj", [P, D])
        xin = sb("xin", [P, UNIT, D])
        xn = sb("xn", [P, UNIT, MAIN + 2 * TAIL])
        xt_hi, xt_lo, xt_twin_hi, xt_twin_lo = (sb(n, [P, UT], F32R) for n in ("xt_hi", "xt_lo", "xt_twin_hi", "xt_twin_lo"))
        q_hi, q_lo, q_stack, k_hi, k_lo, k_twin_hi, k_twin_lo = (
            sb(n, [P, UG, P], F32R) for n in ("q_hi", "q_lo", "q_stack", "k_hi", "k_lo", "k_twin_hi", "k_twin_lo"))
        probs = sb("probs", [P, QUADS, QUAD, P])
        pt_hi = sb("pt_hi", [P, 2, QUAD, P], F32R)
        pt_lo = sb("pt_lo", [P, 2, QUAD, P], F32R)
        v_flat = sb("v_flat", [P, QKV])
        v_rows = sb("v_rows", [P, GROUPS, D])
        v_hi = sb("v_hi", [P, GROUPS, D], F32R)
        v_lo = sb("v_lo", [P, GROUPS, D], F32R)
        o_hi, o_lo, o_stack = (sb(n, [P, CHUNKS, P], F32R) for n in ("o_hi", "o_lo", "o_stack"))
        residual = sb("residual", [P, UNIT, D])
        h1 = sb("h1", [P, UNIT, D])
        neg_max = sb("neg_max", [P, QUADS, QUAD])
        sums = sb("sums", [P, QUADS, QUAD])
        inverse = sb("inverse", [P, QUADS, QUAD])
        stats = sb("stats", [P, UNIT, 6])
        moments = sb("moments", [P, UNIT, 2])
        half, guess, rstd, work = (sb(n, [P, UNIT]) for n in ("half", "guess", "rstd", "work"))
        ring = ps("ring", [P, RING, 512])
        ps_scores = ps("ps_scores", [P, 2, QUAD, P])
        ps_mixed = ps("ps_mixed", [P, QUAD, P])
        ps_mixed_tail = ps("ps_mixed_tail", [P, QUAD, P])

        QK_SLOTS = 2 * QKV // P
        OUTS = 4
        SLOTS_OF = {"V": 1, "T": 1, "X": 2, "Q": 1}
        HIS_OF = {"T": 1, "X": 2, "Q": 1}
        WAY_IN = "N0 N1 N2 N3 N4 N5 X0 V0 V1 V2 " + " ".join(f"Q{i}" for i in range(QK_SLOTS)).replace("Q11", "Q11 Z11")
        TURN = """B0 S0 +N0 +N1 S1 +N2 I0 +N3 V3 I1 +N4 V4 +N5 S2 V5 +X0 S3 I2 I3
                  T0 +Q0 +Q1 T1 +Q2 M0 R0 +Q3 +Q4 +Q5 +Q6 M1 R1 B1 +Q7 +Q8 +Q9 T2 +Q10 +Q11 +Z11 O0 +Q12 O1 +Q13 O2 T3 +V0 O3
                  M2 R2 F0 +V1 +Q14 +Q15 M3 R3 +V2 +Q16 +Q17 +Q18 O4 +Q19 +Q20 O5 +Q21 +Q22 +Q23 O6 O7 F1"""
        plan = lambda steps, more=True, first=(0, 0): plan_of(steps, SLOTS_OF, HIS_OF, {"M": "T", "V": "X", "Q": "X", "Z": "Q"}, more, first)
        SLOTS_BEFORE = 2 + QK_SLOTS + VCUTS
        HIS_BEFORE = 2 + QK_SLOTS
        _, SLOTS, HIS = plan(TURN)
        assert SLOTS % RING == 0
        bank = lambda slot: (slot + SLOTS_BEFORE) % RING
        ring_filled = Signal(sem("ring_filled"), SLOTS, SLOTS_BEFORE)
        ring_hi = Signal(sem("ring_hi"), HIS, HIS_BEFORE)
        ring_free = Signal(sem("ring_free"), SLOTS, SLOTS_BEFORE, lent=RING)
        x_loaded = Signal(sem("x_loaded"), 1, 1, step=16)
        xn_ready = Signal(sem("xn_ready"), 1, 1)
        TWIN_STEPS = 4
        twin_step = Signal(sem("k_twin_step"), TWIN_STEPS, TWIN_STEPS)
        scored = Signal(sem("scored"), QUADS)
        max_ready = Signal(sem("max_ready"), QUADS)
        exps_ready = Signal(sem("exps_ready"), QUADS, lent=2)
        inverse_ready = Signal(sem("inverse_ready"), QUADS)
        probs_ready = Signal(sem("probs_ready"), QUADS)
        mixed = Signal(sem("mixed"), QUADS, lent=2)
        mixed_hi = Signal(sem("mixed_hi"), QUADS)
        mixed_lo = Signal(sem("mixed_lo"), QUADS, lent=1)
        out_filled = Signal(sem("out_filled"), UNIT, lent=1)
        out_read = Signal(sem("out_read"), UNIT, lent=UNIT)
        v_sent = Signal(sem("v_sent"), UNIT, 1, lent=1, step=16)
        v_rows_loaded = Signal(sem("v_rows_loaded"), UNIT, 1, step=16 * CHUNKS)
        v_hi_ready = Signal(sem("v_hi_ready"), UNIT)
        v_ready = Signal(sem("v_ready"), UNIT)
        residual_loaded = Signal(sem("residual_loaded"), 1, step=16)
        residual_biased = Signal(sem("residual_biased"), 1)
        h1_stored = [Signal(sem(f"h1_stored{b}"), 1, lent=1, step=16) for b in range(UNIT)]
        biases_loaded = sem("biases_loaded")
        dve_step = Signal(sem("dve_step"), NORM_STEPS, NORM_STEPS)
        block = ctx.enter_context(nc.Block())

        rows = lambda turn: bass.ds(turn * UT, UT)
        last_v = lambda i, more: [slot for kind, n, slot, _, _ in plan(TURN, more)[0] if (kind, n) == ("V", i)][0]

        def turns(engine, do, ahead=None):
            walk(0, plan(WAY_IN, first=(-SLOTS_BEFORE, -HIS_BEFORE))[0], do)
            with engine.Fori(0, UNITS - 1) as turn:
                if ahead:
                    ahead(turn)
                walk(turn, plan(TURN)[0], do)
            walk(UNITS - 1, plan(TURN, False)[0], do)

        @block.sync
        def _(sp):
            def move_v(turn, event, slot):
                there = dram["v"][event % 2]
                sp.wait_ge(ring_free.sem, ring_free.at(turn, slot))
                sp.dma_start(there, v_flat[:, :]).then_inc(v_sent.sem, 16)
                sp.wait_ge(v_sent.sem, v_sent.at(turn, event))
                apart(sp, keep["passed"])
                if event >= 0:
                    sp.wait_ge(v_ready.sem, v_ready.at(turn, event))
                back = there.rearrange("(g t) (c d) -> c t g d", t=GROUP, c=CHUNKS)
                for c in range(CHUNKS):
                    sp.dma_start(v_rows[c * GROUP:(c + 1) * GROUP, :, :], back[c]).then_inc(v_rows_loaded.sem, 16)

            def store(turn, b):
                sp.wait_ge(out_read.sem, out_read.at(turn, b))
                sp.dma_start(dram["h1"][bass.ds(turn * UT + b * P, P), :], h1[:, b, :]).then_inc(h1_stored[b].sem, 16)

            def body(turn, more):
                sp.wait_ge(out_read.sem, out_read.at(turn, -1))
                sp.dma_start(residual[:, :, :], dram["h0"][rows(turn), :].rearrange("(b p) d -> p b d", p=P)).then_inc(residual_loaded.sem, 16)
                move_v(turn, 0, last_v(2 * VCUTS - 1, more))
                store(turn, 0)
                if more:
                    move_v(turn, 1, last_v(VCUTS - 1, more))
                store(turn, 1)

            move_v(0, -1, -1 - QK_SLOTS)
            with sp.Fori(0, UNITS - 1) as turn:
                body(turn, True)
            body(UNITS - 1, False)
            for b in range(UNIT):
                sp.wait_ge(h1_stored[b].sem, h1_stored[b].at(UNITS - 1, 0))

        @block.gpsimd
        def _(pool):
            def twins(turn, _, slot, hi, source):
                steps = Steps(pool, twin_step, turn, event_of(slot) * TWIN_STEPS)
                if event_of(slot) == 0:
                    pool.wait_ge(v_ready.sem, v_ready.at(turn, UNIT - 1))
                pool.wait_ge(ring_free.sem, ring_free.at(turn, source))
                apart(pool, keep["passed"])
                for k_twin in (k_twin_hi, k_twin_lo):
                    for odd in range(2):
                        chunks = lambda half: k_twin[half * TAIL:(half + 1) * TAIL, :, :].rearrange(
                            "p g (c o t) -> p g c o t", o=2, t=GROUP)[:, :, :, odd, :]
                        if steps.count % TWIN_STEPS:
                            steps.settle()
                            apart(pool, keep["passed"])
                        steps.then(nc.gpsimd.tensor_scalar(chunks(1 - odd), raw(chunks(odd)), 1.0, 1.0, ALU.mult, ALU.mult), settle=False)

            def normalise(turn, n, slot, hi, source):
                pool.wait_ge(inverse_ready.sem, inverse_ready.at(turn, n))
                apart(pool, keep["passed"])
                for j in range(QUAD):
                    last = nc.gpsimd.tensor_scalar(probs[:, n, j, :], probs[:, n, j, :], inverse[:, n, j:j + 1],
                                                   float(D) ** -0.5, ALU.mult, ALU.mult)
                last.then_inc(probs_ready.sem, 1)

            def split_v(turn, b, slot, hi, source):
                if b == 0:
                    pool.wait_ge(twin_step.sem, twin_step.at(turn, -1))
                pool.wait_ge(v_rows_loaded.sem, v_rows_loaded.at(turn, b - 1))
                pool.wait_ge(mixed.sem, mixed.at(turn, b * (QUADS // UNIT) - 1))
                apart(pool, keep["passed"])
                nc.gpsimd.tensor_scalar(v_hi[:, :, :], v_rows[:, :, :], 1.0, 1.0, ALU.mult, ALU.mult).then_inc(v_hi_ready.sem, 1)
                pool.wait_ge(v_hi_ready.sem, v_hi_ready.at(turn, b))
                nc.gpsimd.tensor_tensor(v_lo[:, :, :], v_rows[:, :, :], raw(v_hi[:, :, :]), ALU.subtract).then_inc(v_ready.sem, 1)

            turns(pool, {"B": split_v, "I": normalise, "Z": twins})

        out_of = lambda b: ps_scores[:, b, :, :].rearrange("p j k -> p (j k)")[:, 0:D]

        @block.tensor
        def _(pe):
            def slot_free(turn, slot):
                pe.wait_ge(ring_free.sem, ring_free.at(turn, slot - RING))

            def transposes(turn, _, slot, hi, source):
                pe.wait_ge(xn_ready.sem, xn_ready.at(turn, event_of(slot)))
                for part in range(2):
                    slot_free(turn, slot + part)
                    for b in range(UNIT):
                        last = nc.tensor.transpose(ring[:, bank(slot + part), b * P:(b + 1) * P], xn[:, b, part * P:(part + 1) * P], keep["ident"][:, :])
                    last.then_inc(ring_filled.sem, 1)

            def project_qk(turn, i, slot, hi, source):
                is_k, s = i < QK_SLOTS // 2, i % (QK_SLOTS // 2)
                w_hi, w_lo, w_stack, _ = w_k if is_k else w_q
                cols = slice(s * P, (s + 1) * P)
                if i == 0:
                    pe.wait_ge(ring_free.sem, ring_free.at(turn, source))
                slot_free(turn, slot)
                passes = ((w_hi, xt_hi), (w_hi, xt_lo), (w_lo, xt_hi), (w_stack, xt_twin_hi), (w_stack, xt_twin_lo))
                for k, (w, x) in enumerate(passes):
                    last = nc.tensor.matmul(ring[:, bank(slot), 0:UT], w[:, cols], x[:, :], start=k == 0, stop=k == 4)
                last.then_inc(ring_filled.sem, 1)

            def project_v(turn, i, slot, hi, source):
                w_hi, w_lo, w_stack, _ = w_v
                b, s = divmod(i, VCUTS)
                tile, cols = slice(b * P, (b + 1) * P), slice(s * VCUT, (s + 1) * VCUT)
                if i == 0:
                    pe.wait_ge(ring_free.sem, ring_free.at(turn, source))
                slot_free(turn, slot)
                passes = ((xt_hi, w_hi), (xt_lo, w_hi), (xt_hi, w_lo), (xt_twin_hi, w_stack), (xt_twin_lo, w_stack))
                for k, (x, w) in enumerate(passes):
                    last = nc.tensor.matmul(ring[:, bank(slot), :], x[:, tile], w[:, cols], start=k == 0, stop=k == 4)
                last.then_inc(ring_filled.sem, 1)

            def scores(turn, n, slot, hi, source):
                if n == 0:
                    pe.wait_ge(twin_step.sem, twin_step.at(turn, -1))
                    pe.wait_ge(ring_free.sem, ring_free.at(turn, -1))
                if n < UNIT:
                    pe.wait_ge(out_read.sem, out_read.at(turn, n - UNIT))
                pe.wait_ge(exps_ready.sem, exps_ready.at(turn, n - 2))
                for j in range(QUAD):
                    g = n * QUAD + j
                    passes = ((q_hi, k_hi), (q_lo, k_hi), (q_hi, k_lo), (q_stack, k_twin_hi), (q_stack, k_twin_lo))
                    for i, (q, k) in enumerate(passes):
                        last = nc.tensor.matmul(ps_scores[:, n % 2, j, :], q[:, g, :], k[:, g, :], start=i == 0, stop=i == 4)
                last.then_inc(scored.sem, 1)

            def turn_probs(turn, n, slot, hi, source):
                pe.wait_ge(probs_ready.sem, probs_ready.at(turn, n))
                slot_free(turn, slot)
                for j in range(QUAD):
                    last = nc.tensor.transpose(ring[:, bank(slot), j * P:(j + 1) * P], probs[:, n, j, :], keep["ident"][:, :])
                last.then_inc(ring_filled.sem, 1)

            def mix(turn, n, slot, hi, source):
                b = n // (QUADS // UNIT)
                pe.wait_ge(v_ready.sem, v_ready.at(turn, b))
                pe.wait_ge(ring_free.sem, ring_free.at(turn, source))
                pe.wait_ge(mixed_lo.sem, mixed_lo.at(turn, n - 1))
                for cols, out in ((slice(0, MAIN), ps_mixed), (slice(MAIN, D), ps_mixed_tail)):
                    for j in range(QUAD):
                        g = n * QUAD + j - b * GROUPS
                        passes = ((v_hi, pt_hi), (v_lo, pt_hi), (v_hi, pt_lo))
                        for i, (v, p) in enumerate(passes):
                            last = nc.tensor.matmul(out[0:cols.stop - cols.start, j, :], v[:, g, cols], p[:, n % 2, j, :], start=i == 0, stop=i == 2)
                last.then_inc(mixed.sem, 1)

            def project_out(turn, i, slot, hi, source):
                b, part = divmod(i, OUTS)
                if part == 0:
                    pe.wait_ge(mixed_lo.sem, mixed_lo.at(turn, (b + 1) * (QUADS // UNIT) - 1))
                    pe.wait_ge(exps_ready.sem, exps_ready.at(turn, QUADS - UNIT + b))
                passes = ((o_hi, wp_hi), (o_lo, wp_hi), (o_hi, wp_lo), (o_stack, wp_twin_hi), (o_stack, wp_twin_lo))
                for c in range(part * CHUNKS // OUTS, (part + 1) * CHUNKS // OUTS):
                    for k, (o, w) in enumerate(passes):
                        last = nc.tensor.matmul(out_of(b), o[:, c, :], w[:, c, :], start=c + k == 0, stop=c == CHUNKS - 1 and k == 4)
                if part == OUTS - 1:
                    last.then_inc(out_filled.sem, 1)

            turns(pe, {"S": scores, "V": project_v, "X": transposes, "T": turn_probs, "Q": project_qk, "M": mix, "O": project_out})

        def qk_place(i):
            is_k, s = i < QK_SLOTS // 2, i % (QK_SLOTS // 2)
            bias = b_qk[:, s + is_k * QK_SLOTS // 2:s + is_k * QK_SLOTS // 2 + 1]
            return is_k, s if s < CHUNKS else None, 2 * (s - CHUNKS), bias

        def spread(tensor, half, c):
            part = slice(0, P) if half is None else slice(half * TAIL, (half + 1) * TAIL)
            return tensor[part, :, c * GROUP:(c + 1) * GROUP]

        def from_ring(slot, half=None):
            part = slice(0, P) if half is None else slice(half * TAIL, (half + 1) * TAIL)
            return ring[part, bank(slot), 0:UT].rearrange("p (g t) -> p g t", t=GROUP)

        def o_place(tensor, part, n):
            at = (n % (QUADS // UNIT)) * QUAD * GROUP
            return tensor[part, :, at:at + QUAD * GROUP].rearrange("p c (j t) -> p j c t", t=GROUP)

        def from_mixed(tensor, part):
            return tensor[part, :, :].rearrange("p j (c t) -> p j c t", t=GROUP)

        @block.scalar
        def _(act):
            act.dma_start(b_qk[:, :], dram["b_qk"]).then_inc(biases_loaded, 16)
            act.dma_start(b_v[:, :], dram["b_v"].to_broadcast([P, QKV])).then_inc(biases_loaded, 16)
            act.dma_start(b_proj[:, :], dram["b_proj"].to_broadcast([P, D])).then_inc(biases_loaded, 16)
            for signal in (ring_free, exps_ready, mixed, mixed_lo, out_filled, out_read, v_sent, *h1_stored):
                signal.lend(act)

            def load_x(turn, event, unit):
                if event == 0:
                    act.wait_ge(xn_ready.sem, xn_ready.at(turn, -1))
                act.dma_start(xin[:, :, :], dram["h0"][rows(unit), :].rearrange("(b p) d -> p b d", p=P)).then_inc(x_loaded.sem, 16)

            def split_x(turn, _, slot, hi, source):
                for part, to in enumerate((xt_hi, xt_twin_hi)):
                    act.wait_ge(ring_filled.sem, ring_filled.at(turn, slot + part))
                    nc.scalar.activation(to[:, :], ring[:, bank(slot + part), 0:UT], ACT.Copy).then_inc(ring_hi.sem, 1)

            def split_qk(turn, i, slot, hi, source):
                is_k, main, pair, bias = qk_place(i)
                act.wait_ge(ring_filled.sem, ring_filled.at(turn, slot))
                if main is not None:
                    last = nc.scalar.activation(spread(k_hi if is_k else q_hi, None, main), from_ring(slot), ACT.Identity, bias=bias)
                else:
                    for half in range(2):
                        last = nc.scalar.activation(spread(k_twin_hi if is_k else q_stack, half, pair + half), from_ring(slot, half),
                                                    ACT.Identity, bias=bias[half * TAIL:(half + 1) * TAIL, :])
                last.then_inc(ring_hi.sem, 1)

            def exps(turn, n, slot, hi, source):
                act.wait_ge(max_ready.sem, max_ready.at(turn, n))
                for j in range(QUAD):
                    last = nc.scalar.activation(probs[:, n, j, :], ps_scores[:, n % 2, j, :], ACT.Exp,
                                                bias=neg_max[:, n, j:j + 1], accum_out=sums[:, n, j:j + 1])
                last.then_inc(exps_ready.sem, 1)

            def turned_probs(turn, n, slot, hi, source):
                act.wait_ge(ring_filled.sem, ring_filled.at(turn, slot))
                act.wait_ge(mixed.sem, mixed.at(turn, n - 2))
                nc.scalar.activation(pt_hi[:, n % 2, :, :], ring[:, bank(slot), :].rearrange("p (j k) -> p j k", j=QUAD), ACT.Copy).then_inc(ring_hi.sem, 1)

            def mixed_rows(turn, n, slot, hi, source):
                b = n // (QUADS // UNIT)
                if n % (QUADS // UNIT) == 0:
                    act.wait_ge(out_filled.sem, out_filled.at(turn, b - 1))
                act.wait_ge(mixed.sem, mixed.at(turn, n))
                full, low = slice(0, P), slice(0, TAIL)
                nc.scalar.activation(o_place(o_hi, full, n), from_mixed(ps_mixed, full), ACT.Copy)
                nc.scalar.activation(o_place(o_stack, low, n), from_mixed(ps_mixed_tail, low), ACT.Copy).then_inc(mixed_hi.sem, 1)

            load_x(0, -1, 0)
            act.wait_ge(biases_loaded, 48)
            turns(act, {"S": exps, "X": split_x, "T": turned_probs, "Q": split_qk, "R": mixed_rows},
                  lambda turn: load_x(turn, 0, turn + 1))

        @block.vector
        def _(dve):
            def norm(turn, part, slot, hi, source):
                event = event_of(slot)
                steps = Steps(dve, dve_step, turn, event * NORM_STEPS + min(part, 1) * 2 + max(part - 1, 0) * 3, passed=keep["passed"])
                if part == 0:
                    dve.wait_ge(x_loaded.sem, x_loaded.at(turn, event))
                    moments_of(nc, steps, stats, moments, [xin[:, b, :] for b in range(UNIT)])
                elif part <= ROOT_PARTS:
                    inverse_root(nc, steps, part - 1, moments[:, :, 1], 1e-5, half[:, :], guess[:, :], rstd[:, :], work[:, :])
                else:
                    for b in range(UNIT):
                        for to, of in ((slice(0, D), slice(0, D)), (slice(D, D + TAIL), slice(MAIN, D))):
                            last = nc.vector.tensor_scalar(xn[:, b, to], xin[:, b, of], moments[:, b, 0:1], rstd[:, b:b + 1],
                                                           ALU.subtract, ALU.mult)
                    last.then_inc(xn_ready.sem, 1)

            def split_x(turn, _, slot, hi, source):
                for part, (to, of) in enumerate(((xt_lo, xt_hi), (xt_twin_lo, xt_twin_hi))):
                    dve.wait_ge(ring_hi.sem, ring_hi.at(turn, hi + part))
                    nc.vector.tensor_tensor(to[:, :], ring[:, bank(slot + part), 0:UT], raw(of[:, :]), ALU.subtract).then_inc(ring_free.sem, 1)

            def split_qk(turn, i, slot, hi, source):
                is_k, main, pair, bias = qk_place(i)
                dve.wait_ge(ring_hi.sem, ring_hi.at(turn, hi))
                if main is not None:
                    of, to = (k_hi, k_lo) if is_k else (q_hi, q_lo)
                    last = nc.vector.scalar_tensor_tensor(out=spread(to, None, main), in0=from_ring(slot), scalar=bias,
                                                          in1=raw(spread(of, None, main)), op0=ALU.add, op1=ALU.subtract)
                else:
                    for half in range(2):
                        of = spread(k_twin_hi if is_k else q_stack, half, pair + half)
                        to = spread(k_twin_lo, half, pair + half) if is_k else spread(q_stack, 1 - half, pair + half)
                        last = nc.vector.scalar_tensor_tensor(out=to, in0=from_ring(slot, half), scalar=bias[half * TAIL:(half + 1) * TAIL, :],
                                                              in1=raw(of), op0=ALU.add, op1=ALU.subtract)
                last.then_inc(ring_free.sem, 1)

            def biased_v(turn, i, slot, hi, source):
                b, s = divmod(i, VCUTS)
                if s == 0:
                    event = (-1 if slot < 0 else 1) if b == 0 else 0
                    dve.wait_ge(v_sent.sem, v_sent.at(turn, event - 1))
                cols = slice(s * VCUT, (s + 1) * VCUT)
                dve.wait_ge(ring_filled.sem, ring_filled.at(turn, slot))
                nc.vector.tensor_tensor(v_flat[:, cols], ring[:, bank(slot), :], b_v[:, cols], ALU.add).then_inc(ring_free.sem, 1)

            def row_max(turn, n, slot, hi, source):
                dve.wait_ge(scored.sem, scored.at(turn, n))
                nc.vector.tensor_reduce(out=neg_max[:, n, :], in_=ps_scores[:, n % 2, :, :], op=ALU.max, axis=X, negate=True).then_inc(max_ready.sem, 1)

            def invert(turn, n, slot, hi, source):
                dve.wait_ge(exps_ready.sem, exps_ready.at(turn, n))
                nc.vector.reciprocal(inverse[:, n, :], sums[:, n, :]).then_inc(inverse_ready.sem, 1)

            def turned_probs(turn, n, slot, hi, source):
                dve.wait_ge(ring_hi.sem, ring_hi.at(turn, hi))
                nc.vector.tensor_tensor(pt_lo[:, n % 2, :, :], ring[:, bank(slot), :].rearrange("p (j k) -> p j k", j=QUAD), raw(pt_hi[:, n % 2, :, :]),
                                        ALU.subtract).then_inc(ring_free.sem, 1)

            def mixed_rows(turn, n, slot, hi, source):
                full, low, high = slice(0, P), slice(0, TAIL), slice(TAIL, P)
                dve.wait_ge(mixed_hi.sem, mixed_hi.at(turn, n))
                nc.vector.tensor_tensor(o_place(o_lo, full, n), from_mixed(ps_mixed, full), raw(o_place(o_hi, full, n)), ALU.subtract)
                nc.vector.tensor_tensor(o_place(o_stack, high, n), from_mixed(ps_mixed_tail, low), raw(o_place(o_stack, low, n)), ALU.subtract).then_inc(mixed_lo.sem, 1)

            def finish(turn, b, slot, hi, source):
                if b == 0:
                    dve.wait_ge(residual_loaded.sem, residual_loaded.at(turn, 0))
                    nc.vector.tensor_tensor(residual[:, :, :], residual[:, :, :], b_proj[:, :].unsqueeze(1).to_broadcast([P, UNIT, D]), ALU.add).then_inc(residual_biased.sem, 1)
                dve.wait_ge(residual_biased.sem, residual_biased.at(turn, 0))
                dve.wait_ge(h1_stored[b].sem, h1_stored[b].at(turn, -1))
                dve.wait_ge(out_filled.sem, out_filled.at(turn, b))
                nc.vector.tensor_tensor(h1[:, b, :], out_of(b), residual[:, b, :], ALU.add).then_inc(out_read.sem, 1)

            dve.wait_ge(biases_loaded, 48)
            turns(dve, {"N": norm, "S": row_max, "I": invert, "V": biased_v, "X": split_x, "T": turned_probs, "Q": split_qk,
                        "R": mixed_rows, "F": finish})


def mixer(nc, keep, dram):
    UNIT = 4
    UNITS = TILES // UNIT
    UT = UNIT * P
    RING = 3
    SETS = HEADS // QUAD
    HALVES = 2 * UNIT
    PER_HALF = QUAD // 2
    VV = 2 * HD
    with ExitStack() as ctx:
        sb = lambda name, shape, dt=F32: ctx.enter_context(nc.sbuf_tensor(f"mix_{name}", shape, dt))
        ps = lambda name, shape: ctx.enter_context(nc.psum_tensor(f"mix_{name}", shape, F32))
        sem = lambda name: ctx.enter_context(nc.semaphore(f"mix_{name}"))
        QK = 2 * SETS * P
        W_IN = QK + D
        raw_in = sb("raw_in", [P, 2, W_IN + D])
        w_hi, w_lo, w_half, w_stack = (sb(f"w_{n}", [P, W_IN + D], F32R) for n in ("hi", "lo", "half", "stack"))
        b_qk = sb("b_qk", [P, 2 * SETS])
        b_low = sb("b_low", [P, 2 * SETS])
        b_v, b_out, gain, shift = (sb(n, [P, D]) for n in ("b_v", "b_out", "gain", "shift"))
        low_rows = sb("low_rows", [P, 1])
        lane = sb("lane", [P, 1], I32)
        hin = sb("hin", [P, UNIT, D])
        y = sb("y", [P, UNIT, D])
        residual = sb("residual", [P, UNIT, D])
        zn = sb("zn", [P, UNIT, MAIN + 2 * TAIL])
        zt_hi, zt_lo = (sb(n, [P, 2, UT], F32R) for n in ("zt_hi", "zt_lo"))
        q_low, q_stack, k_hi, k_lo = (sb(n, [P, SETS, UT], F32R) for n in ("q_low", "q_stack", "k_hi", "k_lo"))
        v_sum = sb("v_sum", [P, UNIT, D])
        vv = sb("vv", [P, UNIT, HEADS, VV], F32R)
        probs = sb("probs", [P, 2, PER_HALF, SETS, P])
        pt_hi, pt_lo = (sb(n, [P, 2 * PER_HALF, SETS, P], F32R) for n in ("pt_hi", "pt_lo"))
        context = sb("context", [P, 2, MAIN + 2 * TAIL])
        ct_hi, ct_lo = (sb(n, [P, 2, P], F32R) for n in ("ct_hi", "ct_lo"))
        x2 = sb("x2", [P, 2, D])
        top, neg_max, sums = (sb(n, [P, 2, PER_HALF, SETS]) for n in ("top", "neg_max", "sums"))
        inverse = sb("inverse", [P, 2, SETS, QUAD])
        stats = sb("stats", [P, UNIT, 6])
        moments = sb("moments", [P, UNIT, 2])
        half, guess, rstd, work = (sb(n, [P, UNIT]) for n in ("half", "guess", "rstd", "work"))
        stage, w1_half = raw_in[:, :, 0:HID], w_half[:, 0:HID]
        stage2 = sb("stage2", [P, HC, D])
        ps_scores = ps("ps_scores", [P, QUAD, 512])
        ring = ps("ring", [P, RING, 512])
        ps_context = ps("ps_context", [P, 512])

        QK_SLOTS = 2 * SETS
        SLOTS_OF = {"V": 1, "T": PER_HALF, "FT": 1, "FO": 1, "X": 2, "Q": 1}
        HIS_OF = {"T": PER_HALF, "FT": 1, "X": 2, "Q": 1}
        WAY_IN = " ".join(f"N{i}" for i in range(14)) + " X0 Q0 Q1 Q2 Q3 Q4 Q5"
        TURN = """S0 S1 V0 V1 V2 V3 T0 W0 W1 W2 W3 S2 +N0 T1 +N1 A0 +N2 S3 +N3 T2 +N4 A1 +N5 S4 C0 T3 +N6 A2 +N7 FT0 S5 +N8 T4 FO0 +N9 A3
                  +N10 S6 C1 T5 +N11 A4 FT1 S7 +N12 T6 FO1 +N13 A5 C2 T7 FT2 +X0 +Q0 A6 +Q1 FO2 +Q2 A7 +Q3 C3 +Q4 FT3 +Q5 FO3"""
        plan = lambda steps, more=True, first=(0, 0): plan_of(steps, SLOTS_OF, HIS_OF, {"A": "T", "FO": "FT", "Q": "X"}, more, first)
        SLOTS_BEFORE = 2 + QK_SLOTS
        _, SLOTS, HIS = plan(TURN)
        assert SLOTS % RING == 0
        bank = lambda slot: (slot + SLOTS_BEFORE) % RING
        out_slots = {more: [slot for kind, _, slot, _, _ in plan(TURN, more)[0] if kind == "FO"] for more in (True, False)}
        ring_filled = Signal(sem("ring_filled"), SLOTS, SLOTS_BEFORE)
        ring_hi = Signal(sem("ring_hi"), HIS, SLOTS_BEFORE)
        ring_free = Signal(sem("ring_free"), SLOTS, SLOTS_BEFORE, lent=RING)
        h_loaded = Signal(sem("h_loaded"), 1, 1, step=16)
        zn_ready = Signal(sem("zn_ready"), 1, 1)
        v_hi_ready = Signal(sem("v_hi_ready"), UNIT)
        vv_ready = Signal(sem("vv_ready"), UNIT)
        scored = Signal(sem("scored"), HALVES)
        max_ready = Signal(sem("max_ready"), HALVES)
        exps_ready = Signal(sem("exps_ready"), HALVES, lent=2)
        mixed = Signal(sem("mixed"), HALVES)
        inverse_ready = Signal(sem("inverse_ready"), HALVES)
        context_read = Signal(sem("context_read"), UNIT, lent=1)
        context_ready = Signal(sem("context_ready"), UNIT)
        x2_stored = [Signal(sem(f"x2_stored{b}"), UNIT // 2, lent=1, step=16) for b in range(2)]
        consts_loaded, weights_ready, lane_ready, raw_loaded = sem("consts_loaded"), sem("weights_ready"), sem("lane_ready"), sem("raw_loaded")
        weight_hi = sem("weight_hi")
        residual_ready = Signal(sem("residual_ready"), 1, 1)
        dve_setup = Signal(sem("dve_setup"), 0)
        NORM = 2 * NORM_STEPS + 4
        dve_norm = Signal(sem("dve_norm"), NORM, NORM)
        MAXES = 1
        dve_max = Signal(sem("dve_max"), HALVES * MAXES)
        CONTEXTS = 1
        dve_context = Signal(sem("dve_context"), UNIT * CONTEXTS)
        pool_step = Signal(sem("pool_step"), 0)
        stage_loaded = sem("stage_loaded")
        block = ctx.enter_context(nc.Block())

        def turns(engine, do, following=None):
            walk(0, plan(WAY_IN, first=(-SLOTS_BEFORE, -SLOTS_BEFORE))[0], do)
            if following:
                following(0, -1)
            with engine.Fori(0, UNITS - 1) as turn:
                walk(turn, plan(TURN)[0], do)
                if following:
                    following(turn, 0)
            walk(UNITS - 1, plan(TURN, False)[0], do)

        @block.sync
        def _(sp):
            for part, (to, of) in enumerate(((slice(0, P), slice(0, MAIN)), (slice(0, TAIL), slice(MAIN, D)), (slice(TAIL, P), slice(MAIN, D)))):
                sp.dma_start(raw_in[to, min(part, 1), :], dram["w_mix"][of, :]).then_inc(raw_loaded, 16)

            def load(turn, event, unit):
                if event == 0:
                    sp.wait_ge(zn_ready.sem, zn_ready.at(turn, -1))
                sp.dma_start(hin[:, :, :], dram["h1"][bass.ds(unit * UT, UT), :].rearrange("(b p) d -> p b d", p=P)).then_inc(h_loaded.sem, 16)

            def store(turn, more, b):
                sp.wait_ge(ring_free.sem, ring_free.at(turn, out_slots[more][b]))
                sp.dma_start(dram["x2"][bass.ds(turn * UT + b * P, P), :], x2[:, b % 2, :]).then_inc(x2_stored[b % 2].sem, 16)

            def body(turn, more):
                if more:
                    load(turn, 0, turn + 1)
                for b in range(UNIT):
                    store(turn, more, b)

            load(0, -1, 0)
            with sp.Fori(0, UNITS - 1) as turn:
                body(turn, True)
            body(UNITS - 1, False)
            for b in range(2):
                sp.wait_ge(x2_stored[b].sem, x2_stored[b].at(UNITS - 1, UNIT // 2 - 1))

        @block.gpsimd
        def _(pool):
            nc.gpsimd.iota(lane[:, :], pattern=[[0, 1]], base=0, channel_multiplier=1).then_inc(lane_ready, 1)
            steps = Steps(pool, pool_step, 0)
            pool.wait_ge(weights_ready, 1)
            for f in range(FFNS):
                w1_hi, w1_lo, w1_stack, w2_hi, w2_lo = keep["ffn"][f]
                for half_rows in range(2):
                    pool.dma_start(stage[half_rows * TAIL:(half_rows + 1) * TAIL, 1, :], dram["w1"][f, MAIN:D, :]).then_inc(stage_loaded, 16)
                pool.dma_start(stage[:, 0, :], dram["w1"][f, 0:MAIN, :]).then_inc(stage_loaded, 16)
                pool.dma_start(stage2[:, :, :], dram["w2"][f].rearrange("(c p) n -> p c n", p=P)).then_inc(stage_loaded, 16)
                pool.wait_ge(stage_loaded, 64 * (f + 1))
                main, tail = stage[:, 0, :], stage[:, 1, :]
                nc.gpsimd.tensor_scalar(w1_hi[:, :], main, 1.0, 1.0, ALU.mult, ALU.mult)
                nc.gpsimd.tensor_scalar(w2_hi[:, :, :], stage2[:, :, :], 1.0, 1.0, ALU.mult, ALU.mult)
                steps.then(nc.gpsimd.tensor_scalar(w1_half, tail, keep["low_rows"][:, 0:1], 1.0, ALU.mult, ALU.mult))
                nc.gpsimd.tensor_tensor(w1_lo[:, :], main, raw(w1_hi[:, :]), ALU.subtract)
                nc.gpsimd.tensor_tensor(w2_lo[:, :, :], stage2[:, :, :], raw(w2_hi[:, :, :]), ALU.subtract)
                steps.then(nc.gpsimd.tensor_tensor(w1_stack[:, :], tail, raw(w1_half), ALU.subtract))

        @block.tensor
        def _(pe):
            def slot_free(turn, slot):
                pe.wait_ge(ring_free.sem, ring_free.at(turn, slot - RING))

            def scores(turn, n, slot, hi, source):
                b, half = divmod(n, 2)
                if n == 0:
                    pe.wait_ge(ring_free.sem, ring_free.at(turn, -1))
                pe.wait_ge(exps_ready.sem, exps_ready.at(turn, n - 2))
                tile = slice(b * P, (b + 1) * P)
                for s in range(SETS):
                    for i, k in enumerate((k_hi, k_lo)):
                        for j in range(PER_HALF * half, PER_HALF * (half + 1)):
                            rows = slice(32 * j, 32 * j + 32)
                            last = nc.tensor.matmul(ps_scores[:, j, s * P:(s + 1) * P], q_stack[rows, s, tile], k[rows, s, tile], start=i == 0, stop=i == 1)
                last.then_inc(scored.sem, 1)

            def turned(turn, n, slot, hi, source):
                pe.wait_ge(exps_ready.sem, exps_ready.at(turn, n))
                for j in range(PER_HALF):
                    slot_free(turn, slot + j)
                    for s in range(SETS):
                        last = nc.tensor.transpose(ring[:, bank(slot + j), s * P:(s + 1) * P], probs[:, n % 2, j, s, :], keep["ident"][:, :])
                    last.then_inc(ring_filled.sem, 1)

            def mix(turn, n, slot, hi, source):
                b, half = divmod(n, 2)
                if half == 0:
                    pe.wait_ge(vv_ready.sem, vv_ready.at(turn, b))
                    pe.wait_ge(context_read.sem, context_read.at(turn, b - 1))
                pe.wait_ge(ring_free.sem, ring_free.at(turn, source))
                for j in range(PER_HALF):
                    piece = PER_HALF * half + j
                    for s in range(SETS):
                        h = s * QUAD + piece
                        nc.tensor.matmul(ps_context[:, h * VV:(h + 1) * VV], pt_hi[:, piece, s, :], vv[:, b, h, :], start=True, stop=False)
                        last = nc.tensor.matmul(ps_context[:, h * VV:(h + 1) * VV], pt_lo[:, piece, s, :], vv[:, b, h, :], start=False, stop=True)
                last.then_inc(mixed.sem, 1)

            def turn_context(turn, b, slot, hi, source):
                pe.wait_ge(context_ready.sem, context_ready.at(turn, b))
                slot_free(turn, slot)
                for part in range(2):
                    last = nc.tensor.transpose(ring[:, bank(slot), part * P:(part + 1) * P], context[:, b % 2, part * P:(part + 1) * P], keep["ident"][:, :])
                last.then_inc(ring_filled.sem, 1)

            def project_out(turn, b, slot, hi, source):
                pe.wait_ge(ring_free.sem, ring_free.at(turn, source))
                slot_free(turn, slot)
                out = slice(W_IN, W_IN + D)
                passes = ((ct_hi[:, 0, :], w_hi), (ct_lo[:, 0, :], w_hi), (ct_hi[:, 0, :], w_lo), (ct_hi[:, 1, :], w_stack), (ct_lo[:, 1, :], w_stack))
                for i, (c, w) in enumerate(passes):
                    last = nc.tensor.matmul(ring[:, bank(slot), 0:D], c, w[:, out], start=i == 0, stop=i == 4)
                last.then_inc(ring_filled.sem, 1)

            def transposes(turn, _, slot, hi, source):
                pe.wait_ge(zn_ready.sem, zn_ready.at(turn, event_of(slot)))
                for part in range(2):
                    slot_free(turn, slot + part)
                    for b in range(UNIT):
                        last = nc.tensor.transpose(ring[:, bank(slot + part), b * P:(b + 1) * P], zn[:, b, part * P:(part + 1) * P], keep["ident"][:, :])
                    last.then_inc(ring_filled.sem, 1)

            def project_qk(turn, s, slot, hi, source):
                if s == 0:
                    pe.wait_ge(ring_free.sem, ring_free.at(turn, source))
                slot_free(turn, slot)
                cols = slice(s * P, (s + 1) * P)
                passes = ((w_hi, zt_hi, 0), (w_hi, zt_lo, 0), (w_lo, zt_hi, 0), (w_stack, zt_hi, 1), (w_stack, zt_lo, 1))
                for i, (w, z, part) in enumerate(passes):
                    last = nc.tensor.matmul(ring[:, bank(slot), :], w[:, cols], z[:, part, :], start=i == 0, stop=i == 4)
                last.then_inc(ring_filled.sem, 1)

            def project_v(turn, b, slot, hi, source):
                slot_free(turn, slot)
                tile = slice(b * P, (b + 1) * P)
                passes = ((w_hi, zt_hi, 0), (w_hi, zt_lo, 0), (w_lo, zt_hi, 0), (w_stack, zt_hi, 1), (w_stack, zt_lo, 1))
                for i, (w, z, part) in enumerate(passes):
                    last = nc.tensor.matmul(ring[:, bank(slot), 0:D], z[:, part, tile], w[:, QK:W_IN], start=i == 0, stop=i == 4)
                last.then_inc(ring_filled.sem, 1)

            pe.wait_ge(weights_ready, 1)
            turns(pe, {"S": scores, "V": project_v, "T": turned, "A": mix, "FT": turn_context, "FO": project_out, "X": transposes, "Q": project_qk})

        @block.scalar
        def _(act):
            act.dma_start(b_qk[:, :], dram["b_mix_qk"]).then_inc(consts_loaded, 16)
            for to, of in ((b_v, "b_mix_v"), (b_out, "b_mix_out"), (gain, "ln1_g"), (shift, "ln1_b")):
                act.dma_start(to[:, :], dram[of].to_broadcast([P, D])).then_inc(consts_loaded, 16)
            for signal in (ring_free, exps_ready, context_read, *x2_stored):
                signal.lend(act)
            act.wait_ge(raw_loaded, 48)
            nc.scalar.activation(w_hi[:, :], raw_in[:, 0, :], ACT.Copy)
            nc.scalar.activation(w_half[:, :], raw_in[:, 1, :], ACT.Copy, scale=keep["low_rows"][:, 0:1]).then_inc(weight_hi, 1)

            def exps(turn, n, slot, hi, source):
                act.wait_ge(max_ready.sem, max_ready.at(turn, n))
                for j in range(PER_HALF):
                    for s in range(SETS):
                        last = nc.scalar.activation(probs[:, n % 2, j, s, :], ps_scores[:, PER_HALF * (n % 2) + j, s * P:(s + 1) * P], ACT.Exp,
                                                    bias=neg_max[:, n % 2, j, s:s + 1], scale=float(HD) ** -0.5, accum_out=sums[:, n % 2, j, s:s + 1])
                last.then_inc(exps_ready.sem, 1)

            def take_hi(to, slot, of=lambda bank: bank[:, :]):
                act.wait_ge(ring_filled.sem, ring_filled.at(slot[0], slot[1]))
                nc.scalar.activation(to, of(ring[:, bank(slot[1]), :]), ACT.Copy).then_inc(ring_hi.sem, 1)

            def turned(turn, n, slot, hi, source):
                for j in range(PER_HALF):
                    take_hi(pt_hi[:, PER_HALF * (n % 2) + j, :, :], (turn, slot + j), lambda bank: bank[:, 0:SETS * P].rearrange("p (s k) -> p s k", k=P))

            def turn_context(turn, b, slot, hi, source):
                take_hi(ct_hi[:, :, :], (turn, slot), lambda bank: bank[:, 0:2 * P].rearrange("p (a t) -> p a t", a=2))

            def transposes(turn, _, slot, hi, source):
                for part in range(2):
                    take_hi(zt_hi[:, part, :], (turn, slot + part))

            def project_qk(turn, s, slot, hi, source):
                act.wait_ge(ring_filled.sem, ring_filled.at(turn, slot))
                if s < SETS:
                    last = nc.scalar.activation(q_low[:, s, :], ring[:, bank(slot), :], ACT.Identity, scale=low_rows[:, 0:1], bias=b_low[:, s:s + 1])
                else:
                    last = nc.scalar.activation(k_hi[:, s - SETS, :], ring[:, bank(slot), :], ACT.Identity, bias=b_qk[:, s:s + 1])
                last.then_inc(ring_hi.sem, 1)

            def project_v(turn, b, slot, hi, source):
                act.wait_ge(ring_free.sem, ring_free.at(turn, slot))
                nc.scalar.activation(vv[:, b, :, 0:HD], v_sum[:, b, :].rearrange("p (h d) -> p h d", d=HD), ACT.Copy).then_inc(v_hi_ready.sem, 1)

            act.wait_ge(weights_ready, 1)
            turns(act, {"S": exps, "V": project_v, "T": turned, "FT": turn_context, "X": transposes, "Q": project_qk})

        @block.vector
        def _(dve):
            def setup():
                steps = Steps(dve, dve_setup, 0)
                dve.wait_ge(lane_ready, 1)
                steps.then(nc.vector.tensor_scalar(lane[:, :], lane[:, :], HD, None, ALU.bitwise_and))
                steps.then(nc.vector.tensor_scalar(low_rows[:, :], lane[:, :], 1.0 / HD, 1.0, ALU.mult, ALU.mult))
                dve.wait_ge(consts_loaded, 16 * 5)
                nc.vector.tensor_scalar(b_low[:, :], b_qk[:, :], low_rows[:, 0:1], 1.0, ALU.mult, ALU.mult)
                dve.wait_ge(weight_hi, 1)
                nc.vector.tensor_tensor(w_lo[:, :], raw_in[:, 0, :], raw(w_hi[:, :]), ALU.subtract)
                nc.vector.tensor_tensor(w_stack[:, :], raw_in[:, 1, :], raw(w_half[:, :]), ALU.subtract).then_inc(weights_ready, 1)

            def norm(turn, part, slot, hi, source):
                event = event_of(slot)
                ONE = NORM_STEPS + 1
                second, k = divmod(part, ROOT_PARTS + 2)
                done = second * ONE + ((0, 2, 5, 8, 11, 14)[k] if second < 2 else k)
                steps = Steps(dve, dve_norm, turn, event * NORM + done, passed=keep["passed"])
                wide = lambda row: row[:, :].unsqueeze(1).to_broadcast([P, UNIT, D])
                if part == 0:
                    dve.wait_ge(h_loaded.sem, h_loaded.at(turn, event))
                if second == 2 and k == 0:
                    steps.then(nc.vector.tensor_tensor(zn[:, :, 0:D], zn[:, :, 0:D], wide(gain), ALU.mult))
                elif second == 2:
                    steps.then(nc.vector.tensor_tensor(zn[:, :, 0:D], zn[:, :, 0:D], wide(shift), ALU.add))
                    nc.vector.tensor_copy(zn[:, :, D:D + TAIL], zn[:, :, MAIN:D]).then_inc(zn_ready.sem, 1)
                elif k == 0:
                    moments_of(nc, steps, stats, moments, [(y if second else hin)[:, b, :] for b in range(UNIT)])
                elif k <= ROOT_PARTS:
                    inverse_root(nc, steps, k - 1, moments[:, :, 1], 1e-5, half[:, :], guess[:, :], rstd[:, :], work[:, :])
                else:
                    to, of = (zn, y) if second else (y, hin)
                    for b in range(UNIT):
                        last = nc.vector.tensor_scalar(to[:, b, 0:D], of[:, b, :], moments[:, b, 0:1], rstd[:, b:b + 1], ALU.subtract, ALU.mult)
                    steps.then(last)

            def row_max(turn, n, slot, hi, source):
                steps = Steps(dve, dve_max, turn, n)
                dve.wait_ge(scored.sem, scored.at(turn, n))
                banks = slice(PER_HALF * (n % 2), PER_HALF * (n % 2 + 1))
                steps.then(nc.vector.tensor_reduce(out=top[:, n % 2, :, :], in_=ps_scores[:, banks, 0:SETS * P].rearrange("p j (s k) -> p j s k", k=P),
                                                   op=ALU.max, axis=X, negate=True))
                nc.vector.tensor_scalar(neg_max[:, n % 2, :, :], top[:, n % 2, :, :], float(HD) ** -0.5, 1.0, ALU.mult, ALU.mult).then_inc(max_ready.sem, 1)

            def turned(turn, n, slot, hi, source):
                b, half = divmod(n, 2)
                mine = slice(PER_HALF * half, PER_HALF * (half + 1))
                dve.wait_ge(exps_ready.sem, exps_ready.at(turn, n))
                nc.vector.reciprocal(inverse[:, b % 2, :, mine].rearrange("p s j -> p j s"), sums[:, n % 2, :, :]).then_inc(inverse_ready.sem, 1)
                for j in range(PER_HALF):
                    piece = PER_HALF * half + j
                    dve.wait_ge(ring_hi.sem, ring_hi.at(turn, hi + j))
                    nc.vector.tensor_tensor(pt_lo[:, piece, :, :], ring[:, bank(slot + j), 0:SETS * P].rearrange("p (s k) -> p s k", k=P),
                                            raw(pt_hi[:, piece, :, :]), ALU.subtract).then_inc(ring_free.sem, 1)

            def contexts(turn, b, slot, hi, source):
                steps = Steps(dve, dve_context, turn, b * CONTEXTS)
                own = context[:, b % 2, 0:D]
                dve.wait_ge(mixed.sem, mixed.at(turn, 2 * b + 1))
                nc.vector.tensor_reduce(out=own, in_=ps_context[:, 0:HEADS * VV].rearrange("p (h a d) -> p h d a", a=2, d=HD),
                                        op=ALU.add, axis=X).then_inc(context_read.sem, 1)
                dve.wait_ge(context_read.sem, context_read.at(turn, b))
                dve.wait_ge(inverse_ready.sem, inverse_ready.at(turn, 2 * b + 1))
                by_head = own.rearrange("p (h d) -> p h d", d=HD)
                of_head = inverse[:, b % 2, :, :].rearrange("p s j -> p (s j)")
                steps.then(nc.vector.tensor_tensor(by_head, by_head, of_head.unsqueeze(2).to_broadcast([P, HEADS, HD]), ALU.mult))
                nc.vector.tensor_copy(context[:, b % 2, D:D + TAIL], context[:, b % 2, MAIN:D]).then_inc(context_ready.sem, 1)

            def turn_context(turn, b, slot, hi, source):
                dve.wait_ge(ring_hi.sem, ring_hi.at(turn, hi))
                nc.vector.tensor_tensor(ct_lo[:, :, :], ring[:, bank(slot), 0:2 * P].rearrange("p (a t) -> p a t", a=2), raw(ct_hi[:, :, :]), ALU.subtract).then_inc(ring_free.sem, 1)

            def add_out(turn, b, slot, hi, source):
                if b == 0:
                    dve.wait_ge(residual_ready.sem, residual_ready.at(turn, -1))
                dve.wait_ge(x2_stored[b % 2].sem, x2_stored[b % 2].at(turn, b // 2 - 1))
                dve.wait_ge(ring_filled.sem, ring_filled.at(turn, slot))
                nc.vector.tensor_tensor(x2[:, b % 2, :], ring[:, bank(slot), 0:D], residual[:, b, :], ALU.add).then_inc(ring_free.sem, 1)

            def transposes(turn, _, slot, hi, source):
                for part in range(2):
                    dve.wait_ge(ring_hi.sem, ring_hi.at(turn, hi + part))
                    nc.vector.tensor_tensor(zt_lo[:, part, :], ring[:, bank(slot + part), :], raw(zt_hi[:, part, :]), ALU.subtract).then_inc(ring_free.sem, 1)

            def project_qk(turn, s, slot, hi, source):
                dve.wait_ge(ring_hi.sem, ring_hi.at(turn, hi))
                out, low = (q_stack[:, s, :], q_low[:, s, :]) if s < SETS else (k_lo[:, s - SETS, :], k_hi[:, s - SETS, :])
                nc.vector.scalar_tensor_tensor(out=out, in0=ring[:, bank(slot), :], scalar=b_qk[:, s:s + 1], in1=raw(low),
                                               op0=ALU.add, op1=ALU.subtract).then_inc(ring_free.sem, 1)

            def project_v(turn, b, slot, hi, source):
                dve.wait_ge(ring_filled.sem, ring_filled.at(turn, slot))
                nc.vector.tensor_tensor(v_sum[:, b, :], ring[:, bank(slot), 0:D], b_v[:, :], ALU.add).then_inc(ring_free.sem, 1)

            def split_v(turn, b, slot, hi, source):
                dve.wait_ge(v_hi_ready.sem, v_hi_ready.at(turn, b))
                by_head = lambda t: t.rearrange("p (h d) -> p h d", d=HD)
                nc.vector.tensor_tensor(vv[:, b, :, HD:VV], by_head(v_sum[:, b, :]), raw(vv[:, b, :, 0:HD]), ALU.subtract).then_inc(vv_ready.sem, 1)

            def add_bias(turn, event):
                if event == 0:
                    dve.wait_ge(ring_free.sem, ring_free.at(turn, SLOTS - 1))
                nc.vector.tensor_tensor(residual[:, :, :], y[:, :, :], b_out[:, :].unsqueeze(1).to_broadcast([P, UNIT, D]), ALU.add).then_inc(residual_ready.sem, 1)

            setup()
            turns(dve, {"N": norm, "S": row_max, "V": project_v, "W": split_v, "T": turned, "C": contexts, "FT": turn_context, "FO": add_out,
                        "X": transposes, "Q": project_qk}, add_bias)


def experts(nc, keep, dram):
    UNIT = 4
    UNITS = TILES // UNIT
    UT = UNIT * P
    RING = 4
    with ExitStack() as ctx:
        sb = lambda name, shape, dt=F32: ctx.enter_context(nc.sbuf_tensor(f"ffn_{name}", shape, dt))
        ps = lambda name, shape: ctx.enter_context(nc.psum_tensor(f"ffn_{name}", shape, F32))
        sem = lambda name: ctx.enter_context(nc.semaphore(f"ffn_{name}"))
        b1 = sb("b1", [P, FFNS * HC])
        b2 = sb("b2", [P, FFNS, D])
        gain, shift = sb("gain", [P, D]), sb("shift", [P, D])
        raw_gate = sb("raw_gate", [P, 2, NEXP])
        g_hi, g_lo, g_half, g_stack = (sb(f"gate_{n}", [P, NEXP], F32R) for n in ("hi", "lo", "half", "stack"))
        b_gate = sb("b_gate", [P, NEXP])
        earlier = sb("earlier", [P, NEXP, NEXP])
        x2 = sb("x2", [P, UNIT, MAIN + 2 * TAIL])
        h1 = sb("h1", [P, UNIT, D])
        x3 = sb("x3", [P, UNIT, D])
        base = sb("base", [P, UNIT, D])
        xn = sb("xn", [P, UNIT, MAIN + 2 * TAIL])
        bias_sum = sb("bias_sum", [P, UNIT, D])
        bias_part = sb("bias_part", [P, UNIT, D])
        total = sb("total", [P, UNIT, D])
        xt = {kind: tuple(sb(f"{kind}_{n}", [P, 2, UT], F32R) for n in ("hi", "lo")) for kind in ("mlp", "exp")}
        gelu = sb("gelu", [P, 2, UT])
        hid_hi = sb("hid_hi", [P, 3, UT], F32R)
        hid_lo = sb("hid_lo", [P, 3, UT], F32R)
        logits = sb("logits", [P, UNIT, NEXP])
        rank4 = sb("rank4", [P, UNIT, NEXP, NEXP])
        ties = sb("ties", [P, UNIT, NEXP, NEXP])
        rank = sb("rank", [P, UNIT, NEXP])
        best = sb("best", [P, UNIT])
        chosen = sb("chosen", [P, UNIT, NEXP])
        exps = sb("exps", [P, UNIT, NEXP])
        gates = sb("gates", [P, UNIT, NEXP])
        stats = sb("stats", [P, UNIT, 6])
        moments = sb("moments", [P, UNIT, 2])
        half, guess, rstd, work = (sb(n, [P, UNIT]) for n in ("half", "guess", "rstd", "work"))
        ring = ps("ring", [P, RING, 512])
        ps_out = ps("ps_out", [P, UNIT, 512])

        LAG = 2
        chunks_of = lambda ffns: [(f, c) for f in ffns for c in range(HC)]
        CHUNKS_TURN, CHUNKS_BEFORE = FFNS * HC, HC
        assert CHUNKS_TURN % 6 == 0 and CHUNKS_BEFORE % 6 == 0
        IN, GATE = 2, 2
        SLOTS_BEFORE = IN + CHUNKS_BEFORE + IN + GATE
        SLOTS = IN + CHUNKS_TURN + IN + GATE
        assert SLOTS_BEFORE % RING == 0 and SLOTS % RING == 0
        bank = lambda slot: slot % RING
        ring_filled = Signal(sem("ring_filled"), SLOTS, SLOTS_BEFORE)
        ring_free = Signal(sem("ring_free"), SLOTS, SLOTS_BEFORE, lent=RING)
        chunk_read = Signal(sem("chunk_read"), CHUNKS_TURN, CHUNKS_BEFORE)
        inputs_hi = Signal(sem("inputs_hi"), 2 * IN, 2 * IN)
        hi_ready = Signal(sem("hi_ready"), CHUNKS_TURN, CHUNKS_BEFORE)
        lo_ready = Signal(sem("lo_ready"), CHUNKS_TURN, CHUNKS_BEFORE, lent=2)
        hid_used = Signal(sem("hid_used"), CHUNKS_TURN, CHUNKS_BEFORE, lent=3)
        out_free = Signal(sem("out_free"), FFNS * UNIT, UNIT, lent=UNIT)
        x2_loaded = Signal(sem("x2_loaded"), 1, 1, step=48)
        mlp_done = Signal(sem("mlp_done"), 1, 1)
        xn_scaled = Signal(sem("xn_scaled"), 1, 1)
        xn_ready = Signal(sem("xn_ready"), 1, 1)
        gates_ready = Signal(sem("gates_ready"), 1)
        biases_ready = Signal(sem("biases_ready"), 1)
        pool_norm = Signal(sem("pool_norm"), 2, 2)
        pool_biases = Signal(sem("pool_biases"), 2 * NEXP)
        logits_ready = Signal(sem("logits_ready"), 1)
        gate_exps = Signal(sem("gate_exps"), 1)
        total_ready = Signal(sem("total_ready"), 1)
        out_stored = Signal(sem("out_stored"), 1, lent=1, step=16)
        consts_loaded, gate_loaded, gate_hi, gate_ready, ones_ready = (sem(n) for n in ("consts_loaded", "gate_loaded", "gate_hi", "gate_ready", "ones_ready"))
        NORM = NORM_STEPS + 1
        NORM_PARTS = 3 + ROOT_PARTS
        dve_norm = Signal(sem("dve_norm"), NORM, NORM)
        GATE_STEPS = 9
        dve_gate = Signal(sem("dve_gate"), GATE_STEPS)
        block = ctx.enter_context(nc.Block())

        def steps_of(turn, ffns, first, slot, out, following, do):
            chunks = chunks_of(ffns)
            mlp_parts = []

            def second(i):
                f, c = chunks[i]
                do.layer2(turn, first + i, out + i // HC, f, c)
                if c == HC - 1:
                    do.finish(turn, first + i, out + i // HC, f)
                    if f == 0:
                        mlp_parts.extend(range(NORM_PARTS))

            for i, (f, c) in enumerate(chunks):
                if (f, c) == (0, 0):
                    do.inputs(turn, slot, 0, following)
                    slot += IN
                do.layer1(turn, first + i, slot, f, c)
                slot += 1
                if mlp_parts:
                    do.norm(turn, following, mlp_parts.pop(0))
                if i >= LAG:
                    second(i - LAG)
                if first + i == LAG:
                    do.rank(turn)
            behind = list(range(len(chunks) - LAG, len(chunks)))
            if ffns[-1] == 0:
                for i in behind:
                    second(i)
                for part in mlp_parts:
                    do.norm(turn, following, part)
            if following is not None:
                do.inputs(turn, slot, 1, following)
            if ffns[-1] != 0:
                second(behind[0])
            if following is not None:
                do.gates(turn, slot + IN)
            if ffns[-1] != 0:
                for i in behind[1:]:
                    second(i)

        def turns(engine, do):
            steps_of(0, [0], -CHUNKS_BEFORE, -SLOTS_BEFORE, -1, -1, do)
            with engine.Fori(0, UNITS - 1) as turn:
                do.begin(turn)
                steps_of(turn, [1, 2, 0, 3, 4], 0, 0, 0, 0, do)
            do.begin(UNITS - 1)
            steps_of(UNITS - 1, [1, 2, 3, 4], 0, 0, 0, None, do)

        class Steps_of:

            def begin(self, turn): pass
            def rank(self, turn): pass
            def norm(self, turn, event, part): pass
            def inputs(self, turn, slot, kind, event): pass
            def gates(self, turn, slot): pass
            def layer1(self, turn, i, slot, f, c): pass
            def layer2(self, turn, i, out, f, c): pass
            def finish(self, turn, i, out, f): pass

        @block.sync
        def _(sp):
            def load(turn, event, unit):
                if event == 0:
                    sp.wait_ge(mlp_done.sem, mlp_done.at(turn, -1))
                view = lambda name: dram[name][bass.ds(unit * UT, UT), :].rearrange("(b p) d -> p b d", p=P)
                sp.dma_start(x2[:, :, 0:D], view("x2")).then_inc(x2_loaded.sem, 16)
                sp.dma_start(x2[:, :, D:D + TAIL], view("x2")[:, :, MAIN:D]).then_inc(x2_loaded.sem, 16)
                sp.dma_start(h1[:, :, :], view("h1")).then_inc(x2_loaded.sem, 16)

            def store(turn):
                sp.wait_ge(total_ready.sem, total_ready.at(turn, 0))
                sp.dma_start(dram["out"][bass.ds(turn * UT, UT), :].rearrange("(b p) d -> p b d", p=P), total[:, :, :]).then_inc(out_stored.sem, 16)

            load(0, -1, 0)
            with sp.Fori(0, UNITS - 1) as turn:
                load(turn, 0, turn + 1)
                store(turn)
            store(UNITS - 1)
            sp.wait_ge(out_stored.sem, out_stored.at(UNITS - 1, 0))

        @block.gpsimd
        def _(pool):
            nc.gpsimd.memset(earlier[:, :, :], 1.0).then_inc(ones_ready, 1)
            pool.wait_ge(ones_ready, 1)
            nc.gpsimd.affine_select(out=earlier[:, :, :], in_=earlier[:, :, :], compare_op=ALU.is_gt, fill=0.0,
                                    base=0, pattern=[[1, NEXP], [-1, NEXP]], channel_multiplier=0).then_inc(ones_ready, 1)
            pool.wait_ge(consts_loaded, 16 * 5)

            class Do(Steps_of):
                def norm(self, turn, event, part):
                    if part != NORM_PARTS - 1:
                        return
                    steps = Steps(pool, pool_norm, turn, event * 2)
                    wide = lambda row: row.unsqueeze(1).to_broadcast([P, UNIT, D])
                    pool.wait_ge(xn_scaled.sem, xn_scaled.at(turn, event))
                    steps.then(nc.gpsimd.tensor_tensor(xn[:, :, 0:D], xn[:, :, 0:D], wide(gain[:, :]), ALU.mult))
                    steps.then(nc.gpsimd.tensor_tensor(xn[:, :, 0:D], xn[:, :, 0:D], wide(shift[:, :]), ALU.add))
                    apart(pool, keep["passed"])
                    nc.gpsimd.tensor_scalar(xn[:, :, D:D + TAIL], xn[:, :, MAIN:D], 1.0, 1.0, ALU.mult, ALU.mult).then_inc(xn_ready.sem, 1)
                    nc.gpsimd.tensor_tensor(base[:, :, :], x3[:, :, :], h1[:, :, :], ALU.add).then_inc(mlp_done.sem, 1)

                def rank(self, turn):
                    steps = Steps(pool, pool_biases, turn)
                    pool.wait_ge(mlp_done.sem, mlp_done.at(turn, -1))
                    pool.wait_ge(gates_ready.sem, gates_ready.at(turn, 0))
                    apart(pool, keep["passed"])
                    for e in range(NEXP):
                        if e:
                            apart(pool, keep["passed"])
                        for b in range(UNIT):
                            last = nc.gpsimd.tensor_scalar(bias_part[:, b, :], b2[:, 1 + e, :], gates[:, b, e:e + 1], 1.0, ALU.mult, ALU.mult)
                        steps.then(last)
                        steps.then(nc.gpsimd.tensor_tensor(bias_sum[:, :, :], bias_part[:, :, :], (bias_sum if e else base)[:, :, :], ALU.add))
                    pool.sem_inc(biases_ready.sem, 1)

            turns(pool, Do())

        @block.tensor
        def _(pe):
            def slot_free(turn, slot):
                pe.wait_ge(ring_free.sem, ring_free.at(turn, slot - RING))

            class Do(Steps_of):
                def inputs(self, turn, slot, kind, event):
                    x = (x2, xn)[kind]
                    if kind == 0:
                        pe.wait_ge(x2_loaded.sem, x2_loaded.at(turn, event))
                    else:
                        pe.wait_ge(xn_ready.sem, xn_ready.at(turn, event))
                    for part in range(2):
                        slot_free(turn, slot + part)
                        for b in range(UNIT):
                            last = nc.tensor.transpose(ring[:, bank(slot + part), b * P:(b + 1) * P], x[:, b, part * P:(part + 1) * P], keep["ident"][:, :])
                        last.then_inc(ring_filled.sem, 1)
                    if kind == 0:
                        pe.wait_ge(ring_free.sem, ring_free.at(turn, slot + 1))

                def gates(self, turn, slot):
                    pe.wait_ge(gate_ready, 1)
                    pe.wait_ge(ring_free.sem, ring_free.at(turn, slot - 1))
                    x_hi, x_lo = xt["exp"]
                    passes = ((g_hi, x_hi, 0), (g_hi, x_lo, 0), (g_lo, x_hi, 0), (g_stack, x_hi, 1), (g_stack, x_lo, 1))
                    for b in range(UNIT):
                        at, column = slot + b // 2, (b % 2) * NEXP
                        slot_free(turn, at)
                        for k, (g, x, part) in enumerate(passes):
                            last = nc.tensor.matmul(ring[:, bank(at), column:column + NEXP], x[:, part, b * P:(b + 1) * P], g[:, :], start=k == 0, stop=k == 4)
                        if b % 2:
                            last.then_inc(ring_filled.sem, 1)

                def layer1(self, turn, i, slot, f, c):
                    w1_hi, w1_lo, w1_stack, _, _ = keep["ffn"][f]
                    x_hi, x_lo = xt["mlp" if f == 0 else "exp"]
                    slot_free(turn, slot)
                    cols = slice(c * P, (c + 1) * P)
                    passes = ((w1_hi, x_hi, 0), (w1_hi, x_lo, 0), (w1_lo, x_hi, 0), (w1_stack, x_hi, 1), (w1_stack, x_lo, 1))
                    for k, (w, x, part) in enumerate(passes):
                        last = nc.tensor.matmul(ring[:, bank(slot), :], w[:, cols], x[:, part, :], start=k == 0, stop=k == 4)
                    last.then_inc(ring_filled.sem, 1)

                def layer2(self, turn, i, out, f, c):
                    _, _, _, w2_hi, w2_lo = keep["ffn"][f]
                    pe.wait_ge(lo_ready.sem, lo_ready.at(turn, i))
                    for b in range(UNIT):
                        if c == 0:
                            pe.wait_ge(out_free.sem, out_free.at(turn, (out - 1) * UNIT + b))
                        for k, (h, w) in enumerate(((hid_hi, w2_hi), (hid_lo, w2_hi), (hid_hi, w2_lo))):
                            last = nc.tensor.matmul(ps_out[:, b, 0:D], h[:, i % 3, b * P:(b + 1) * P], w[:, c, :], start=c + k == 0, stop=c == HC - 1 and k == 2)
                    last.then_inc(hid_used.sem, 1)

            turns(pe, Do())

        @block.scalar
        def _(act):
            act.dma_start(b1[:, :], dram["b1"]).then_inc(consts_loaded, 16)
            act.dma_start(b2[:, :, :], dram["b2"].rearrange("a (f d) -> a f d", d=D).to_broadcast([P, FFNS, D])).then_inc(consts_loaded, 16)
            for to, of, n in ((gain, "ln2_g", D), (shift, "ln2_b", D), (b_gate, "b_gate", NEXP)):
                act.dma_start(to[:, :], dram[of].to_broadcast([P, n])).then_inc(consts_loaded, 16)
            for part, (to, of) in enumerate(((slice(0, P), slice(0, MAIN)), (slice(0, TAIL), slice(MAIN, D)), (slice(TAIL, P), slice(MAIN, D)))):
                act.dma_start(raw_gate[to, min(part, 1), :], dram["w_gate"][of, :]).then_inc(gate_loaded, 16)
            for signal in (ring_free, lo_ready, hid_used, out_free, out_stored):
                signal.lend(act)
            act.wait_ge(gate_loaded, 48)
            nc.scalar.activation(g_hi[:, :], raw_gate[:, 0, :], ACT.Copy)
            nc.scalar.activation(g_half[:, :], raw_gate[:, 1, :], ACT.Copy, scale=keep["low_rows"][:, 0:1]).then_inc(gate_hi, 1)
            act.wait_ge(consts_loaded, 16 * 5)

            class Do(Steps_of):
                def inputs(self, turn, slot, kind, event):
                    for part in range(2):
                        act.wait_ge(ring_filled.sem, ring_filled.at(turn, slot + part))
                        nc.scalar.activation(xt[("mlp", "exp")[kind]][0][:, part, :], ring[:, bank(slot + part), :], ACT.Copy).then_inc(inputs_hi.sem, 1)

                def layer1(self, turn, i, slot, f, c):
                    if i == HC - 2:
                        act.wait_ge(logits_ready.sem, logits_ready.at(turn, 0))
                        nc.scalar.activation(exps[:, :, :], logits[:, :, :], ACT.Exp).then_inc(gate_exps.sem, 1)
                    act.wait_ge(ring_filled.sem, ring_filled.at(turn, slot))
                    act.wait_ge(lo_ready.sem, lo_ready.at(turn, i - 2))
                    nc.scalar.activation(gelu[:, i % 2, :], ring[:, bank(slot), :], ACT.Gelu, bias=b1[:, f * HC + c:f * HC + c + 1]).then_inc(chunk_read.sem, 1)
                    act.wait_ge(chunk_read.sem, chunk_read.at(turn, i))
                    act.wait_ge(hid_used.sem, hid_used.at(turn, i - 3))
                    nc.scalar.activation(hid_hi[:, i % 3, :], gelu[:, i % 2, :], ACT.Copy).then_inc(hi_ready.sem, 1)

            turns(act, Do())

        @block.vector
        def _(dve):
            def weighed(b, e):
                return gates[:, b, e:e + 1]

            class Do(Steps_of):
                def inputs(self, turn, slot, kind, event):
                    hi, lo = xt[("mlp", "exp")[kind]]
                    for part in range(2):
                        dve.wait_ge(inputs_hi.sem, inputs_hi.at(turn, 2 * IN * event + IN * kind + part))
                        nc.vector.tensor_tensor(lo[:, part, :], ring[:, bank(slot + part), :], raw(hi[:, part, :]), ALU.subtract).then_inc(ring_free.sem, 1)

                def layer1(self, turn, i, slot, f, c):
                    dve.wait_ge(hi_ready.sem, hi_ready.at(turn, i))
                    dve.sem_inc(ring_free.sem, 1)
                    nc.vector.tensor_tensor(hid_lo[:, i % 3, :], gelu[:, i % 2, :], raw(hid_hi[:, i % 3, :]), ALU.subtract).then_inc(lo_ready.sem, 1)

                def begin(self, turn):
                    steps = Steps(dve, dve_gate, turn)
                    for part in range(GATE):
                        dve.wait_ge(ring_filled.sem, ring_filled.at(turn, part - GATE))
                        nc.vector.tensor_tensor(logits[:, 2 * part:2 * part + 2, :], ring[:, bank(part - GATE), 0:2 * NEXP].rearrange("p (b e) -> p b e", e=NEXP),
                                                b_gate[:, :].unsqueeze(1).to_broadcast([P, 2, NEXP]), ALU.add).then_inc(ring_free.sem, 1)
                    dve.wait_ge(ring_free.sem, ring_free.at(turn, -1))
                    steps.then(nc.vector.tensor_reduce(out=best[:, :], in_=logits[:, :, :], op=ALU.max, axis=X))
                    nc.vector.tensor_tensor(logits[:, :, :], logits[:, :, :], best[:, :].unsqueeze(2).to_broadcast([P, UNIT, NEXP]), ALU.subtract).then_inc(logits_ready.sem, 1)
                    self.steps = steps

                def rank(self, turn):
                    steps = self.steps
                    dve.wait_ge(logits_ready.sem, logits_ready.at(turn, 0))
                    pairs = [P, UNIT, NEXP, NEXP]
                    other, own = logits[:, :, :].unsqueeze(2).to_broadcast(pairs), logits[:, :, :].unsqueeze(3).to_broadcast(pairs)
                    nc.vector.tensor_tensor(rank4[:, :, :, :], other, own, ALU.is_gt)
                    steps.then(nc.vector.tensor_tensor(ties[:, :, :, :], other, own, ALU.is_equal))
                    steps.then(nc.vector.tensor_tensor(ties[:, :, :, :], ties[:, :, :, :], earlier[:, :, :].unsqueeze(1).to_broadcast(pairs), ALU.mult))
                    steps.then(nc.vector.tensor_tensor(rank4[:, :, :, :], rank4[:, :, :, :], ties[:, :, :, :], ALU.add))
                    steps.then(nc.vector.tensor_reduce(out=rank[:, :, :], in_=rank4[:, :, :, :], op=ALU.add, axis=X))
                    steps.then(nc.vector.tensor_scalar(chosen[:, :, :], rank[:, :, :], 2.0, None, ALU.is_lt))

                def weigh(self, turn):
                    steps = self.steps
                    dve.wait_ge(gate_exps.sem, gate_exps.at(turn, 0))
                    steps.then(nc.vector.tensor_tensor(gates[:, :, :], exps[:, :, :], chosen[:, :, :], ALU.mult))
                    steps.then(nc.vector.tensor_reduce(out=best[:, :], in_=gates[:, :, :], op=ALU.add, axis=X))
                    steps.then(nc.vector.reciprocal(best[:, :], best[:, :]))
                    nc.vector.tensor_tensor(gates[:, :, :], gates[:, :, :], best[:, :].unsqueeze(2).to_broadcast([P, UNIT, NEXP]), ALU.mult).then_inc(gates_ready.sem, 1)
                    dve.wait_ge(gates_ready.sem, gates_ready.at(turn, 0))
                    assert steps.count == GATE_STEPS

                def finish(self, turn, i, out, f):
                    if f == 0:
                        return self.finish_mlp(turn, i, out, -1 if out < 0 else 0)
                    e = f - 1
                    if e == 0:
                        self.weigh(turn)
                        dve.wait_ge(out_stored.sem, out_stored.at(turn, -1))
                    else:
                        dve.wait_ge(out_free.sem, out_free.at(turn, out * UNIT - 1))
                    dve.wait_ge(hid_used.sem, hid_used.at(turn, i))
                    for b in range(UNIT):
                        if e == 0:
                            last = nc.vector.tensor_scalar(total[:, b, :], ps_out[:, b, 0:D], weighed(b, e), 1.0, ALU.mult, ALU.mult)
                        else:
                            last = nc.vector.scalar_tensor_tensor(out=total[:, b, :], in0=ps_out[:, b, 0:D], scalar=weighed(b, e), in1=total[:, b, :],
                                                                  op0=ALU.mult, op1=ALU.add)
                        last.then_inc(out_free.sem, 1)
                    if e == NEXP - 1:
                        dve.wait_ge(out_free.sem, out_free.at(turn, (out + 1) * UNIT - 1))
                        dve.wait_ge(biases_ready.sem, biases_ready.at(turn, 0))
                        nc.vector.tensor_tensor(total[:, :, :], total[:, :, :], bias_sum[:, :, :], ALU.add).then_inc(total_ready.sem, 1)

                def finish_mlp(self, turn, i, out, event):
                    if event == 0:
                        dve.wait_ge(mlp_done.sem, mlp_done.at(turn, -1))
                    dve.wait_ge(hid_used.sem, hid_used.at(turn, i))
                    for b in range(UNIT):
                        nc.vector.tensor_tensor(x3[:, b, :], ps_out[:, b, 0:D], x2[:, b, 0:D], ALU.add).then_inc(out_free.sem, 1)
                    dve.wait_ge(out_free.sem, out_free.at(turn, (out + 1) * UNIT - 1))

                def norm(self, turn, event, part):
                    steps = Steps(dve, dve_norm, turn, event * NORM + (0, 1, 3, 6, 9, 12, NORM)[part], passed=keep["passed"])
                    if part == 0:
                        steps.then(nc.vector.tensor_tensor(x3[:, :, :], x3[:, :, :], b2[:, 0, :].unsqueeze(1).to_broadcast([P, UNIT, D]), ALU.add))
                    elif part == 1:
                        moments_of(nc, steps, stats, moments, [x3[:, b, :] for b in range(UNIT)])
                    elif part < NORM_PARTS - 1:
                        inverse_root(nc, steps, part - 2, moments[:, :, 1], 1e-5, half[:, :], guess[:, :], rstd[:, :], work[:, :])
                    else:
                        for b in range(UNIT):
                            last = nc.vector.tensor_scalar(xn[:, b, 0:D], x3[:, b, :], moments[:, b, 0:1], rstd[:, b:b + 1], ALU.subtract, ALU.mult)
                        last.then_inc(xn_scaled.sem, 1)

            dve.wait_ge(gate_hi, 1)
            nc.vector.tensor_tensor(g_lo[:, :], raw_gate[:, 0, :], raw(g_hi[:, :]), ALU.subtract)
            nc.vector.tensor_tensor(g_stack[:, :], raw_gate[:, 1, :], raw(g_half[:, :]), ALU.subtract).then_inc(gate_ready, 1)
            dve.wait_ge(ones_ready, 2)
            dve.wait_ge(consts_loaded, 16 * 5)
            turns(dve, Do())


def tower(nc, given, out, scratch):
    dram = {**given, **scratch, "out": out}
    with ExitStack() as ctx:
        sb = lambda name, shape, dt=F32: ctx.enter_context(nc.sbuf_tensor(name, shape, dt))
        keep = {"ident": sb("ident", [P, P]), "low_rows": sb("low_rows", [P, 1]), "passed": ctx.enter_context(nc.semaphore("passed"))}
        with ExitStack() as weights:
            wb = lambda name: weights.enter_context(nc.sbuf_tensor(name, [P, QKV], F32R))
            keep["w_qkv"] = [(wb(f"w_{x}_hi")[:, :], wb(f"w_{x}_lo")[:, :], wb(f"w_{x}_stack")[:, :], None) for x in "qkv"]
            keep["w_proj"] = tuple(wb(f"w_proj_{x}")[:, :] for x in ("hi", "lo", "twin_hi", "twin_lo"))
            embed(nc, keep, dram)
            attention(nc, keep, dram)
        ffn = lambda name, shape: sb(f"ffn_weights_{name}", shape, F32R)
        keep["ffn"] = [(ffn(f"w1_hi{f}", [P, HID]), ffn(f"w1_lo{f}", [P, HID]), ffn(f"w1_stack{f}", [P, HID]),
                        ffn(f"w2_hi{f}", [P, HC, D]), ffn(f"w2_lo{f}", [P, HC, D])) for f in range(FFNS)]
        mixer(nc, keep, dram)
        experts(nc, keep, dram)


def host_layout(inputs):
    a = {k: np.asarray(v) for k, v in inputs.items()}
    ids = np.stack([a["x"].T, a["mask_BS_i1_0"].T], axis=1).reshape(P, 2 * TILES)
    chunk = np.arange(QKV).reshape(CHUNKS, D)
    order = np.concatenate([chunk[:, :MAIN].ravel(), chunk[:, MAIN:].ravel()])
    w, b = a["L0_attn_W_qkv"], a["L0_attn_b_qkv"]
    w_qkv = np.concatenate([w[:, order], w[:, QKV + order], w[:, 2 * QKV:]], axis=1)
    b_qk = np.concatenate([b[order], b[QKV + order]]).reshape(2 * QKV // P, P).T
    w_proj = a["L0_attn_W_proj"].reshape(CHUNKS, D, D)
    heads = lambda x: x.reshape(*x.shape[:-1], 2 * HEADS, HD)
    twice = lambda x: np.stack([x, x], axis=-2).reshape(*x.shape[:-2], -1)
    w_in = a["L0_ffn_in_w"].T
    w_mix = np.concatenate([twice(heads(w_in[:, :2 * D])), w_in[:, 2 * D:], a["L0_ffn_out_w"].T], axis=1)
    given = {
        "ids": ids, "token_emb": a["L0_tok_token_emb"], "type_emb": a["L0_tok_type_emb"], "pos_emb": a["L0_tok_pos_emb"],
        "gamma": a["L0_tok_gamma"][None], "beta": a["L0_tok_beta"][None],
        "w_qkv": w_qkv, "b_qk": b_qk, "b_v": b[None, 2 * QKV:],
        "w_proj_main": w_proj[:, :MAIN].transpose(1, 0, 2).reshape(MAIN, QKV),
        "w_proj_tail": w_proj[:, MAIN:].transpose(1, 0, 2).reshape(TAIL, QKV),
        "b_proj": a["L0_attn_b_proj"][None],
        "w_mix": w_mix, "b_mix_qk": twice(heads(a["L0_ffn_in_b"][:2 * D])).reshape(-1, P).T,
        "b_mix_v": a["L0_ffn_in_b"][None, 2 * D:], "b_mix_out": a["L0_ffn_out_b"][None],
        "ln1_g": a["L0_ffn_ln1_g"][None], "ln1_b": a["L0_ffn_ln1_b"][None],
        "ln2_g": a["L0_ffn_ln2_g"][None], "ln2_b": a["L0_ffn_ln2_b"][None],
        "w1": np.concatenate([a["L0_ffn_mlp_w1"][None], a["L0_ffn_exp_w1"]]),
        "w2": np.concatenate([a["L0_ffn_mlp_w2"][None], a["L0_ffn_exp_w2"]]),
        "b1": np.concatenate([a["L0_ffn_mlp_b1"][None], a["L0_ffn_exp_b1"]]).reshape(FFNS * HC, P).T,
        "b2": np.concatenate([a["L0_ffn_mlp_b2"][None], a["L0_ffn_exp_b2"]]).reshape(1, FFNS * D),
        "w_gate": a["L0_ffn_gate_w"].T, "b_gate": a["L0_ffn_gate_b"][None],
    }
    return {k: np.ascontiguousarray(v) for k, v in given.items()}


def kernel(**inputs):
    import concourse.bacc as bacc
    from concourse.bass_utils import run_bass_kernel_spmd

    nc = bacc.Bacc("TRN2", target_bir_lowering=False, num_devices=1)
    given = host_layout(inputs)
    aps = {k: nc.dram_tensor(f"in_{k}", v.shape, mybir.dt.from_np(v.dtype), kind="ExternalInput").ap() for k, v in given.items()}
    out = nc.dram_tensor("out", (TOKENS, D), F32, kind="ExternalOutput").ap()
    internal = lambda name, shape: nc.dram_tensor(name, shape, F32, kind="Internal").ap()
    scratch = {k: internal(f"{k}_rows", (TOKENS, D)) for k in ("h0", "h1", "y", "x2")}
    scratch["v"] = [internal(f"v_rows{i}", (P, QKV)) for i in range(2)]
    tower(nc, aps, out, scratch)
    ran = run_bass_kernel_spmd(nc, [{f"in_{k}": v for k, v in given.items()}], core_ids=[0])
    return ran.results[0]["out"].reshape(BATCH, SEQ, D)
```

```python
import numpy as np
from contextlib import ExitStack

import concourse.bass as bass
from concourse import mybir
from concourse.alu_op_type import AluOpType as ALU


F32 = mybir.dt.float32
F32R = mybir.dt.float32r
I32 = mybir.dt.int32
ACT = mybir.ActivationFunctionType
X = mybir.AxisListType.X

P = 128
BATCH, SEQ = 16, 128
TOKENS = BATCH * SEQ
TILES = TOKENS // P
D = 192
MAIN, TAIL = P, D - P
CHUNKS = 8
QKV = CHUNKS * D
GROUP = P // CHUNKS
GROUPS = P // GROUP
QUAD = 4
HEADS, HD = 12, 16
HID = 768
HC = HID // P
NEXP = 4
FFNS = 1 + NEXP


class Signal:

    def __init__(self, sem, per_turn, before=0, lent=0, step=1):
        self.sem, self.per_turn, self.before, self.lent, self.step = sem, per_turn, before + lent, lent, step

    def lend(self, engine):
        engine.sem_inc(self.sem, self.lent * self.step)

    def at(self, turn, event):
        if isinstance(turn, int) and isinstance(event, int):
            value = (self.before + turn * self.per_turn + event + 1) * self.step
            assert value > 0
            return value
        return turn * (self.per_turn * self.step) + (self.before + event + 1) * self.step


class Steps:

    def __init__(self, engine, signal, turn, first=0, passed=None):
        self.engine, self.mark, self.turn, self.count, self.passed = engine, signal, turn, first, passed

    def then(self, instruction, settle=True):
        instruction.then_inc(self.mark.sem, 1)
        self.count += 1
        if settle:
            self.settle()

    def settle(self):
        self.engine.wait_ge(self.mark.sem, self.mark.at(self.turn, self.count - 1))


def apart(engine, passed):
    engine.sem_inc(passed, 1)


def raw(hi):
    return hi.bitcast(F32)


def plan_of(steps, slots_of, his_of, sources, more, first=(0, 0)):
    found, (slot, hi), filled = [], first, {}
    for word in steps.split():
        kind, i = word.strip("+0123456789"), int("".join(c for c in word if c.isdigit()))
        if more or word[0] != "+":
            of = sources.get(kind)
            found.append((kind, i, slot, hi, filled.get((of, i), filled.get((of, 0)))))
            slot += slots_of.get(kind, 0)
            hi += his_of.get(kind, 0)
            filled[kind, i] = slot - 1
    return found, slot, hi


def walk(turn, steps, do):
    for kind, *place in steps:
        if kind in do:
            do[kind](turn, *place)


def event_of(slot):
    return -1 if slot < 0 else 0


def inverse_root(nc, steps, part, variance, eps, half, guess, rstd, work):
    MAGIC = 0x5F3759DF
    if part == 0:
        steps.then(nc.vector.tensor_scalar(work, variance, eps, 1.0, ALU.add, ALU.mult))
        nc.vector.tensor_scalar(half, work, -0.5, 1.0, ALU.mult, ALU.mult)
        steps.then(nc.vector.tensor_scalar(guess.bitcast(I32), work.bitcast(I32), 1, None, ALU.arith_shift_right))
        steps.then(nc.vector.tensor_scalar(rstd.bitcast(I32), guess.bitcast(I32), -1.0, float(MAGIC), ALU.mult, ALU.add))
    else:
        steps.then(nc.vector.tensor_tensor(work, rstd, rstd, ALU.mult))
        steps.then(nc.vector.tensor_tensor(work, work, half, ALU.mult))
        steps.then(nc.vector.scalar_tensor_tensor(out=rstd, in0=work, scalar=1.5, in1=rstd, op0=ALU.add, op1=ALU.mult))


ROOT_PARTS = 4
ROOT_STEPS = 3 * ROOT_PARTS


def moments_of(nc, steps, stats, moments, tiles):
    for i, tile in enumerate(tiles):
        last = nc.vector.bn_stats(stats[:, i, :], tile)
    steps.then(last)
    apart(steps.engine, steps.passed)
    for i in range(len(tiles)):
        last = nc.vector.bn_aggr(moments[:, i, :], stats[:, i, :])
    steps.then(last)


NORM_STEPS = 2 + ROOT_STEPS


TAKE = TILES // 2


def embed(nc, keep, dram):
    TAKES = TILES // TAKE
    with ExitStack() as ctx:
        sb = lambda name, shape, dt=F32: ctx.enter_context(nc.sbuf_tensor(f"embed_{name}", shape, dt))
        sem = lambda name: ctx.enter_context(nc.semaphore(f"embed_{name}"))
        ids = sb("ids", [P, 2, TILES], I32)
        emb = [sb("emb", [P, TAKE, D]), keep["last_emb"]]
        type_id = sb("type_id", [P, TILES])
        pos, types = sb("pos", [P, D]), sb("types", [P, 2, D])
        first, step_up = sb("first", [P, D]), sb("step_up", [P, D])
        gamma = sb("gamma", [P, D])
        beta = sb("beta", [P, D])
        stats = sb("stats", [P, TILES, 6])
        moments = sb("moments", [P, TILES, 2])
        half, guess, rstd, work, offset = (sb(n, [P, TILES]) for n in ("half", "guess", "rstd", "work", "offset"))
        stage = [(sb(f"stage_main{i}", [P, QKV]), sb(f"stage_tail{i}", [P if i == 3 else TAIL, QKV])) for i in range(4)]

        ids_loaded, rows_loaded, pos_loaded = sem("ids_loaded"), sem("rows_loaded"), sem("pos_loaded")
        token_rows = [sem(f"token_rows{i}") for i in range(TAKES)]
        weights_loaded = [sem(f"weights_loaded{i}") for i in range(4)]
        const_ready = sem("const_ready")
        roots_ready, scaled = sem("roots_ready"), sem("scaled")
        h0_ready = sem("h0_ready")
        hi_ready, proj_hi_ready, pool_lo_ready = sem("w_hi_ready"), sem("w_proj_hi_ready"), sem("w_pool_lo_ready")
        dve_step = Signal(sem("dve_step"), 0)
        block = ctx.enter_context(nc.Block())

        def main_lo_of(engine, i):
            main_hi, main_lo, _ = keep["w_qkv"][i]
            return engine.tensor_tensor(main_lo, stage[i][0][:, :], raw(main_hi), ALU.subtract)

        def tail_lo_of(engine, i):
            stack = keep["w_qkv"][i][2]
            return engine.tensor_tensor(stack[TAIL:P, :], stage[i][1][:, :], raw(stack[0:TAIL, :]), ALU.subtract)

        @block.sync
        def _(sp):
            sp.dma_start(ids[:, :, :], dram["ids"].rearrange("p (a b) -> p a b", a=2)).then_inc(ids_loaded, 16)
            for i in range(4):
                main, tail = stage[i]
                cut = dram["w_qkv"][:, i * QKV:(i + 1) * QKV] if i < 3 else None
                src_main = cut[0:MAIN, :] if i < 3 else dram["w_proj_main"]
                src_tail = cut[MAIN:D, :] if i < 3 else dram["w_proj_tail"]
                if i == 1:
                    sp.wait_ge(token_rows[0], 16 * TAKE)
                sp.dma_start(main[:, :], src_main).then_inc(weights_loaded[i], 16)
                for half in range(2 if i == 3 else 1):
                    sp.dma_start(tail[half * TAIL:(half + 1) * TAIL, :], src_tail).then_inc(weights_loaded[i], 16)
            for t in range(TAKES):
                sp.wait_ge(h0_ready, t + 1)
                sp.dma_start(dram["h0"].rearrange("(b p) d -> p b d", p=P)[:, t * TAKE:(t + 1) * TAKE, :],
                             emb[t][:, :, :]).then_inc(keep["h0_stored"][t], 16)
            sp.wait_ge(keep["h0_stored"][0], 16)

        @block.gpsimd
        def _(pool):
            pool.wait_ge(ids_loaded, 16)
            for t in range(TAKES):
                for i in range(t * TAKE, (t + 1) * TAKE):
                    nc.gpsimd.indirect_dma_start(emb[t][:, i % TAKE, :], None, dram["token_emb"],
                                                 bass.IndirectOffsetOnAxis(ap=ids[:, 0, i:i + 1], axis=0)).then_inc(token_rows[t], 16)
            nc.gpsimd.memset(keep["ident"][:, :], 0.0).then_inc(const_ready, 1)
            pool.wait_ge(const_ready, 1)
            nc.gpsimd.affine_select(out=keep["ident"][:, :], in_=keep["ident"][:, :], compare_op=ALU.not_equal,
                                    fill=1.0, base=0, pattern=[[-1, P]], channel_multiplier=1).then_inc(const_ready, 1)
            pool.wait_ge(weights_loaded[3], 48)
            views = [w.rearrange("p (c n) -> p c n", c=CHUNKS) for w in (stage[3][0][:, :], stage[3][1][:, :])]
            for w, view in zip(keep["w_proj"], views):
                nc.gpsimd.tensor_scalar(w[:, :, 0, :], view, 1.0, 1.0, ALU.mult, ALU.mult).then_inc(proj_hi_ready, 1)
            pool.wait_ge(proj_hi_ready, 2)
            for w, view in zip(keep["w_proj"], views):
                nc.gpsimd.tensor_tensor(w[:, :, 1, :], view, raw(w[:, :, 0, :]), ALU.subtract).then_inc(pool_lo_ready, 1)
            pool.wait_ge(hi_ready, 3)
            main_lo_of(nc.gpsimd, 2).then_inc(pool_lo_ready, 1)
            pool.wait_ge(pool_lo_ready, 3)
            tail_lo_of(nc.gpsimd, 2)

        @block.scalar
        def _(act):
            act.dma_start(pos[:, :], dram["pos_emb"]).then_inc(pos_loaded, 16)
            act.dma_start(types[:, :, :], dram["type_emb"].rearrange("a d -> (a d)").unsqueeze(0).to_broadcast([P, 2 * D]).rearrange("p (a d) -> p a d", a=2)).then_inc(pos_loaded, 16)
            act.dma_start(gamma[:, :], dram["gamma"].to_broadcast([P, D])).then_inc(rows_loaded, 16)
            act.dma_start(beta[:, :], dram["beta"].to_broadcast([P, D])).then_inc(rows_loaded, 16)
            for i, (main_hi, _, stack) in enumerate(keep["w_qkv"]):
                main, tail = stage[i]
                act.wait_ge(weights_loaded[i], 32)
                nc.scalar.activation(main_hi, main[:, :], ACT.Copy)
                nc.scalar.activation(stack[0:TAIL, :], tail[:, :], ACT.Copy).then_inc(hi_ready, 1)
            for t in range(TAKES):
                act.wait_ge(roots_ready, t + 1)
                for i in range(t * TAKE, (t + 1) * TAKE):
                    last = nc.scalar.activation(emb[t][:, i % TAKE, :], emb[t][:, i % TAKE, :], ACT.Identity, scale=rstd[:, i:i + 1], bias=offset[:, i:i + 1])
                last.then_inc(scaled, 1)

        @block.vector
        def _(dve):
            steps = Steps(dve, dve_step, 0, passed=keep["passed"])
            steps.then(nc.vector.memset(keep["low_rows"][0:TAIL, :], 0.0))
            steps.then(nc.vector.memset(keep["low_rows"][TAIL:P, :], 1.0))

            def prepare():
                dve.wait_ge(ids_loaded, 16)
                nc.vector.tensor_copy(type_id[:, :], ids[:, 1, :])
                dve.wait_ge(pos_loaded, 32)
                nc.vector.tensor_tensor(first[:, :], pos[:, :], types[:, 0, :], ALU.add)
                steps.then(nc.vector.tensor_tensor(step_up[:, :], types[:, 1, :], types[:, 0, :], ALU.subtract))

            wide = lambda row: row[:, :].unsqueeze(1).to_broadcast([P, TAKE, D])

            def sums_and_roots(t):
                take = slice(t * TAKE, (t + 1) * TAKE)
                dve.wait_ge(token_rows[t], 16 * TAKE)
                for i in range(t * TAKE, (t + 1) * TAKE):
                    last = nc.vector.scalar_tensor_tensor(out=emb[t][:, i % TAKE, :], in0=step_up[:, :], scalar=type_id[:, i:i + 1], in1=emb[t][:, i % TAKE, :],
                                                          op0=ALU.mult, op1=ALU.add)
                steps.then(last)
                steps.then(nc.vector.tensor_tensor(emb[t][:, :, :], emb[t][:, :, :], wide(first), ALU.add))
                moments_of(nc, steps, stats[:, take, :], moments[:, take, :], [emb[t][:, i, :] for i in range(TAKE)])
                for part in range(ROOT_PARTS):
                    inverse_root(nc, steps, part, moments[:, take, 1], 1e-12, half[:, take], guess[:, take], rstd[:, take], work[:, take])
                nc.vector.scalar_tensor_tensor(out=offset[:, take], in0=moments[:, take, 0], scalar=-1.0, in1=rstd[:, take],
                                               op0=ALU.mult, op1=ALU.mult).then_inc(roots_ready, 1)

            def gain_and_shift(t):
                dve.wait_ge(scaled, t + 1)
                if t == 0:
                    dve.wait_ge(rows_loaded, 32)
                steps.then(nc.vector.tensor_tensor(emb[t][:, :, :], emb[t][:, :, :], wide(gamma), ALU.mult))
                nc.vector.tensor_tensor(emb[t][:, :, :], emb[t][:, :, :], wide(beta), ALU.add).then_inc(h0_ready, 1)

            prepare()
            for t in range(TAKES):
                dve.wait_ge(hi_ready, t + 1)
                main_lo_of(nc.vector, t)
                tail_lo_of(nc.vector, t)
                sums_and_roots(t)
            gain_and_shift(0)
            gain_and_shift(1)


def attention(nc, keep, dram):
    UNIT = 2
    UNITS = TILES // UNIT
    UT = UNIT * P
    UG = UNIT * GROUPS
    QUADS = UG // QUAD
    RING = 4
    VCUT = 512
    VCUTS = QKV // VCUT
    with ExitStack() as ctx:
        sb = lambda name, shape, dt=F32: ctx.enter_context(nc.sbuf_tensor(f"attn_{name}", shape, dt))
        ps = lambda name, shape: ctx.enter_context(nc.psum_tensor(name, shape, F32))
        sem = lambda name: ctx.enter_context(nc.semaphore(f"attn_{name}"))
        w_q, w_k, w_v = keep["w_qkv"]
        w_out, w_out_twin = keep["w_proj"]
        b_qk = sb("b_qk", [P, 2 * QKV // P])
        b_v = sb("b_v", [P, QKV])
        b_proj = sb("b_proj", [P, D])
        xin = sb("xin", [P, UNIT, D])
        xn = sb("xn", [P, UNIT, MAIN + 2 * TAIL])
        xt_hi, xt_lo, xt_twin_hi, xt_twin_lo = (sb(n, [P, UT], F32R) for n in ("xt_hi", "xt_lo", "xt_twin_hi", "xt_twin_lo"))
        q_hi, q_lo, q_stack, k_hi, k_lo, k_twin_hi, k_twin_lo = (
            sb(n, [P, UG, P], F32R) for n in ("q_hi", "q_lo", "q_stack", "k_hi", "k_lo", "k_twin_hi", "k_twin_lo"))
        probs = sb("probs", [P, QUADS, QUAD, P])
        pt_hi = sb("pt_hi", [P, 2, QUAD, P], F32R)
        pt_lo = sb("pt_lo", [P, 2, QUAD, P], F32R)
        v_flat = sb("v_flat", [P, QKV])
        v_rows = sb("v_rows", [P, GROUPS, D])
        v_hi = sb("v_hi", [P, GROUPS, D], F32R)
        v_lo = sb("v_lo", [P, GROUPS, D], F32R)
        o_hi, o_lo, o_stack = (sb(n, [P, CHUNKS, P], F32R) for n in ("o_hi", "o_lo", "o_stack"))
        residual, h1 = (keep["last_emb"][:, i * UNIT:(i + 1) * UNIT, :] for i in range(2))
        neg_max = sb("neg_max", [P, QUADS, QUAD])
        sums = sb("sums", [P, QUADS, QUAD])
        inverse = sb("inverse", [P, QUADS, QUAD])
        stats = sb("stats", [P, UNIT, 6])
        moments = sb("moments", [P, UNIT, 2])
        half, guess, rstd, work = (sb(n, [P, UNIT]) for n in ("half", "guess", "rstd", "work"))
        ring = ps("ring", [P, RING, 512])
        ps_scores = ps("ps_scores", [P, 2, QUAD, P])
        ps_mixed = ps("ps_mixed", [P, QUAD, P])
        ps_mixed_tail = ps("ps_mixed_tail", [P, QUAD, P])

        QK_SLOTS = 2 * QKV // P
        OUTS = 4
        SLOTS_OF = {"V": 1, "T": 1, "X": 2, "Q": 1}
        HIS_OF = {"T": 1, "X": 2, "Q": 1}
        WAY_IN = "N0 N1 N2 N3 N4 N5 X0 V0 V1 V2 " + " ".join(f"Q{i}" for i in range(QK_SLOTS)).replace("Q11", "Q11 Z11")
        TURN = """S0 B0 +N0 +N1 S1 +N2 I0 V3 +N3 +N4 V4 +N5 I1 S2 V5 +X0 S3 T0 +Q0 I2 I3 +Q1 T1 +Q2 M0 R0 +Q3 +Q4 +Q5 +Q6 M1 R1 B1
                  +Q7 +Q8 +Q9 T2 +Q10 +Q11 +Z11 O0 +Q12 O1 +Q13 +V0 O2 T3 O3 M2 R2 +V1 +Q14 +Q15 +Q16 F0 M3 R3 +V2 +Q17 +Q18 O4
                  +Q19 +Q20 O5 +Q21 +Q22 +Q23 O6 O7 F1"""
        plan = lambda steps, more=True, first=(0, 0): plan_of(steps, SLOTS_OF, HIS_OF, {"M": "T", "V": "X", "Q": "X", "Z": "Q"}, more, first)
        SLOTS_BEFORE = 2 + QK_SLOTS + VCUTS
        HIS_BEFORE = 2 + QK_SLOTS
        _, SLOTS, HIS = plan(TURN)
        assert SLOTS % RING == 0
        bank = lambda slot: (slot + SLOTS_BEFORE) % RING
        ring_filled = Signal(sem("ring_filled"), SLOTS, SLOTS_BEFORE)
        ring_hi = Signal(sem("ring_hi"), HIS, HIS_BEFORE)
        ring_free = Signal(sem("ring_free"), SLOTS, SLOTS_BEFORE, lent=RING)
        x_loaded = Signal(sem("x_loaded"), 1, 1, step=16)
        xn_ready = Signal(sem("xn_ready"), 1, 1)
        TWIN_STEPS = 4
        twin_step = Signal(sem("k_twin_step"), TWIN_STEPS, TWIN_STEPS)
        scored = Signal(sem("scored"), QUADS)
        max_ready = Signal(sem("max_ready"), QUADS)
        exps_ready = Signal(sem("exps_ready"), QUADS, lent=2)
        inverse_ready = Signal(sem("inverse_ready"), QUADS)
        probs_ready = Signal(sem("probs_ready"), QUADS)
        mixed = Signal(sem("mixed"), QUADS, lent=2)
        mixed_hi = Signal(sem("mixed_hi"), QUADS)
        mixed_lo = Signal(sem("mixed_lo"), QUADS, lent=1)
        out_filled = Signal(sem("out_filled"), UNIT, lent=1)
        out_added = Signal(sem("out_added"), UNIT)
        out_read = Signal(sem("out_read"), UNIT, lent=UNIT)
        v_sent = Signal(sem("v_sent"), UNIT, 1, lent=1, step=16)
        v_rows_loaded = Signal(sem("v_rows_loaded"), UNIT, 1, step=16 * CHUNKS)
        v_hi_ready = Signal(sem("v_hi_ready"), UNIT)
        v_ready = Signal(sem("v_ready"), UNIT)
        residual_loaded = Signal(sem("residual_loaded"), 1, step=16)
        residual_biased = Signal(sem("residual_biased"), 1)
        h1_stored = [Signal(sem(f"h1_stored{b}"), 1, lent=1, step=16) for b in range(UNIT)]
        biases_loaded = sem("biases_loaded")
        dve_step = Signal(sem("dve_step"), NORM_STEPS, NORM_STEPS)
        block = ctx.enter_context(nc.Block())

        rows = lambda turn: bass.ds(turn * UT, UT)
        last_v = lambda i, more: [slot for kind, n, slot, _, _ in plan(TURN, more)[0] if (kind, n) == ("V", i)][0]

        def turns(engine, do, ahead=None):
            walk(0, plan(WAY_IN, first=(-SLOTS_BEFORE, -HIS_BEFORE))[0], do)
            with engine.Fori(0, UNITS - 1) as turn:
                if ahead:
                    ahead(turn)
                walk(turn, plan(TURN)[0], do)
            walk(UNITS - 1, plan(TURN, False)[0], do)

        @block.sync
        def _(sp):
            def move_v(turn, event, slot):
                there = dram["v"][event % 2]
                sp.wait_ge(ring_free.sem, ring_free.at(turn, slot))
                sp.dma_start(there, v_flat[:, :]).then_inc(v_sent.sem, 16)
                sp.wait_ge(v_sent.sem, v_sent.at(turn, event))
                apart(sp, keep["passed"])
                if event >= 0:
                    sp.wait_ge(v_ready.sem, v_ready.at(turn, event))
                back = there.rearrange("(g t) (c d) -> c t g d", t=GROUP, c=CHUNKS)
                for c in range(CHUNKS):
                    sp.dma_start(v_rows[c * GROUP:(c + 1) * GROUP, :, :], back[c]).then_inc(v_rows_loaded.sem, 16)

            def store(turn, b):
                sp.wait_ge(out_read.sem, out_read.at(turn, b))
                sp.dma_start(dram["h1"][bass.ds(turn * UT + b * P, P), :], h1[:, b, :]).then_inc(h1_stored[b].sem, 16)

            def body(turn, more):
                sp.wait_ge(out_read.sem, out_read.at(turn, -1))
                sp.dma_start(residual[:, :, :], dram["h0"][rows(turn), :].rearrange("(b p) d -> p b d", p=P)).then_inc(residual_loaded.sem, 16)
                move_v(turn, 0, last_v(2 * VCUTS - 1, more))
                store(turn, 0)
                if more:
                    move_v(turn, 1, last_v(VCUTS - 1, more))
                store(turn, 1)

            sp.wait_ge(keep["h0_stored"][1], 16)
            move_v(0, -1, -1 - QK_SLOTS)
            with sp.Fori(0, UNITS - 1) as turn:
                body(turn, True)
            body(UNITS - 1, False)
            for b in range(UNIT):
                sp.wait_ge(h1_stored[b].sem, h1_stored[b].at(UNITS - 1, 0))

        @block.gpsimd
        def _(pool):
            def twins(turn, _, slot, hi, source):
                steps = Steps(pool, twin_step, turn, event_of(slot) * TWIN_STEPS)
                if event_of(slot) == 0:
                    pool.wait_ge(v_ready.sem, v_ready.at(turn, UNIT - 1))
                pool.wait_ge(ring_free.sem, ring_free.at(turn, source))
                apart(pool, keep["passed"])
                for k_twin in (k_twin_hi, k_twin_lo):
                    for odd in range(2):
                        chunks = lambda half: k_twin[half * TAIL:(half + 1) * TAIL, :, :].rearrange(
                            "p g (c o t) -> p g c o t", o=2, t=GROUP)[:, :, :, odd, :]
                        if steps.count % TWIN_STEPS:
                            steps.settle()
                            apart(pool, keep["passed"])
                        steps.then(nc.gpsimd.tensor_scalar(chunks(1 - odd), raw(chunks(odd)), 1.0, 1.0, ALU.mult, ALU.mult), settle=False)

            def normalise(turn, n, slot, hi, source):
                pool.wait_ge(inverse_ready.sem, inverse_ready.at(turn, n))
                apart(pool, keep["passed"])
                for j in range(QUAD):
                    last = nc.gpsimd.tensor_scalar(probs[:, n, j, :], probs[:, n, j, :], inverse[:, n, j:j + 1],
                                                   float(D) ** -0.5, ALU.mult, ALU.mult)
                last.then_inc(probs_ready.sem, 1)

            def split_v(turn, b, slot, hi, source):
                if b == 0:
                    pool.wait_ge(twin_step.sem, twin_step.at(turn, -1))
                pool.wait_ge(v_rows_loaded.sem, v_rows_loaded.at(turn, b - 1))
                pool.wait_ge(mixed.sem, mixed.at(turn, b * (QUADS // UNIT) - 1))
                apart(pool, keep["passed"])
                nc.gpsimd.tensor_scalar(v_hi[:, :, :], v_rows[:, :, :], 1.0, 1.0, ALU.mult, ALU.mult).then_inc(v_hi_ready.sem, 1)
                pool.wait_ge(v_hi_ready.sem, v_hi_ready.at(turn, b))
                nc.gpsimd.tensor_tensor(v_lo[:, :, :], v_rows[:, :, :], raw(v_hi[:, :, :]), ALU.subtract).then_inc(v_ready.sem, 1)

            turns(pool, {"B": split_v, "I": normalise, "Z": twins})

        out_of = lambda b: ps_scores[:, b, :, :].rearrange("p j k -> p (j k)")[:, 0:2 * D]

        @block.tensor
        def _(pe):
            def slot_free(turn, slot):
                pe.wait_ge(ring_free.sem, ring_free.at(turn, slot - RING))

            def transposes(turn, _, slot, hi, source):
                pe.wait_ge(xn_ready.sem, xn_ready.at(turn, event_of(slot)))
                for part in range(2):
                    slot_free(turn, slot + part)
                    for b in range(UNIT):
                        last = nc.tensor.transpose(ring[:, bank(slot + part), b * P:(b + 1) * P], xn[:, b, part * P:(part + 1) * P], keep["ident"][:, :])
                    last.then_inc(ring_filled.sem, 1)

            def project_qk(turn, i, slot, hi, source):
                is_k, s = i < QK_SLOTS // 2, i % (QK_SLOTS // 2)
                w_hi, w_lo, w_stack = w_k if is_k else w_q
                cols = slice(s * P, (s + 1) * P)
                if i == 0:
                    pe.wait_ge(ring_free.sem, ring_free.at(turn, source))
                slot_free(turn, slot)
                passes = ((w_hi, xt_hi), (w_hi, xt_lo), (w_lo, xt_hi), (w_stack, xt_twin_hi), (w_stack, xt_twin_lo))
                for k, (w, x) in enumerate(passes):
                    last = nc.tensor.matmul(ring[:, bank(slot), 0:UT], w[:, cols], x[:, :], start=k == 0, stop=k == 4)
                last.then_inc(ring_filled.sem, 1)

            def project_v(turn, i, slot, hi, source):
                w_hi, w_lo, w_stack = w_v
                b, s = divmod(i, VCUTS)
                tile, cols = slice(b * P, (b + 1) * P), slice(s * VCUT, (s + 1) * VCUT)
                if i == 0:
                    pe.wait_ge(ring_free.sem, ring_free.at(turn, source))
                slot_free(turn, slot)
                passes = ((xt_hi, w_hi), (xt_lo, w_hi), (xt_hi, w_lo), (xt_twin_hi, w_stack), (xt_twin_lo, w_stack))
                for k, (x, w) in enumerate(passes):
                    last = nc.tensor.matmul(ring[:, bank(slot), :], x[:, tile], w[:, cols], start=k == 0, stop=k == 4)
                last.then_inc(ring_filled.sem, 1)

            def scores(turn, n, slot, hi, source):
                if n == 0:
                    pe.wait_ge(twin_step.sem, twin_step.at(turn, -1))
                    pe.wait_ge(ring_free.sem, ring_free.at(turn, -1))
                if n < UNIT:
                    pe.wait_ge(out_read.sem, out_read.at(turn, n - UNIT))
                pe.wait_ge(exps_ready.sem, exps_ready.at(turn, n - 2))
                for j in range(QUAD):
                    g = n * QUAD + j
                    passes = ((q_hi, k_hi), (q_lo, k_hi), (q_hi, k_lo), (q_stack, k_twin_hi), (q_stack, k_twin_lo))
                    for i, (q, k) in enumerate(passes):
                        last = nc.tensor.matmul(ps_scores[:, n % 2, j, :], q[:, g, :], k[:, g, :], start=i == 0, stop=i == 4)
                last.then_inc(scored.sem, 1)

            def turn_probs(turn, n, slot, hi, source):
                pe.wait_ge(probs_ready.sem, probs_ready.at(turn, n))
                slot_free(turn, slot)
                for j in range(QUAD):
                    last = nc.tensor.transpose(ring[:, bank(slot), j * P:(j + 1) * P], probs[:, n, j, :], keep["ident"][:, :])
                last.then_inc(ring_filled.sem, 1)

            def mix(turn, n, slot, hi, source):
                b = n // (QUADS // UNIT)
                pe.wait_ge(v_ready.sem, v_ready.at(turn, b))
                pe.wait_ge(ring_free.sem, ring_free.at(turn, source))
                pe.wait_ge(mixed_lo.sem, mixed_lo.at(turn, n - 1))
                for cols, out in ((slice(0, MAIN), ps_mixed), (slice(MAIN, D), ps_mixed_tail)):
                    for j in range(QUAD):
                        g = n * QUAD + j - b * GROUPS
                        passes = ((v_hi, pt_hi), (v_lo, pt_hi), (v_hi, pt_lo))
                        for i, (v, p) in enumerate(passes):
                            last = nc.tensor.matmul(out[0:cols.stop - cols.start, j, :], v[:, g, cols], p[:, n % 2, j, :], start=i == 0, stop=i == 2)
                last.then_inc(mixed.sem, 1)

            def project_out(turn, i, slot, hi, source):
                b, part = divmod(i, OUTS)
                if part == 0:
                    pe.wait_ge(mixed_lo.sem, mixed_lo.at(turn, (b + 1) * (QUADS // UNIT) - 1))
                    pe.wait_ge(exps_ready.sem, exps_ready.at(turn, QUADS - UNIT + b))
                for c in range(part * CHUNKS // OUTS, (part + 1) * CHUNKS // OUTS):
                    done = c == CHUNKS - 1
                    nc.tensor.matmul(out_of(b), o_hi[:, c, :], w_out[:, c, :, :], start=c == 0, stop=False)
                    nc.tensor.matmul(out_of(b)[:, 0:D], o_lo[:, c, :], w_out[:, c, 0, :], start=False, stop=False)
                    last = nc.tensor.matmul(out_of(b), o_stack[:, c, :], w_out_twin[:, c, :, :], start=False, stop=done)
                if part == OUTS - 1:
                    last.then_inc(out_filled.sem, 1)

            turns(pe, {"S": scores, "V": project_v, "X": transposes, "T": turn_probs, "Q": project_qk, "M": mix, "O": project_out})

        def qk_place(i):
            is_k, s = i < QK_SLOTS // 2, i % (QK_SLOTS // 2)
            bias = b_qk[:, s + is_k * QK_SLOTS // 2:s + is_k * QK_SLOTS // 2 + 1]
            return is_k, s if s < CHUNKS else None, 2 * (s - CHUNKS), bias

        def spread(tensor, half, c):
            part = slice(0, P) if half is None else slice(half * TAIL, (half + 1) * TAIL)
            return tensor[part, :, c * GROUP:(c + 1) * GROUP]

        def from_ring(slot, half=None):
            part = slice(0, P) if half is None else slice(half * TAIL, (half + 1) * TAIL)
            return ring[part, bank(slot), 0:UT].rearrange("p (g t) -> p g t", t=GROUP)

        def o_place(tensor, part, n):
            at = (n % (QUADS // UNIT)) * QUAD * GROUP
            return tensor[part, :, at:at + QUAD * GROUP].rearrange("p c (j t) -> p j c t", t=GROUP)

        def from_mixed(tensor, part):
            return tensor[part, :, :].rearrange("p j (c t) -> p j c t", t=GROUP)

        @block.scalar
        def _(act):
            for signal in (ring_free, exps_ready, mixed, mixed_lo, out_filled, out_read, v_sent, *h1_stored):
                signal.lend(act)

            def load_x(turn, event, unit):
                if event == 0:
                    act.wait_ge(xn_ready.sem, xn_ready.at(turn, -1))
                act.dma_start(xin[:, :, :], dram["h0"][rows(unit), :].rearrange("(b p) d -> p b d", p=P)).then_inc(x_loaded.sem, 16)

            def split_x(turn, _, slot, hi, source):
                for part, to in enumerate((xt_hi, xt_twin_hi)):
                    act.wait_ge(ring_filled.sem, ring_filled.at(turn, slot + part))
                    nc.scalar.activation(to[:, :], ring[:, bank(slot + part), 0:UT], ACT.Copy).then_inc(ring_hi.sem, 1)

            def split_qk(turn, i, slot, hi, source):
                is_k, main, pair, bias = qk_place(i)
                act.wait_ge(ring_filled.sem, ring_filled.at(turn, slot))
                if main is not None:
                    last = nc.scalar.activation(spread(k_hi if is_k else q_hi, None, main), from_ring(slot), ACT.Identity, bias=bias)
                else:
                    for half in range(2):
                        last = nc.scalar.activation(spread(k_twin_hi if is_k else q_stack, half, pair + half), from_ring(slot, half),
                                                    ACT.Identity, bias=bias[half * TAIL:(half + 1) * TAIL, :])
                last.then_inc(ring_hi.sem, 1)

            def exps(turn, n, slot, hi, source):
                act.wait_ge(max_ready.sem, max_ready.at(turn, n))
                for j in range(QUAD):
                    last = nc.scalar.activation(probs[:, n, j, :], ps_scores[:, n % 2, j, :], ACT.Exp,
                                                bias=neg_max[:, n, j:j + 1], accum_out=sums[:, n, j:j + 1])
                last.then_inc(exps_ready.sem, 1)

            def turned_probs(turn, n, slot, hi, source):
                act.wait_ge(ring_filled.sem, ring_filled.at(turn, slot))
                act.wait_ge(mixed.sem, mixed.at(turn, n - 2))
                nc.scalar.activation(pt_hi[:, n % 2, :, :], ring[:, bank(slot), :].rearrange("p (j k) -> p j k", j=QUAD), ACT.Copy).then_inc(ring_hi.sem, 1)

            def mixed_rows(turn, n, slot, hi, source):
                b = n // (QUADS // UNIT)
                if n % (QUADS // UNIT) == 0:
                    act.wait_ge(out_filled.sem, out_filled.at(turn, b - 1))
                act.wait_ge(mixed.sem, mixed.at(turn, n))
                full, low = slice(0, P), slice(0, TAIL)
                nc.scalar.activation(o_place(o_hi, full, n), from_mixed(ps_mixed, full), ACT.Copy)
                nc.scalar.activation(o_place(o_stack, low, n), from_mixed(ps_mixed_tail, low), ACT.Copy).then_inc(mixed_hi.sem, 1)

            load_x(0, -1, 0)
            act.dma_start(b_qk[:, :], dram["b_qk"]).then_inc(biases_loaded, 16)
            act.dma_start(b_v[:, :], dram["b_v"].to_broadcast([P, QKV])).then_inc(biases_loaded, 16)
            act.dma_start(b_proj[:, :], dram["b_proj"].to_broadcast([P, D])).then_inc(biases_loaded, 16)
            act.wait_ge(keep["h0_stored"][1], 16)
            act.wait_ge(biases_loaded, 48)
            turns(act, {"S": exps, "X": split_x, "T": turned_probs, "Q": split_qk, "R": mixed_rows},
                  lambda turn: load_x(turn, 0, turn + 1))

        @block.vector
        def _(dve):
            def norm(turn, part, slot, hi, source):
                event = event_of(slot)
                steps = Steps(dve, dve_step, turn, event * NORM_STEPS + min(part, 1) * 2 + max(part - 1, 0) * 3, passed=keep["passed"])
                if part == 0:
                    dve.wait_ge(x_loaded.sem, x_loaded.at(turn, event))
                    moments_of(nc, steps, stats, moments, [xin[:, b, :] for b in range(UNIT)])
                elif part <= ROOT_PARTS:
                    inverse_root(nc, steps, part - 1, moments[:, :, 1], 1e-5, half[:, :], guess[:, :], rstd[:, :], work[:, :])
                else:
                    if event == -1:
                        dve.wait_ge(biases_loaded, 48)
                    for b in range(UNIT):
                        for to, of in ((slice(0, D), slice(0, D)), (slice(D, D + TAIL), slice(MAIN, D))):
                            last = nc.vector.tensor_scalar(xn[:, b, to], xin[:, b, of], moments[:, b, 0:1], rstd[:, b:b + 1],
                                                           ALU.subtract, ALU.mult)
                    last.then_inc(xn_ready.sem, 1)

            def split_x(turn, _, slot, hi, source):
                for part, (to, of) in enumerate(((xt_lo, xt_hi), (xt_twin_lo, xt_twin_hi))):
                    dve.wait_ge(ring_hi.sem, ring_hi.at(turn, hi + part))
                    nc.vector.tensor_tensor(to[:, :], ring[:, bank(slot + part), 0:UT], raw(of[:, :]), ALU.subtract).then_inc(ring_free.sem, 1)

            def split_qk(turn, i, slot, hi, source):
                is_k, main, pair, bias = qk_place(i)
                dve.wait_ge(ring_hi.sem, ring_hi.at(turn, hi))
                if main is not None:
                    of, to = (k_hi, k_lo) if is_k else (q_hi, q_lo)
                    last = nc.vector.scalar_tensor_tensor(out=spread(to, None, main), in0=from_ring(slot), scalar=bias,
                                                          in1=raw(spread(of, None, main)), op0=ALU.add, op1=ALU.subtract)
                else:
                    for half in range(2):
                        of = spread(k_twin_hi if is_k else q_stack, half, pair + half)
                        to = spread(k_twin_lo, half, pair + half) if is_k else spread(q_stack, 1 - half, pair + half)
                        last = nc.vector.scalar_tensor_tensor(out=to, in0=from_ring(slot, half), scalar=bias[half * TAIL:(half + 1) * TAIL, :],
                                                              in1=raw(of), op0=ALU.add, op1=ALU.subtract)
                last.then_inc(ring_free.sem, 1)

            def biased_v(turn, i, slot, hi, source):
                b, s = divmod(i, VCUTS)
                if s == 0:
                    event = (-1 if slot < 0 else 1) if b == 0 else 0
                    dve.wait_ge(v_sent.sem, v_sent.at(turn, event - 1))
                cols = slice(s * VCUT, (s + 1) * VCUT)
                dve.wait_ge(ring_filled.sem, ring_filled.at(turn, slot))
                nc.vector.tensor_tensor(v_flat[:, cols], ring[:, bank(slot), :], b_v[:, cols], ALU.add).then_inc(ring_free.sem, 1)

            def row_max(turn, n, slot, hi, source):
                dve.wait_ge(scored.sem, scored.at(turn, n))
                nc.vector.tensor_reduce(out=neg_max[:, n, :], in_=ps_scores[:, n % 2, :, :], op=ALU.max, axis=X, negate=True).then_inc(max_ready.sem, 1)

            def invert(turn, n, slot, hi, source):
                dve.wait_ge(exps_ready.sem, exps_ready.at(turn, n))
                nc.vector.reciprocal(inverse[:, n, :], sums[:, n, :]).then_inc(inverse_ready.sem, 1)

            def turned_probs(turn, n, slot, hi, source):
                dve.wait_ge(ring_hi.sem, ring_hi.at(turn, hi))
                nc.vector.tensor_tensor(pt_lo[:, n % 2, :, :], ring[:, bank(slot), :].rearrange("p (j k) -> p j k", j=QUAD), raw(pt_hi[:, n % 2, :, :]),
                                        ALU.subtract).then_inc(ring_free.sem, 1)

            def mixed_rows(turn, n, slot, hi, source):
                full, low, high = slice(0, P), slice(0, TAIL), slice(TAIL, P)
                dve.wait_ge(mixed_hi.sem, mixed_hi.at(turn, n))
                nc.vector.tensor_tensor(o_place(o_lo, full, n), from_mixed(ps_mixed, full), raw(o_place(o_hi, full, n)), ALU.subtract)
                nc.vector.tensor_tensor(o_place(o_stack, high, n), from_mixed(ps_mixed_tail, low), raw(o_place(o_stack, low, n)), ALU.subtract).then_inc(mixed_lo.sem, 1)

            def finish(turn, b, slot, hi, source):
                if b == 0:
                    dve.wait_ge(residual_loaded.sem, residual_loaded.at(turn, 0))
                    nc.vector.tensor_tensor(residual[:, :, :], residual[:, :, :], b_proj[:, :].unsqueeze(1).to_broadcast([P, UNIT, D]), ALU.add).then_inc(residual_biased.sem, 1)
                dve.wait_ge(residual_biased.sem, residual_biased.at(turn, 0))
                dve.wait_ge(h1_stored[b].sem, h1_stored[b].at(turn, -1))
                dve.wait_ge(out_filled.sem, out_filled.at(turn, b))
                nc.vector.tensor_tensor(h1[:, b, :], out_of(b)[:, 0:D], residual[:, b, :], ALU.add).then_inc(out_added.sem, 1)
                dve.wait_ge(out_added.sem, out_added.at(turn, b))
                nc.vector.tensor_tensor(h1[:, b, :], out_of(b)[:, D:2 * D], h1[:, b, :], ALU.add).then_inc(out_read.sem, 1)

            turns(dve, {"N": norm, "S": row_max, "I": invert, "V": biased_v, "X": split_x, "T": turned_probs, "Q": split_qk,
                        "R": mixed_rows, "F": finish})


def mixer(nc, keep, dram):
    UNIT = 4
    UNITS = TILES // UNIT
    UT = UNIT * P
    RING = 4
    SETS = HEADS // QUAD
    HALVES = 2 * UNIT
    PER_HALF = QUAD // 2
    PIECE = SETS * 2 * HD
    VV = 2 * HD
    with ExitStack() as ctx:
        sb = lambda name, shape, dt=F32: ctx.enter_context(nc.sbuf_tensor(f"mix_{name}", shape, dt))
        ps = lambda name, shape: ctx.enter_context(nc.psum_tensor(f"mix_{name}", shape, F32))
        sem = lambda name: ctx.enter_context(nc.semaphore(f"mix_{name}"))
        QK = 2 * SETS * P
        W_IN = QK + D
        raw_in = sb("raw_in", [P, 2, W_IN + D])
        w_hi, w_lo, w_half, w_stack = (sb(f"w_{n}", [P, W_IN + D], F32R) for n in ("hi", "lo", "half", "stack"))
        b_qk = sb("b_qk", [P, 2 * SETS])
        b_low = sb("b_low", [P, 2 * SETS])
        b_v, b_out, gain, shift = (sb(n, [P, D]) for n in ("b_v", "b_out", "gain", "shift"))
        low_rows = sb("low_rows", [P, 1])
        lane = sb("lane", [P, 1], I32)
        hin = sb("hin", [P, UNIT, D])
        y = sb("y", [P, UNIT, D])
        residual = sb("residual", [P, UNIT, D])
        zn = sb("zn", [P, UNIT, MAIN + 2 * TAIL])
        zt_hi, zt_lo = (sb(n, [P, 2, UT], F32R) for n in ("zt_hi", "zt_lo"))
        q_low, q_stack, k_hi, k_lo = (sb(n, [P, SETS, UT], F32R) for n in ("q_low", "q_stack", "k_hi", "k_lo"))
        v_sum = sb("v_sum", [P, UNIT, D])
        vv = sb("vv", [P, UNIT, QUAD, SETS, VV], F32R)
        mixed = sb("mixed", [PIECE, QUAD, P])
        probs = sb("probs", [P, 2, PER_HALF, SETS, P])
        pt_hi, pt_lo = (sb(n, [P, 2 * PER_HALF, SETS, P], F32R) for n in ("pt_hi", "pt_lo"))
        context = sb("context", [P, 2, MAIN + 2 * TAIL])
        ct_hi, ct_lo = (sb(n, [P, 2, P], F32R) for n in ("ct_hi", "ct_lo"))
        x2 = sb("x2", [P, 2, D])
        top, neg_max, sums = (sb(n, [P, 2, PER_HALF, SETS]) for n in ("top", "neg_max", "sums"))
        inverse = sb("inverse", [P, 2, QUAD, SETS])
        stats = sb("stats", [P, UNIT, 6])
        moments = sb("moments", [P, UNIT, 2])
        half, guess, rstd, work = (sb(n, [P, UNIT]) for n in ("half", "guess", "rstd", "work"))
        stage, w1_half = raw_in[:, :, 0:HID], w_half[:, 0:HID]
        stage2 = sb("stage2", [P, HC, D])
        ps_scores = ps("ps_scores", [P, QUAD, 512])
        ring = ps("ring", [P, RING, 512])

        QK_SLOTS = 2 * SETS
        SLOTS_OF = {"V": 1, "T": PER_HALF, "A": PER_HALF, "G": 1, "FT": 1, "FO": 1, "X": 2, "Q": 1}
        HIS_OF = {"T": PER_HALF, "FT": 1, "X": 2, "Q": 1}
        WAY_IN = "L0 " + " ".join(f"N{i}" for i in range(12)) + " B0 N12 N13 X0 Q0 Q1 Q2 Q3 Q4 Q5"
        TURN = """S0 E0 S1 E1 V0 V1 V2 V3 W0 W1 W2 W3 S2 T0 +N0 E2 S3 T1 +N1 A0 +N2 D0 E3 S4 T2 +N3 A1 D1 E4 S5 +N4 G1 C1 T3 +N5 A2 D2 E5
                  S6 FT0 +N6 T4 A3 +N7 D3 E6 FO0 S7 G3 +N8 C3 T5 +N9 A4 D4 E7 FT1 +N10 T6 A5 D5 FO1 +N11 G5 +N12 C5 T7 A6 D6 +N13
                  FT2 +X0 +Q0 A7 D7 FO2 +Q1 G7 C7 +Q2 +Q3 FT3 +Q4 FO3 +Q5"""
        plan = lambda steps, more=True, first=(0, 0): plan_of(steps, SLOTS_OF, HIS_OF, {"A": "T", "D": "A", "G": "A", "C": "G", "FO": "FT", "Q": "X"}, more, first)
        SLOTS_BEFORE = 2 + QK_SLOTS
        _, SLOTS, HIS = plan(TURN)
        assert SLOTS % RING == 0
        bank = lambda slot: (slot + SLOTS_BEFORE) % RING
        out_slots = {more: [slot for kind, _, slot, _, _ in plan(TURN, more)[0] if kind == "FO"] for more in (True, False)}
        ring_filled = Signal(sem("ring_filled"), SLOTS, SLOTS_BEFORE)
        ring_hi = Signal(sem("ring_hi"), HIS, SLOTS_BEFORE)
        ring_free = Signal(sem("ring_free"), SLOTS, SLOTS_BEFORE, lent=RING)
        h_loaded = Signal(sem("h_loaded"), 1, 1, step=16)
        zn_ready = Signal(sem("zn_ready"), 1, 1)
        v_hi_ready = Signal(sem("v_hi_ready"), UNIT)
        vv_ready = Signal(sem("vv_ready"), UNIT)
        scored = Signal(sem("scored"), HALVES)
        max_ready = Signal(sem("max_ready"), HALVES)
        exps_ready = Signal(sem("exps_ready"), HALVES, lent=2)
        blocks_taken = Signal(sem("blocks_taken"), HALVES)
        inverse_ready = Signal(sem("inverse_ready"), HALVES, lent=2)
        context_ready = Signal(sem("context_ready"), UNIT)
        x2_stored = [Signal(sem(f"x2_stored{b}"), UNIT // 2, lent=1, step=16) for b in range(2)]
        consts_loaded, weights_ready, lane_ready, raw_loaded = sem("consts_loaded"), sem("weights_ready"), sem("lane_ready"), sem("raw_loaded")
        weight_hi = sem("weight_hi")
        residual_ready = Signal(sem("residual_ready"), 1, 1)
        dve_setup = Signal(sem("dve_setup"), 0)
        NORM = 2 * NORM_STEPS + 4
        dve_norm = Signal(sem("dve_norm"), NORM, NORM)
        dve_max = Signal(sem("dve_max"), HALVES)
        dve_context = Signal(sem("dve_context"), UNIT)
        pool_step = Signal(sem("pool_step"), 0)
        stage_loaded = sem("stage_loaded")
        block = ctx.enter_context(nc.Block())

        def turns(engine, do, following=None):
            walk(0, plan(WAY_IN, first=(-SLOTS_BEFORE, -SLOTS_BEFORE))[0], do)
            if following:
                following(0, -1)
            with engine.Fori(0, UNITS - 1) as turn:
                walk(turn, plan(TURN)[0], do)
                if following:
                    following(turn, 0)
            walk(UNITS - 1, plan(TURN, False)[0], do)

        of_heads = lambda v: v.rearrange("p j s d -> p (j s) d")

        @block.sync
        def _(sp):
            def load(turn, event, unit):
                if event == 0:
                    sp.wait_ge(zn_ready.sem, zn_ready.at(turn, -1))
                sp.dma_start(hin[:, :, :], dram["h1"][bass.ds(unit * UT, UT), :].rearrange("(b p) d -> p b d", p=P)).then_inc(h_loaded.sem, 16)

            def store(turn, more, b):
                sp.wait_ge(ring_free.sem, ring_free.at(turn, out_slots[more][b]))
                sp.dma_start(dram["x2"][bass.ds(turn * UT + b * P, P), :], x2[:, b % 2, :]).then_inc(x2_stored[b % 2].sem, 16)

            def body(turn, more):
                if more:
                    load(turn, 0, turn + 1)
                for b in range(UNIT):
                    store(turn, more, b)

            load(0, -1, 0)
            for part, (to, of) in enumerate(((slice(0, P), slice(0, MAIN)), (slice(0, TAIL), slice(MAIN, D)), (slice(TAIL, P), slice(MAIN, D)))):
                sp.dma_start(raw_in[to, min(part, 1), :], dram["w_mix"][of, :]).then_inc(raw_loaded, 16)
            with sp.Fori(0, UNITS - 1) as turn:
                body(turn, True)
            body(UNITS - 1, False)
            for b in range(2):
                sp.wait_ge(x2_stored[b].sem, x2_stored[b].at(UNITS - 1, UNIT // 2 - 1))

        @block.gpsimd
        def _(pool):
            nc.gpsimd.iota(lane[:, :], pattern=[[0, 1]], base=0, channel_multiplier=1).then_inc(lane_ready, 1)
            pool.wait_ge(weight_hi, 1)
            nc.gpsimd.tensor_tensor(w_lo[:, :], raw_in[:, 0, :], raw(w_hi[:, :]), ALU.subtract)
            nc.gpsimd.tensor_tensor(w_stack[:, :], raw_in[:, 1, :], raw(w_half[:, :]), ALU.subtract).then_inc(weights_ready, 1)
            steps = Steps(pool, pool_step, 0)
            pool.wait_ge(weights_ready, 1)
            for f in range(FFNS):
                w1_hi, w1_lo, w1_stack, w2 = keep["ffn"][f]
                w2_hi, w2_lo = w2[:, :, 0, :], w2[:, :, 1, :]
                for half_rows in range(2):
                    pool.dma_start(stage[half_rows * TAIL:(half_rows + 1) * TAIL, 1, :], dram["w1"][f, MAIN:D, :]).then_inc(stage_loaded, 16)
                pool.dma_start(stage[:, 0, :], dram["w1"][f, 0:MAIN, :]).then_inc(stage_loaded, 16)
                pool.dma_start(stage2[:, :, :], dram["w2"][f].rearrange("(c p) n -> p c n", p=P)).then_inc(stage_loaded, 16)
                pool.wait_ge(stage_loaded, 64 * (f + 1))
                main, tail = stage[:, 0, :], stage[:, 1, :]
                nc.gpsimd.tensor_scalar(w1_hi[:, :], main, 1.0, 1.0, ALU.mult, ALU.mult)
                nc.gpsimd.tensor_scalar(w2_hi, stage2[:, :, :], 1.0, 1.0, ALU.mult, ALU.mult)
                steps.then(nc.gpsimd.tensor_scalar(w1_half, tail, keep["low_rows"][:, 0:1], 1.0, ALU.mult, ALU.mult))
                nc.gpsimd.tensor_tensor(w1_lo[:, :], main, raw(w1_hi[:, :]), ALU.subtract)
                nc.gpsimd.tensor_tensor(w2_lo, stage2[:, :, :], raw(w2_hi), ALU.subtract)
                steps.then(nc.gpsimd.tensor_tensor(w1_stack[:, :], tail, raw(w1_half), ALU.subtract))

        @block.tensor
        def _(pe):
            def slot_free(turn, slot, source=None):
                needed = slot - RING if source is None else max(source, slot - RING)
                pe.wait_ge(ring_free.sem, ring_free.at(turn, needed))

            def scores(turn, n, slot, hi, source):
                b, half = divmod(n, 2)
                if n == 0:
                    pe.wait_ge(ring_free.sem, ring_free.at(turn, -1))
                pe.wait_ge(exps_ready.sem, exps_ready.at(turn, n - 2))
                tile = slice(b * P, (b + 1) * P)
                for s in range(SETS):
                    for i, k in enumerate((k_hi, k_lo)):
                        for j in range(PER_HALF * half, PER_HALF * (half + 1)):
                            rows = slice(32 * j, 32 * j + 32)
                            last = nc.tensor.matmul(ps_scores[:, j, s * P:(s + 1) * P], q_stack[rows, s, tile], k[rows, s, tile], start=i == 0, stop=i == 1)
                last.then_inc(scored.sem, 1)

            def turned(turn, n, slot, hi, source):
                pe.wait_ge(exps_ready.sem, exps_ready.at(turn, n))
                for j in range(PER_HALF):
                    slot_free(turn, slot + j)
                    for s in range(SETS):
                        last = nc.tensor.transpose(ring[:, bank(slot + j), s * P:(s + 1) * P], probs[:, n % 2, j, s, :], keep["ident"][:, :])
                    last.then_inc(ring_filled.sem, 1)

            def mix(turn, n, slot, hi, source):
                b, half = divmod(n, 2)
                if half == 0:
                    pe.wait_ge(vv_ready.sem, vv_ready.at(turn, b))
                for j in range(PER_HALF):
                    slot_free(turn, slot + j, source)
                    piece = PER_HALF * half + j
                    v = vv[:, b, piece, :, :].rearrange("p s d -> p (s d)")
                    for i, p in enumerate((pt_hi, pt_lo)):
                        last = nc.tensor.matmul(ring[0:PIECE, bank(slot + j), 0:SETS * P], v, p[:, piece, :, :].rearrange("p s k -> p (s k)"), start=i == 0, stop=i == 1)
                    last.then_inc(ring_filled.sem, 1)

            def turn_back(turn, n, slot, hi, source):
                slot_free(turn, slot, source)
                for j in range(QUAD):
                    last = nc.tensor.transpose(ring[:, bank(slot), j * PIECE:(j + 1) * PIECE], mixed[:, j, :], keep["ident"][0:PIECE, 0:PIECE])
                last.then_inc(ring_filled.sem, 1)

            def turn_context(turn, b, slot, hi, source):
                pe.wait_ge(context_ready.sem, context_ready.at(turn, b))
                slot_free(turn, slot)
                for part in range(2):
                    last = nc.tensor.transpose(ring[:, bank(slot), part * P:(part + 1) * P], context[:, b % 2, part * P:(part + 1) * P], keep["ident"][:, :])
                last.then_inc(ring_filled.sem, 1)

            def project_out(turn, b, slot, hi, source):
                slot_free(turn, slot, source)
                out = slice(W_IN, W_IN + D)
                passes = ((ct_hi[:, 0, :], w_hi), (ct_lo[:, 0, :], w_hi), (ct_hi[:, 0, :], w_lo), (ct_hi[:, 1, :], w_stack), (ct_lo[:, 1, :], w_stack))
                for i, (c, w) in enumerate(passes):
                    last = nc.tensor.matmul(ring[:, bank(slot), 0:D], c, w[:, out], start=i == 0, stop=i == 4)
                last.then_inc(ring_filled.sem, 1)

            def transposes(turn, _, slot, hi, source):
                pe.wait_ge(zn_ready.sem, zn_ready.at(turn, event_of(slot)))
                for part in range(2):
                    slot_free(turn, slot + part)
                    for b in range(UNIT):
                        last = nc.tensor.transpose(ring[:, bank(slot + part), b * P:(b + 1) * P], zn[:, b, part * P:(part + 1) * P], keep["ident"][:, :])
                    last.then_inc(ring_filled.sem, 1)

            def project_qk(turn, s, slot, hi, source):
                if s == 0:
                    pe.wait_ge(weights_ready, 1)
                slot_free(turn, slot, source)
                cols = slice(s * P, (s + 1) * P)
                passes = ((w_hi, zt_hi, 0), (w_hi, zt_lo, 0), (w_lo, zt_hi, 0), (w_stack, zt_hi, 1), (w_stack, zt_lo, 1))
                for i, (w, z, part) in enumerate(passes):
                    last = nc.tensor.matmul(ring[:, bank(slot), :], w[:, cols], z[:, part, :], start=i == 0, stop=i == 4)
                last.then_inc(ring_filled.sem, 1)

            def project_v(turn, b, slot, hi, source):
                slot_free(turn, slot)
                tile = slice(b * P, (b + 1) * P)
                passes = ((w_hi, zt_hi, 0), (w_hi, zt_lo, 0), (w_lo, zt_hi, 0), (w_stack, zt_hi, 1), (w_stack, zt_lo, 1))
                for i, (w, z, part) in enumerate(passes):
                    last = nc.tensor.matmul(ring[:, bank(slot), 0:D], z[:, part, tile], w[:, QK:W_IN], start=i == 0, stop=i == 4)
                last.then_inc(ring_filled.sem, 1)

            turns(pe, {"S": scores, "V": project_v, "T": turned, "A": mix, "G": turn_back, "FT": turn_context, "FO": project_out, "X": transposes, "Q": project_qk})

        @block.scalar
        def _(act):
            act.dma_start(b_qk[:, :], dram["b_mix_qk"]).then_inc(consts_loaded, 16)
            for to, of in ((b_v, "b_mix_v"), (b_out, "b_mix_out"), (gain, "ln1_g"), (shift, "ln1_b")):
                act.dma_start(to[:, :], dram[of].to_broadcast([P, D])).then_inc(consts_loaded, 16)
            for signal in (ring_free, exps_ready, inverse_ready, *x2_stored):
                signal.lend(act)

            def weights(turn, *_):
                act.wait_ge(raw_loaded, 48)
                nc.scalar.activation(w_hi[:, :], raw_in[:, 0, :], ACT.Copy)
                nc.scalar.activation(w_half[:, :], raw_in[:, 1, :], ACT.Copy, scale=keep["low_rows"][:, 0:1]).then_inc(weight_hi, 1)

            def take_blocks(turn, n, slot, hi, source):
                first = source - PER_HALF + 1
                act.wait_ge(ring_filled.sem, ring_filled.at(turn, first))
                for s in range(SETS):
                    rows, queries = slice(s * VV, (s + 1) * VV), slice(s * P, (s + 1) * P)
                    last = nc.scalar.activation(mixed[rows, PER_HALF * (n % 2), :], ring[rows, bank(first), queries], ACT.Copy)
                last.then_inc(blocks_taken.sem, 1)

            def exps(turn, n, slot, hi, source):
                act.wait_ge(max_ready.sem, max_ready.at(turn, n))
                act.wait_ge(inverse_ready.sem, inverse_ready.at(turn, n - 2))
                for j in range(PER_HALF):
                    for s in range(SETS):
                        last = nc.scalar.activation(probs[:, n % 2, j, s, :], ps_scores[:, PER_HALF * (n % 2) + j, s * P:(s + 1) * P], ACT.Exp,
                                                    bias=neg_max[:, n % 2, j, s:s + 1], scale=float(HD) ** -0.5, accum_out=sums[:, n % 2, j, s:s + 1])
                last.then_inc(exps_ready.sem, 1)

            def take_hi(to, slot, of=lambda bank: bank[:, :]):
                act.wait_ge(ring_filled.sem, ring_filled.at(slot[0], slot[1]))
                nc.scalar.activation(to, of(ring[:, bank(slot[1]), :]), ACT.Copy).then_inc(ring_hi.sem, 1)

            def turned(turn, n, slot, hi, source):
                for j in range(PER_HALF):
                    take_hi(pt_hi[:, PER_HALF * (n % 2) + j, :, :], (turn, slot + j), lambda bank: bank[:, 0:SETS * P].rearrange("p (s k) -> p s k", k=P))

            def turn_context(turn, b, slot, hi, source):
                take_hi(ct_hi[:, :, :], (turn, slot), lambda bank: bank[:, 0:2 * P].rearrange("p (a t) -> p a t", a=2))

            def transposes(turn, _, slot, hi, source):
                for part in range(2):
                    take_hi(zt_hi[:, part, :], (turn, slot + part))

            def project_qk(turn, s, slot, hi, source):
                act.wait_ge(ring_filled.sem, ring_filled.at(turn, slot))
                if s < SETS:
                    last = nc.scalar.activation(q_low[:, s, :], ring[:, bank(slot), :], ACT.Identity, scale=low_rows[:, 0:1], bias=b_low[:, s:s + 1])
                else:
                    last = nc.scalar.activation(k_hi[:, s - SETS, :], ring[:, bank(slot), :], ACT.Identity, bias=b_qk[:, s:s + 1])
                last.then_inc(ring_hi.sem, 1)

            def project_v(turn, b, slot, hi, source):
                act.wait_ge(ring_free.sem, ring_free.at(turn, slot))
                nc.scalar.activation(of_heads(vv[:, b])[:, :, 0:HD], v_sum[:, b, :].rearrange("p (h d) -> p h d", d=HD), ACT.Copy).then_inc(v_hi_ready.sem, 1)

            turns(act, {"L": weights, "D": take_blocks, "E": exps, "V": project_v, "T": turned, "FT": turn_context, "X": transposes, "Q": project_qk})

        @block.vector
        def _(dve):
            def setup():
                steps = Steps(dve, dve_setup, 0)
                dve.wait_ge(lane_ready, 1)
                steps.then(nc.vector.tensor_scalar(lane[:, :], lane[:, :], HD, None, ALU.bitwise_and))
                steps.then(nc.vector.tensor_scalar(low_rows[:, :], lane[:, :], 1.0 / HD, 1.0, ALU.mult, ALU.mult))

            def constants(turn, *_):
                dve.wait_ge(consts_loaded, 16 * 5)
                nc.vector.tensor_scalar(b_low[:, :], b_qk[:, :], low_rows[:, 0:1], 1.0, ALU.mult, ALU.mult)

            def norm(turn, part, slot, hi, source):
                event = event_of(slot)
                ONE = NORM_STEPS + 1
                second, k = divmod(part, ROOT_PARTS + 2)
                done = second * ONE + ((0, 2, 5, 8, 11, 14)[k] if second < 2 else k)
                steps = Steps(dve, dve_norm, turn, event * NORM + done, passed=keep["passed"])
                wide = lambda row: row[:, :].unsqueeze(1).to_broadcast([P, UNIT, D])
                if part == 0:
                    dve.wait_ge(h_loaded.sem, h_loaded.at(turn, event))
                if second == 2 and k == 0:
                    steps.then(nc.vector.tensor_tensor(zn[:, :, 0:D], zn[:, :, 0:D], wide(gain), ALU.mult))
                elif second == 2:
                    steps.then(nc.vector.tensor_tensor(zn[:, :, 0:D], zn[:, :, 0:D], wide(shift), ALU.add))
                    nc.vector.tensor_copy(zn[:, :, D:D + TAIL], zn[:, :, MAIN:D]).then_inc(zn_ready.sem, 1)
                elif k == 0:
                    moments_of(nc, steps, stats, moments, [(y if second else hin)[:, b, :] for b in range(UNIT)])
                elif k <= ROOT_PARTS:
                    inverse_root(nc, steps, k - 1, moments[:, :, 1], 1e-5, half[:, :], guess[:, :], rstd[:, :], work[:, :])
                else:
                    to, of = (zn, y) if second else (y, hin)
                    for b in range(UNIT):
                        last = nc.vector.tensor_scalar(to[:, b, 0:D], of[:, b, :], moments[:, b, 0:1], rstd[:, b:b + 1], ALU.subtract, ALU.mult)
                    steps.then(last)

            def row_max(turn, n, slot, hi, source):
                steps = Steps(dve, dve_max, turn, n)
                dve.wait_ge(scored.sem, scored.at(turn, n))
                banks = slice(PER_HALF * (n % 2), PER_HALF * (n % 2 + 1))
                steps.then(nc.vector.tensor_reduce(out=top[:, n % 2, :, :], in_=ps_scores[:, banks, 0:SETS * P].rearrange("p j (s k) -> p j s k", k=P),
                                                   op=ALU.max, axis=X, negate=True))
                nc.vector.tensor_scalar(neg_max[:, n % 2, :, :], top[:, n % 2, :, :], float(HD) ** -0.5, 1.0, ALU.mult, ALU.mult).then_inc(max_ready.sem, 1)

            def turned(turn, n, slot, hi, source):
                b, half = divmod(n, 2)
                mine = slice(PER_HALF * half, PER_HALF * (half + 1))
                dve.wait_ge(exps_ready.sem, exps_ready.at(turn, n))
                nc.vector.reciprocal(inverse[:, b % 2, mine, :], sums[:, n % 2, :, :]).then_inc(inverse_ready.sem, 1)
                for j in range(PER_HALF):
                    piece = PER_HALF * half + j
                    dve.wait_ge(ring_hi.sem, ring_hi.at(turn, hi + j))
                    nc.vector.tensor_tensor(pt_lo[:, piece, :, :], ring[:, bank(slot + j), 0:SETS * P].rearrange("p (s k) -> p s k", k=P),
                                            raw(pt_hi[:, piece, :, :]), ALU.subtract).then_inc(ring_free.sem, 1)

            def take_blocks(turn, n, slot, hi, source):
                dve.wait_ge(blocks_taken.sem, blocks_taken.at(turn, n))
                dve.wait_ge(ring_filled.sem, ring_filled.at(turn, source))
                for s in range(SETS):
                    rows, queries = slice(s * VV, (s + 1) * VV), slice(s * P, (s + 1) * P)
                    last = nc.vector.tensor_copy(mixed[rows, PER_HALF * (n % 2) + 1, :], ring[rows, bank(source), queries])
                    if s in (0, SETS - 1):
                        last.then_inc(ring_free.sem, 1)

            def contexts(turn, n, slot, hi, source):
                b = n // 2
                steps = Steps(dve, dve_context, turn, b)
                own = context[:, b % 2, 0:D]
                dve.wait_ge(ring_filled.sem, ring_filled.at(turn, source))
                nc.vector.tensor_reduce(out=own, in_=ring[:, bank(source), 0:HEADS * VV].rearrange("p (h a d) -> p h d a", a=2, d=HD),
                                        op=ALU.add, axis=X).then_inc(ring_free.sem, 1)
                dve.wait_ge(ring_free.sem, ring_free.at(turn, source))
                dve.wait_ge(inverse_ready.sem, inverse_ready.at(turn, n))
                by_head = own.rearrange("p (h d) -> p h d", d=HD)
                of_head = inverse[:, b % 2, :, :].rearrange("p j s -> p (j s)")
                steps.then(nc.vector.tensor_tensor(by_head, by_head, of_head.unsqueeze(2).to_broadcast([P, HEADS, HD]), ALU.mult))
                nc.vector.tensor_copy(context[:, b % 2, D:D + TAIL], context[:, b % 2, MAIN:D]).then_inc(context_ready.sem, 1)

            def turn_context(turn, b, slot, hi, source):
                dve.wait_ge(ring_hi.sem, ring_hi.at(turn, hi))
                nc.vector.tensor_tensor(ct_lo[:, :, :], ring[:, bank(slot), 0:2 * P].rearrange("p (a t) -> p a t", a=2), raw(ct_hi[:, :, :]), ALU.subtract).then_inc(ring_free.sem, 1)

            def add_out(turn, b, slot, hi, source):
                if b == 0:
                    dve.wait_ge(residual_ready.sem, residual_ready.at(turn, -1))
                dve.wait_ge(x2_stored[b % 2].sem, x2_stored[b % 2].at(turn, b // 2 - 1))
                dve.wait_ge(ring_filled.sem, ring_filled.at(turn, slot))
                nc.vector.tensor_tensor(x2[:, b % 2, :], ring[:, bank(slot), 0:D], residual[:, b, :], ALU.add).then_inc(ring_free.sem, 1)

            def transposes(turn, _, slot, hi, source):
                for part in range(2):
                    dve.wait_ge(ring_hi.sem, ring_hi.at(turn, hi + part))
                    nc.vector.tensor_tensor(zt_lo[:, part, :], ring[:, bank(slot + part), :], raw(zt_hi[:, part, :]), ALU.subtract).then_inc(ring_free.sem, 1)

            def project_qk(turn, s, slot, hi, source):
                dve.wait_ge(ring_hi.sem, ring_hi.at(turn, hi))
                out, low = (q_stack[:, s, :], q_low[:, s, :]) if s < SETS else (k_lo[:, s - SETS, :], k_hi[:, s - SETS, :])
                nc.vector.scalar_tensor_tensor(out=out, in0=ring[:, bank(slot), :], scalar=b_qk[:, s:s + 1], in1=raw(low),
                                               op0=ALU.add, op1=ALU.subtract).then_inc(ring_free.sem, 1)

            def project_v(turn, b, slot, hi, source):
                dve.wait_ge(ring_filled.sem, ring_filled.at(turn, slot))
                nc.vector.tensor_tensor(v_sum[:, b, :], ring[:, bank(slot), 0:D], b_v[:, :], ALU.add).then_inc(ring_free.sem, 1)

            def split_v(turn, b, slot, hi, source):
                dve.wait_ge(v_hi_ready.sem, v_hi_ready.at(turn, b))
                by_head = lambda t: t.rearrange("p (h d) -> p h d", d=HD)
                nc.vector.tensor_tensor(of_heads(vv[:, b])[:, :, HD:VV], by_head(v_sum[:, b, :]), raw(of_heads(vv[:, b])[:, :, 0:HD]), ALU.subtract).then_inc(vv_ready.sem, 1)

            def add_bias(turn, event):
                if event == 0:
                    dve.wait_ge(ring_free.sem, ring_free.at(turn, SLOTS - 1))
                nc.vector.tensor_tensor(residual[:, :, :], y[:, :, :], b_out[:, :].unsqueeze(1).to_broadcast([P, UNIT, D]), ALU.add).then_inc(residual_ready.sem, 1)

            setup()
            turns(dve, {"B": constants, "D": take_blocks, "N": norm, "S": row_max, "V": project_v, "W": split_v, "T": turned, "C": contexts, "FT": turn_context, "FO": add_out,
                        "X": transposes, "Q": project_qk}, add_bias)


def experts(nc, keep, dram):
    UNIT = 4
    UNITS = TILES // UNIT
    UT = UNIT * P
    RING = 4
    with ExitStack() as ctx:
        sb = lambda name, shape, dt=F32: ctx.enter_context(nc.sbuf_tensor(f"ffn_{name}", shape, dt))
        ps = lambda name, shape: ctx.enter_context(nc.psum_tensor(f"ffn_{name}", shape, F32))
        sem = lambda name: ctx.enter_context(nc.semaphore(f"ffn_{name}"))
        b1 = sb("b1", [P, FFNS * HC])
        b2 = sb("b2", [P, FFNS, D])
        gain, shift = sb("gain", [P, D]), sb("shift", [P, D])
        raw_gate = sb("raw_gate", [P, 2, NEXP])
        g_hi, g_lo, g_half, g_stack = (sb(f"gate_{n}", [P, NEXP], F32R) for n in ("hi", "lo", "half", "stack"))
        b_gate = sb("b_gate", [P, NEXP])
        earlier = sb("earlier", [P, NEXP, NEXP])
        x2 = sb("x2", [P, UNIT, MAIN + 2 * TAIL])
        h1 = sb("h1", [P, UNIT, D])
        x3 = sb("x3", [P, UNIT, D])
        base = sb("base", [P, UNIT, D])
        xn = sb("xn", [P, UNIT, MAIN + 2 * TAIL])
        bias_sum = sb("bias_sum", [P, UNIT, D])
        bias_part = sb("bias_part", [P, UNIT, D])
        total = sb("total", [P, UNIT, D])
        xt = {kind: tuple(sb(f"{kind}_{n}", [P, 2, UT], F32R) for n in ("hi", "lo")) for kind in ("mlp", "exp")}
        gelu = sb("gelu", [P, 2, UT])
        hid_hi = sb("hid_hi", [P, 3, UT], F32R)
        hid_lo = sb("hid_lo", [P, 3, UT], F32R)
        logits_t = sb("logits_t", [NEXP, UT])
        logits = sb("logits", [P, UNIT, NEXP])
        rank4 = sb("rank4", [P, UNIT, NEXP, NEXP])
        ties = sb("ties", [P, UNIT, NEXP, NEXP])
        rank = sb("rank", [P, UNIT, NEXP])
        best = sb("best", [P, UNIT])
        chosen = sb("chosen", [P, UNIT, NEXP])
        exps = sb("exps", [P, UNIT, NEXP])
        gates = sb("gates", [P, UNIT, NEXP])
        stats = sb("stats", [P, UNIT, 6])
        moments = sb("moments", [P, UNIT, 2])
        half, guess, rstd, work = (sb(n, [P, UNIT]) for n in ("half", "guess", "rstd", "work"))
        ring = ps("ring", [P, RING, 512])
        ps_out = ps("ps_out", [P, UNIT, 512])

        LAG = 2
        chunks_of = lambda ffns: [(f, c) for f in ffns for c in range(HC)]
        CHUNKS_TURN, CHUNKS_BEFORE = FFNS * HC, HC
        assert CHUNKS_TURN % 6 == 0 and CHUNKS_BEFORE % 6 == 0
        IN, GATE = 2, 2
        SLOTS_BEFORE = IN + CHUNKS_BEFORE + IN + GATE
        SLOTS = IN + CHUNKS_TURN + IN + GATE
        assert SLOTS_BEFORE % RING == 0 and SLOTS % RING == 0
        bank = lambda slot: slot % RING
        ring_filled = Signal(sem("ring_filled"), SLOTS, SLOTS_BEFORE)
        ring_free = Signal(sem("ring_free"), SLOTS, SLOTS_BEFORE, lent=RING)
        chunk_read = Signal(sem("chunk_read"), CHUNKS_TURN, CHUNKS_BEFORE)
        inputs_hi = Signal(sem("inputs_hi"), 2 * IN, 2 * IN)
        hi_ready = Signal(sem("hi_ready"), CHUNKS_TURN, CHUNKS_BEFORE)
        lo_ready = Signal(sem("lo_ready"), CHUNKS_TURN, CHUNKS_BEFORE, lent=2)
        hid_used = Signal(sem("hid_used"), CHUNKS_TURN, CHUNKS_BEFORE, lent=3)
        out_done = Signal(sem("out_done"), FFNS * (UNIT - 1), UNIT - 1)
        out_added = Signal(sem("out_added"), FFNS * UNIT, UNIT)
        out_free = Signal(sem("out_free"), FFNS * UNIT, UNIT, lent=UNIT)
        x2_loaded = Signal(sem("x2_loaded"), 1, 1, step=2 * 16)
        h1_loaded = Signal(sem("h1_loaded"), 1, 1, step=16)
        mlp_done = Signal(sem("mlp_done"), 1, 1)
        xn_scaled = Signal(sem("xn_scaled"), 1, 1)
        xn_ready = Signal(sem("xn_ready"), 1, 1)
        gates_ready = Signal(sem("gates_ready"), 1)
        biases_ready = Signal(sem("biases_ready"), 1)
        pool_norm = Signal(sem("pool_norm"), 2, 2)
        pool_biases = Signal(sem("pool_biases"), 2 * NEXP)
        logits_ready = Signal(sem("logits_ready"), 1)
        gate_exps = Signal(sem("gate_exps"), 1)
        total_ready = Signal(sem("total_ready"), 1)
        out_stored = Signal(sem("out_stored"), 1, lent=1, step=16)
        consts_loaded, gate_loaded, gate_hi, gate_ready, ones_ready = (sem(n) for n in ("consts_loaded", "gate_loaded", "gate_hi", "gate_ready", "ones_ready"))
        NORM = NORM_STEPS + 1
        NORM_PARTS = 3 + ROOT_PARTS
        dve_norm = Signal(sem("dve_norm"), NORM, NORM)
        GATE_STEPS = 9
        dve_gate = Signal(sem("dve_gate"), GATE_STEPS)
        block = ctx.enter_context(nc.Block())

        def steps_of(turn, ffns, first, slot, out, following, do):
            chunks = chunks_of(ffns)
            mlp_inputs = max(chunks.index((0, 0)) - 1, 0) if 0 in ffns else None
            mlp_parts = []

            def second(i):
                f, c = chunks[i]
                do.layer2(turn, first + i, out + i // HC, f, c)
                if c == HC - 1:
                    do.finish(turn, first + i, out + i // HC, f)
                    if f == 0:
                        mlp_parts.extend(range(NORM_PARTS))

            for i, (f, c) in enumerate(chunks):
                if i == mlp_inputs:
                    do.inputs(turn, slot, 0, following)
                    slot += IN
                early = c == LAG - 1 and i >= LAG
                if early:
                    second(i - LAG)
                do.layer1(turn, first + i, slot, f, c)
                slot += 1
                if mlp_parts:
                    do.norm(turn, following, mlp_parts.pop(0))
                if i >= LAG and not early:
                    second(i - LAG)
                if first + i == LAG:
                    do.rank(turn)
                if first + i == HC:
                    do.weigh(turn)
            behind = list(range(len(chunks) - LAG, len(chunks)))
            if ffns[-1] == 0:
                for i in behind:
                    second(i)
                for part in mlp_parts:
                    do.norm(turn, following, part)
            if following is not None:
                do.inputs(turn, slot, 1, following)
            if ffns[-1] != 0:
                second(behind[0])
            if following is not None:
                do.gates(turn, slot + IN)
            if ffns[-1] != 0:
                for i in behind[1:]:
                    second(i)
            if following is not None:
                do.gates_back(turn, slot + IN + 1)

        def turns(engine, do):
            steps_of(0, [0], -CHUNKS_BEFORE, -SLOTS_BEFORE, -1, -1, do)
            with engine.Fori(0, UNITS - 1) as turn:
                do.begin(turn)
                steps_of(turn, [1, 2, 0, 3, 4], 0, 0, 0, 0, do)
            do.begin(UNITS - 1)
            steps_of(UNITS - 1, [1, 2, 3, 4], 0, 0, 0, None, do)

        class Steps_of:

            def begin(self, turn): pass
            def rank(self, turn): pass
            def weigh(self, turn): pass
            def norm(self, turn, event, part): pass
            def inputs(self, turn, slot, kind, event): pass
            def gates(self, turn, slot): pass
            def gates_back(self, turn, slot): pass
            def layer1(self, turn, i, slot, f, c): pass
            def layer2(self, turn, i, out, f, c): pass
            def finish(self, turn, i, out, f): pass

        @block.sync
        def _(sp):
            def load(turn, event, unit):
                if event == 0:
                    sp.wait_ge(mlp_done.sem, mlp_done.at(turn, -1))
                view = lambda name: dram[name][bass.ds(unit * UT, UT), :].rearrange("(b p) d -> p b d", p=P)
                sp.dma_start(x2[:, :, 0:D], view("x2")).then_inc(x2_loaded.sem, 16)
                sp.dma_start(x2[:, :, D:D + TAIL], view("x2")[:, :, MAIN:D]).then_inc(x2_loaded.sem, 16)
                sp.dma_start(h1[:, :, :], view("h1")).then_inc(h1_loaded.sem, 16)

            def store(turn):
                sp.wait_ge(total_ready.sem, total_ready.at(turn, 0))
                sp.dma_start(dram["out"][bass.ds(turn * UT, UT), :].rearrange("(b p) d -> p b d", p=P), total[:, :, :]).then_inc(out_stored.sem, 16)

            load(0, -1, 0)
            with sp.Fori(0, UNITS - 1) as turn:
                load(turn, 0, turn + 1)
                store(turn)
            store(UNITS - 1)
            sp.wait_ge(out_stored.sem, out_stored.at(UNITS - 1, 0))

        @block.gpsimd
        def _(pool):
            nc.gpsimd.memset(earlier[:, :, :], 1.0).then_inc(ones_ready, 1)
            pool.wait_ge(ones_ready, 1)
            nc.gpsimd.affine_select(out=earlier[:, :, :], in_=earlier[:, :, :], compare_op=ALU.is_gt, fill=0.0,
                                    base=0, pattern=[[1, NEXP], [-1, NEXP]], channel_multiplier=0).then_inc(ones_ready, 1)
            pool.wait_ge(consts_loaded, 16 * 5)

            class Do(Steps_of):
                def norm(self, turn, event, part):
                    if part != NORM_PARTS - 1:
                        return
                    steps = Steps(pool, pool_norm, turn, event * 2)
                    wide = lambda row: row.unsqueeze(1).to_broadcast([P, UNIT, D])
                    pool.wait_ge(xn_scaled.sem, xn_scaled.at(turn, event))
                    steps.then(nc.gpsimd.tensor_tensor(xn[:, :, 0:D], xn[:, :, 0:D], wide(gain[:, :]), ALU.mult))
                    steps.then(nc.gpsimd.tensor_tensor(xn[:, :, 0:D], xn[:, :, 0:D], wide(shift[:, :]), ALU.add))
                    apart(pool, keep["passed"])
                    nc.gpsimd.tensor_scalar(xn[:, :, D:D + TAIL], xn[:, :, MAIN:D], 1.0, 1.0, ALU.mult, ALU.mult).then_inc(xn_ready.sem, 1)
                    pool.wait_ge(h1_loaded.sem, h1_loaded.at(turn, event))
                    nc.gpsimd.tensor_tensor(base[:, :, :], x3[:, :, :], h1[:, :, :], ALU.add).then_inc(mlp_done.sem, 1)

                def weigh(self, turn):
                    steps = Steps(pool, pool_biases, turn)
                    pool.wait_ge(mlp_done.sem, mlp_done.at(turn, -1))
                    pool.wait_ge(gates_ready.sem, gates_ready.at(turn, 0))
                    apart(pool, keep["passed"])
                    for e in range(NEXP):
                        if e:
                            apart(pool, keep["passed"])
                        for b in range(UNIT):
                            last = nc.gpsimd.tensor_scalar(bias_part[:, b, :], b2[:, 1 + e, :], gates[:, b, e:e + 1], 1.0, ALU.mult, ALU.mult)
                        steps.then(last)
                        steps.then(nc.gpsimd.tensor_tensor(bias_sum[:, :, :], bias_part[:, :, :], (bias_sum if e else base)[:, :, :], ALU.add))
                    pool.sem_inc(biases_ready.sem, 1)

            turns(pool, Do())

        @block.tensor
        def _(pe):
            def slot_free(turn, slot):
                pe.wait_ge(ring_free.sem, ring_free.at(turn, slot - RING))

            class Do(Steps_of):
                def inputs(self, turn, slot, kind, event):
                    x = (x2, xn)[kind]
                    if kind == 0:
                        pe.wait_ge(x2_loaded.sem, x2_loaded.at(turn, event))
                    else:
                        pe.wait_ge(xn_ready.sem, xn_ready.at(turn, event))
                    for part in range(2):
                        slot_free(turn, slot + part)
                        for b in range(UNIT):
                            last = nc.tensor.transpose(ring[:, bank(slot + part), b * P:(b + 1) * P], x[:, b, part * P:(part + 1) * P], keep["ident"][:, :])
                        last.then_inc(ring_filled.sem, 1)
                    if kind == 0:
                        self.mlp_input = slot + 1

                def gates(self, turn, slot):
                    pe.wait_ge(gate_ready, 1)
                    pe.wait_ge(ring_free.sem, ring_free.at(turn, slot - 1))
                    x_hi, x_lo = xt["exp"]
                    passes = ((g_hi, x_hi, 0), (g_hi, x_lo, 0), (g_lo, x_hi, 0), (g_stack, x_hi, 1), (g_stack, x_lo, 1))
                    slot_free(turn, slot)
                    for k, (g, x, part) in enumerate(passes):
                        last = nc.tensor.matmul(ring[0:NEXP, bank(slot), :], g[:, :], x[:, part, :], start=k == 0, stop=k == 4)
                    last.then_inc(ring_filled.sem, 1)

                def gates_back(self, turn, slot):
                    pe.wait_ge(ring_free.sem, ring_free.at(turn, slot - 1))
                    apart(pe, keep["passed"])
                    for b in range(UNIT):
                        last = nc.tensor.transpose(ring[:, bank(slot), b * NEXP:(b + 1) * NEXP], logits_t[:, b * P:(b + 1) * P], keep["ident"][0:NEXP, 0:NEXP])
                    last.then_inc(ring_filled.sem, 1)

                def layer1(self, turn, i, slot, f, c):
                    w1_hi, w1_lo, w1_stack, _ = keep["ffn"][f]
                    x_hi, x_lo = xt["mlp" if f == 0 else "exp"]
                    if (f, c) == (0, 0):
                        pe.wait_ge(ring_free.sem, ring_free.at(turn, self.mlp_input))
                    else:
                        slot_free(turn, slot)
                    cols = slice(c * P, (c + 1) * P)
                    passes = ((w1_hi, x_hi, 0), (w1_hi, x_lo, 0), (w1_lo, x_hi, 0), (w1_stack, x_hi, 1), (w1_stack, x_lo, 1))
                    for k, (w, x, part) in enumerate(passes):
                        last = nc.tensor.matmul(ring[:, bank(slot), :], w[:, cols], x[:, part, :], start=k == 0, stop=k == 4)
                    last.then_inc(ring_filled.sem, 1)

                def layer2(self, turn, i, out, f, c):
                    w2 = keep["ffn"][f][3]
                    pe.wait_ge(lo_ready.sem, lo_ready.at(turn, i))
                    for b in range(UNIT):
                        if c == 0:
                            pe.wait_ge(out_free.sem, out_free.at(turn, (out - 1) * UNIT + b))
                        tile = slice(b * P, (b + 1) * P)
                        nc.tensor.matmul(ps_out[:, b, 0:2 * D], hid_hi[:, i % 3, tile], w2[:, c, :, :], start=c == 0, stop=False)
                        last = nc.tensor.matmul(ps_out[:, b, 0:D], hid_lo[:, i % 3, tile], w2[:, c, 0, :], start=False, stop=c == HC - 1)
                        if c == HC - 1 and b < UNIT - 1:
                            last.then_inc(out_done.sem, 1)
                    last.then_inc(hid_used.sem, 1)

            turns(pe, Do())

        @block.scalar
        def _(act):
            act.dma_start(b1[:, :], dram["b1"]).then_inc(consts_loaded, 16)
            act.dma_start(b2[:, :, :], dram["b2"].rearrange("a (f d) -> a f d", d=D).to_broadcast([P, FFNS, D])).then_inc(consts_loaded, 16)
            for to, of, n in ((gain, "ln2_g", D), (shift, "ln2_b", D), (b_gate, "b_gate", NEXP)):
                act.dma_start(to[:, :], dram[of].to_broadcast([P, n])).then_inc(consts_loaded, 16)
            for part, (to, of) in enumerate(((slice(0, P), slice(0, MAIN)), (slice(0, TAIL), slice(MAIN, D)), (slice(TAIL, P), slice(MAIN, D)))):
                act.dma_start(raw_gate[to, min(part, 1), :], dram["w_gate"][of, :]).then_inc(gate_loaded, 16)
            for signal in (ring_free, lo_ready, hid_used, out_free, out_stored):
                signal.lend(act)
            act.wait_ge(gate_loaded, 48)
            nc.scalar.activation(g_hi[:, :], raw_gate[:, 0, :], ACT.Copy)
            nc.scalar.activation(g_half[:, :], raw_gate[:, 1, :], ACT.Copy, scale=keep["low_rows"][:, 0:1]).then_inc(gate_hi, 1)
            act.wait_ge(consts_loaded, 16 * 5)

            class Do(Steps_of):
                def inputs(self, turn, slot, kind, event):
                    for part in range(2):
                        act.wait_ge(ring_filled.sem, ring_filled.at(turn, slot + part))
                        nc.scalar.activation(xt[("mlp", "exp")[kind]][0][:, part, :], ring[:, bank(slot + part), :], ACT.Copy).then_inc(inputs_hi.sem, 1)

                def layer1(self, turn, i, slot, f, c):
                    if i == HC - 2:
                        act.wait_ge(logits_ready.sem, logits_ready.at(turn, 0))
                        nc.scalar.activation(exps[:, :, :], logits[:, :, :], ACT.Exp).then_inc(gate_exps.sem, 1)
                    act.wait_ge(ring_filled.sem, ring_filled.at(turn, slot))
                    act.wait_ge(lo_ready.sem, lo_ready.at(turn, i - 2))
                    nc.scalar.activation(gelu[:, i % 2, :], ring[:, bank(slot), :], ACT.Gelu, bias=b1[:, f * HC + c:f * HC + c + 1]).then_inc(chunk_read.sem, 1)
                    act.wait_ge(chunk_read.sem, chunk_read.at(turn, i))
                    act.wait_ge(hid_used.sem, hid_used.at(turn, i - 3))
                    nc.scalar.activation(hid_hi[:, i % 3, :], gelu[:, i % 2, :], ACT.Copy).then_inc(hi_ready.sem, 1)

            turns(act, Do())

        @block.vector
        def _(dve):
            def weighed(b, e):
                return gates[:, b, e:e + 1]

            class Do(Steps_of):
                def inputs(self, turn, slot, kind, event):
                    hi, lo = xt[("mlp", "exp")[kind]]
                    for part in range(2):
                        dve.wait_ge(inputs_hi.sem, inputs_hi.at(turn, 2 * IN * event + IN * kind + part))
                        nc.vector.tensor_tensor(lo[:, part, :], ring[:, bank(slot + part), :], raw(hi[:, part, :]), ALU.subtract).then_inc(ring_free.sem, 1)
                    if kind == 0:
                        dve.wait_ge(ring_free.sem, ring_free.at(turn, slot + 1))
                        apart(dve, keep["passed"])

                def layer1(self, turn, i, slot, f, c):
                    dve.wait_ge(hi_ready.sem, hi_ready.at(turn, i))
                    dve.sem_inc(ring_free.sem, 1)
                    nc.vector.tensor_tensor(hid_lo[:, i % 3, :], gelu[:, i % 2, :], raw(hid_hi[:, i % 3, :]), ALU.subtract).then_inc(lo_ready.sem, 1)

                def gates(self, turn, slot):
                    dve.wait_ge(ring_filled.sem, ring_filled.at(turn, slot))
                    nc.vector.tensor_copy(logits_t[:, :], ring[0:NEXP, bank(slot), :]).then_inc(ring_free.sem, 1)

                def begin(self, turn):
                    steps = Steps(dve, dve_gate, turn)
                    dve.wait_ge(ring_filled.sem, ring_filled.at(turn, -1))
                    nc.vector.tensor_tensor(logits[:, :, :], ring[:, bank(-1), 0:UNIT * NEXP].rearrange("p (b e) -> p b e", e=NEXP),
                                            b_gate[:, :].unsqueeze(1).to_broadcast([P, UNIT, NEXP]), ALU.add).then_inc(ring_free.sem, 1)
                    dve.wait_ge(ring_free.sem, ring_free.at(turn, -1))
                    steps.then(nc.vector.tensor_reduce(out=best[:, :], in_=logits[:, :, :], op=ALU.max, axis=X))
                    nc.vector.tensor_tensor(logits[:, :, :], logits[:, :, :], best[:, :].unsqueeze(2).to_broadcast([P, UNIT, NEXP]), ALU.subtract).then_inc(logits_ready.sem, 1)
                    self.steps = steps

                def rank(self, turn):
                    steps = self.steps
                    dve.wait_ge(logits_ready.sem, logits_ready.at(turn, 0))
                    pairs = [P, UNIT, NEXP, NEXP]
                    other, own = logits[:, :, :].unsqueeze(2).to_broadcast(pairs), logits[:, :, :].unsqueeze(3).to_broadcast(pairs)
                    nc.vector.tensor_tensor(rank4[:, :, :, :], other, own, ALU.is_gt)
                    steps.then(nc.vector.tensor_tensor(ties[:, :, :, :], other, own, ALU.is_equal))
                    steps.then(nc.vector.tensor_tensor(ties[:, :, :, :], ties[:, :, :, :], earlier[:, :, :].unsqueeze(1).to_broadcast(pairs), ALU.mult))
                    steps.then(nc.vector.tensor_tensor(rank4[:, :, :, :], rank4[:, :, :, :], ties[:, :, :, :], ALU.add))
                    steps.then(nc.vector.tensor_reduce(out=rank[:, :, :], in_=rank4[:, :, :, :], op=ALU.add, axis=X))
                    steps.then(nc.vector.tensor_scalar(chosen[:, :, :], rank[:, :, :], 2.0, None, ALU.is_lt))

                def weigh(self, turn):
                    steps = self.steps
                    dve.wait_ge(gate_exps.sem, gate_exps.at(turn, 0))
                    steps.then(nc.vector.tensor_tensor(gates[:, :, :], exps[:, :, :], chosen[:, :, :], ALU.mult))
                    steps.then(nc.vector.tensor_reduce(out=best[:, :], in_=gates[:, :, :], op=ALU.add, axis=X))
                    steps.then(nc.vector.reciprocal(best[:, :], best[:, :]))
                    nc.vector.tensor_tensor(gates[:, :, :], gates[:, :, :], best[:, :].unsqueeze(2).to_broadcast([P, UNIT, NEXP]), ALU.mult).then_inc(gates_ready.sem, 1)
                    dve.wait_ge(gates_ready.sem, gates_ready.at(turn, 0))
                    assert steps.count == GATE_STEPS

                def finish(self, turn, i, out, f):
                    if f == 0:
                        return self.finish_mlp(turn, i, out, -1 if out < 0 else 0)
                    e = f - 1
                    if e == 0:
                        dve.wait_ge(out_stored.sem, out_stored.at(turn, -1))
                    else:
                        dve.wait_ge(out_free.sem, out_free.at(turn, out * UNIT - 1))
                    def first(b):
                        if e == 0:
                            last = nc.vector.tensor_scalar(total[:, b, :], ps_out[:, b, 0:D], weighed(b, e), 1.0, ALU.mult, ALU.mult)
                        else:
                            last = nc.vector.scalar_tensor_tensor(out=total[:, b, :], in0=ps_out[:, b, 0:D], scalar=weighed(b, e), in1=total[:, b, :],
                                                                  op0=ALU.mult, op1=ALU.add)
                        last.then_inc(out_added.sem, 1)

                    def rest(b):
                        nc.vector.scalar_tensor_tensor(out=total[:, b, :], in0=ps_out[:, b, D:2 * D], scalar=weighed(b, e), in1=total[:, b, :],
                                                       op0=ALU.mult, op1=ALU.add).then_inc(out_free.sem, 1)

                    self.in_two(turn, i, out, first, rest)
                    if e == NEXP - 1:
                        dve.wait_ge(out_free.sem, out_free.at(turn, (out + 1) * UNIT - 1))
                        dve.wait_ge(biases_ready.sem, biases_ready.at(turn, 0))
                        nc.vector.tensor_tensor(total[:, :, :], total[:, :, :], bias_sum[:, :, :], ALU.add).then_inc(total_ready.sem, 1)

                def in_two(self, turn, i, out, first, rest):
                    for b in range(-1, UNIT):
                        if b + 1 < UNIT:
                            if b + 1 < UNIT - 1:
                                dve.wait_ge(out_done.sem, out_done.at(turn, out * (UNIT - 1) + b + 1))
                            else:
                                dve.wait_ge(hid_used.sem, hid_used.at(turn, i))
                            first(b + 1)
                        if b < 0:
                            continue
                        dve.wait_ge(out_added.sem, out_added.at(turn, out * UNIT + b))
                        rest(b)

                def finish_mlp(self, turn, i, out, event):
                    if event == 0:
                        dve.wait_ge(mlp_done.sem, mlp_done.at(turn, -1))
                    self.in_two(turn, i, out,
                                lambda b: nc.vector.tensor_tensor(x3[:, b, :], ps_out[:, b, 0:D], x2[:, b, 0:D], ALU.add).then_inc(out_added.sem, 1),
                                lambda b: nc.vector.tensor_tensor(x3[:, b, :], ps_out[:, b, D:2 * D], x3[:, b, :], ALU.add).then_inc(out_free.sem, 1))
                    dve.wait_ge(out_free.sem, out_free.at(turn, (out + 1) * UNIT - 1))

                def norm(self, turn, event, part):
                    steps = Steps(dve, dve_norm, turn, event * NORM + (0, 1, 3, 6, 9, 12, NORM)[part], passed=keep["passed"])
                    if part == 0:
                        steps.then(nc.vector.tensor_tensor(x3[:, :, :], x3[:, :, :], b2[:, 0, :].unsqueeze(1).to_broadcast([P, UNIT, D]), ALU.add))
                    elif part == 1:
                        moments_of(nc, steps, stats, moments, [x3[:, b, :] for b in range(UNIT)])
                    elif part < NORM_PARTS - 1:
                        inverse_root(nc, steps, part - 2, moments[:, :, 1], 1e-5, half[:, :], guess[:, :], rstd[:, :], work[:, :])
                    else:
                        for b in range(UNIT):
                            last = nc.vector.tensor_scalar(xn[:, b, 0:D], x3[:, b, :], moments[:, b, 0:1], rstd[:, b:b + 1], ALU.subtract, ALU.mult)
                        last.then_inc(xn_scaled.sem, 1)

            dve.wait_ge(gate_hi, 1)
            nc.vector.tensor_tensor(g_lo[:, :], raw_gate[:, 0, :], raw(g_hi[:, :]), ALU.subtract)
            nc.vector.tensor_tensor(g_stack[:, :], raw_gate[:, 1, :], raw(g_half[:, :]), ALU.subtract).then_inc(gate_ready, 1)
            dve.wait_ge(ones_ready, 2)
            dve.wait_ge(consts_loaded, 16 * 5)
            turns(dve, Do())


def tower(nc, given, out, scratch):
    dram = {**given, **scratch, "out": out}
    with ExitStack() as ctx:
        sb = lambda name, shape, dt=F32: ctx.enter_context(nc.sbuf_tensor(name, shape, dt))
        keep = {"ident": sb("ident", [P, P]), "low_rows": sb("low_rows", [P, 1]), "passed": ctx.enter_context(nc.semaphore("passed"))}
        with ExitStack() as weights:
            wb = lambda name: weights.enter_context(nc.sbuf_tensor(name, [P, QKV], F32R))
            keep["w_qkv"] = [(wb(f"w_{x}_hi")[:, :], wb(f"w_{x}_lo")[:, :], wb(f"w_{x}_stack")[:, :]) for x in "qkv"]
            keep["w_proj"] = tuple(weights.enter_context(nc.sbuf_tensor(f"w_proj_{x}", [P, CHUNKS, 2, D], F32R)) for x in ("main", "twin"))
            keep["last_emb"] = weights.enter_context(nc.sbuf_tensor("last_emb", [P, TAKE, D], F32))
            keep["h0_stored"] = [weights.enter_context(nc.semaphore(f"h0_stored{t}")) for t in range(2)]
            embed(nc, keep, dram)
            attention(nc, keep, dram)
        ffn = lambda name, shape: sb(f"ffn_weights_{name}", shape, F32R)
        keep["ffn"] = [(ffn(f"w1_hi{f}", [P, HID]), ffn(f"w1_lo{f}", [P, HID]), ffn(f"w1_stack{f}", [P, HID]),
                        ffn(f"w2_{f}", [P, HC, 2, D])) for f in range(FFNS)]
        mixer(nc, keep, dram)
        experts(nc, keep, dram)


def host_layout(inputs):
    a = {k: np.asarray(v) for k, v in inputs.items()}
    ids = np.stack([a["x"].T, a["mask_BS_i1_0"].T], axis=1).reshape(P, 2 * TILES)
    chunk = np.arange(QKV).reshape(CHUNKS, D)
    order = np.concatenate([chunk[:, :MAIN].ravel(), chunk[:, MAIN:].ravel()])
    w, b = a["L0_attn_W_qkv"], a["L0_attn_b_qkv"]
    w_qkv = np.concatenate([w[:, order], w[:, QKV + order], w[:, 2 * QKV:]], axis=1)
    b_qk = np.concatenate([b[order], b[QKV + order]]).reshape(2 * QKV // P, P).T
    w_proj = a["L0_attn_W_proj"].reshape(CHUNKS, D, D)
    heads = lambda x: x.reshape(*x.shape[:-1], 2 * HEADS, HD)
    twice = lambda x: np.stack([x, x], axis=-2).reshape(*x.shape[:-2], -1)
    w_in = a["L0_ffn_in_w"].T
    head = np.arange(D).reshape(-1, QUAD, HD).transpose(1, 0, 2).ravel()
    w_mix = np.concatenate([twice(heads(w_in[:, :2 * D])), w_in[:, 2 * D + head], a["L0_ffn_out_w"].T[head]], axis=1)
    given = {
        "ids": ids, "token_emb": a["L0_tok_token_emb"], "type_emb": a["L0_tok_type_emb"], "pos_emb": a["L0_tok_pos_emb"],
        "gamma": a["L0_tok_gamma"][None], "beta": a["L0_tok_beta"][None],
        "w_qkv": w_qkv, "b_qk": b_qk, "b_v": b[None, 2 * QKV:],
        "w_proj_main": w_proj[:, :MAIN].transpose(1, 0, 2).reshape(MAIN, QKV),
        "w_proj_tail": w_proj[:, MAIN:].transpose(1, 0, 2).reshape(TAIL, QKV),
        "b_proj": a["L0_attn_b_proj"][None],
        "w_mix": w_mix, "b_mix_qk": twice(heads(a["L0_ffn_in_b"][:2 * D])).reshape(-1, P).T,
        "b_mix_v": a["L0_ffn_in_b"][None, 2 * D + head], "b_mix_out": a["L0_ffn_out_b"][None],
        "ln1_g": a["L0_ffn_ln1_g"][None], "ln1_b": a["L0_ffn_ln1_b"][None],
        "ln2_g": a["L0_ffn_ln2_g"][None], "ln2_b": a["L0_ffn_ln2_b"][None],
        "w1": np.concatenate([a["L0_ffn_mlp_w1"][None], a["L0_ffn_exp_w1"]]),
        "w2": np.concatenate([a["L0_ffn_mlp_w2"][None], a["L0_ffn_exp_w2"]]),
        "b1": np.concatenate([a["L0_ffn_mlp_b1"][None], a["L0_ffn_exp_b1"]]).reshape(FFNS * HC, P).T,
        "b2": np.concatenate([a["L0_ffn_mlp_b2"][None], a["L0_ffn_exp_b2"]]).reshape(1, FFNS * D),
        "w_gate": a["L0_ffn_gate_w"].T, "b_gate": a["L0_ffn_gate_b"][None],
    }
    return {k: np.ascontiguousarray(v) for k, v in given.items()}


def kernel(**inputs):
    import concourse.bacc as bacc
    from concourse.bass_utils import run_bass_kernel_spmd

    nc = bacc.Bacc("TRN2", target_bir_lowering=False, num_devices=1)
    given = host_layout(inputs)
    aps = {k: nc.dram_tensor(f"in_{k}", v.shape, mybir.dt.from_np(v.dtype), kind="ExternalInput").ap() for k, v in given.items()}
    out = nc.dram_tensor("out", (TOKENS, D), F32, kind="ExternalOutput").ap()
    internal = lambda name, shape: nc.dram_tensor(name, shape, F32, kind="Internal").ap()
    scratch = {k: internal(f"{k}_rows", (TOKENS, D)) for k in ("h0", "h1", "y", "x2")}
    scratch["v"] = [internal(f"v_rows{i}", (P, QKV)) for i in range(2)]
    tower(nc, aps, out, scratch)
    ran = run_bass_kernel_spmd(nc, [{f"in_{k}": v for k, v in given.items()}], core_ids=[0])
    return ran.results[0]["out"].reshape(BATCH, SEQ, D)
```
